# Optimizing a Trainium2 kernel written in Bass

```python
import numpy as np
import jax
import jax.numpy as jnp

def _softmax(x, axis=-1):
    return jax.nn.softmax(x, axis=axis)

def _gelu(x):
    return jax.nn.gelu(x, approximate=True)

def _silu(x):
    return jax.nn.silu(x)

def _sigmoid(x):
    return jax.nn.sigmoid(x)

def _layernorm(x, axis=-1, eps=1e-05):
    m = jnp.mean(x, axis=axis, keepdims=True)
    v = jnp.var(x, axis=axis, keepdims=True)
    return (x - m) / jnp.sqrt(v + eps)

def _scatter_add(tgt, idx, src, axis=0):
    return tgt.at[idx].add(src)

def _segment_sum(src, seg, n):
    return jax.ops.segment_sum(src, seg, n)
kernel_name = 'mk_gnn_resnorm_d4_gnn_r32_83a416'

def setup_inputs(seed: int=0):
    np.random.seed(seed)
    _w = jnp.asarray

    def _rec_inputs():
        import jax
        import jax.numpy as jnp
        _gk = jax.random.key(seed)
        x = -0.000202 + 1 * jax.random.normal(jax.random.fold_in(_gk, 1), (50000, 128), jnp.float32)
        src = jax.random.randint(jax.random.fold_in(_gk, 2), (50000,), 0, 50000, jnp.int32)
        dst = jnp.minimum((50000 * jax.random.uniform(jax.random.fold_in(_gk, 3), (50000,)) ** 2.0).astype(jnp.int32), 49999)
        _o = jnp.argsort(dst, stable=True)
        src = src[_o]
        dst = dst[_o]
        edge_attr_64 = 0.000167468 + 1.0002 * jax.random.normal(jax.random.fold_in(_gk, 13), (50000, 64), jnp.float32)
        edge_type_100 = jax.random.randint(jax.random.fold_in(_gk, 15), (50000,), 0, 100, jnp.int32)
        return (x, src, dst, edge_attr_64, edge_type_100)
    x, src, dst, edge_attr_64, edge_type_100 = _rec_inputs()

    def _L0_gnn_setup():
        import jax, jax.numpy as jnp
        import numpy as np
        N_NODES = 50000
        N_EDGES = 25000
        IN_CH = 128
        OUT_CH = 128
        key = jax.random.key(seed)
        k1, k2, k3, k4 = jax.random.split(key, 4)
        x = jax.random.normal(k1, (N_NODES, IN_CH), dtype=jnp.float32)
        edge_index = jax.random.randint(k2, (2, N_EDGES), 0, N_NODES, dtype=jnp.int64)
        lim = 1.0 / np.sqrt(2 * IN_CH)
        W = jax.random.uniform(k3, (OUT_CH, 2 * IN_CH), dtype=jnp.float32, minval=-lim, maxval=lim)
        b = jax.random.uniform(k4, (OUT_CH,), dtype=jnp.float32, minval=-lim, maxval=lim)
        return {'x': x, 'edge_index': edge_index, 'W': W, 'b': b}
    _L0_gnn_all = _L0_gnn_setup()
    _L0_gnn_in = {k: v for k, v in _L0_gnn_all.items() if k in ('W', 'b')}
    del _L0_gnn_all

    def _L1_gnn_setup():
        import jax, jax.numpy as jnp
        import numpy as np
        N = 3125
        E = 20000
        WIDTH = 128
        NUM_FEATURES = 64

        def _linear_relu(h, W, b):
            return jax.nn.relu(h @ W + b)
        key = jax.random.key(seed)
        k = jax.random.split(key, 8)
        x = jax.random.normal(k[0], (N, WIDTH), dtype=jnp.float32)
        e = jax.random.randint(k[1], (2, E), 0, N, dtype=jnp.int32)
        e_feat = jax.random.normal(k[2], (E, NUM_FEATURES), dtype=jnp.float32)
        s_e = 1.0 / np.sqrt(WIDTH + NUM_FEATURES)
        s_m = 1.0 / np.sqrt(2 * WIDTH)
        W_edge = jax.random.uniform(k[3], (WIDTH + NUM_FEATURES, WIDTH), jnp.float32, -s_e, s_e)
        b_edge = jax.random.uniform(k[4], (WIDTH,), jnp.float32, -s_e, s_e)
        W_mlp = jax.random.uniform(k[5], (2 * WIDTH, WIDTH), jnp.float32, -s_m, s_m)
        b_mlp = jax.random.uniform(k[6], (WIDTH,), jnp.float32, -s_m, s_m)
        return {'x': x, 'e': e, 'e_feat': e_feat, 'W_edge': W_edge, 'b_edge': b_edge, 'W_mlp': W_mlp, 'b_mlp': b_mlp}
    _L1_gnn_all = _L1_gnn_setup()
    _L1_gnn_in = {k: v for k, v in _L1_gnn_all.items() if k in ('W_edge', 'b_edge', 'W_mlp', 'b_mlp')}
    del _L1_gnn_all

    def _L2_gnn_setup():
        import jax, jax.numpy as jnp
        import numpy as np
        N_NODES = 50000
        N_EDGES = 25000
        IN_DIM = 128
        OUT_DIM = 128
        NUM_RELS = 100
        NUM_BASES = 4
        key = jax.random.key(seed)
        ks = jax.random.split(key, 8)
        h = jax.random.normal(ks[0], (N_NODES, IN_DIM), dtype=jnp.float32)
        norm = jax.random.uniform(ks[1], (N_NODES, 1), dtype=jnp.float32)
        src = jax.random.randint(ks[2], (N_EDGES,), 0, N_NODES, dtype=jnp.int32)
        dst = jax.random.randint(ks[3], (N_EDGES,), 0, N_NODES, dtype=jnp.int32)
        rel_type = jax.random.randint(ks[4], (N_EDGES,), 0, NUM_RELS, dtype=jnp.int32)
        basis_weights = jax.random.normal(ks[5], (NUM_BASES, IN_DIM, OUT_DIM), dtype=jnp.float32) * (2.0 / np.sqrt(IN_DIM + OUT_DIM))
        coefficients = jax.random.normal(ks[6], (NUM_RELS, NUM_BASES), dtype=jnp.float32) * (1.0 / np.sqrt(NUM_RELS + NUM_BASES))
        loop_weight = jax.random.normal(ks[7], (IN_DIM, OUT_DIM), dtype=jnp.float32) * (2.0 / np.sqrt(IN_DIM + OUT_DIM))
        return {'h': h, 'norm': norm, 'src': src, 'dst': dst, 'rel_type': rel_type, 'basis_weights': basis_weights, 'coefficients': coefficients, 'loop_weight': loop_weight}
    _L2_gnn_all = _L2_gnn_setup()
    _L2_gnn_in = {k: v for k, v in _L2_gnn_all.items() if k in ('basis_weights', 'coefficients', 'loop_weight')}
    del _L2_gnn_all

    def _L3_gnn_setup():
        import jax, jax.numpy as jnp
        import numpy as np
        N, E, IN, H, C = (50000, 25000, 128, 4, 32)
        HC = H * C
        EPS = 1e-05
        NEG_SLOPE = 0.2

        def _bn(z, gamma, beta):
            mu = z.mean(0)
            var = z.var(0)
            return (z - mu) * jax.lax.rsqrt(var + EPS) * gamma + beta

        def _ln(z, gamma, beta):
            mu = z.mean(-1, keepdims=True)
            var = z.var(-1, keepdims=True)
            return (z - mu) * jax.lax.rsqrt(var + EPS) * gamma + beta
        key = jax.random.key(seed)
        ks = jax.random.split(key, 12)
        s = 1.0 / np.sqrt(IN)
        return {'x': jax.random.normal(ks[0], (N, IN), jnp.float32), 'edge_index': jax.random.randint(ks[1], (2, E), 0, N, jnp.int64), 'W': jax.random.normal(ks[2], (IN, HC), jnp.float32) * s, 'att_src': jax.random.normal(ks[3], (H, C), jnp.float32) * s, 'att_dst': jax.random.normal(ks[4], (H, C), jnp.float32) * s, 'bias': jnp.zeros((HC,), jnp.float32), 'bn_gamma': jnp.ones((HC,), jnp.float32), 'bn_beta': jnp.zeros((HC,), jnp.float32), 'ln_gamma': jnp.ones((HC,), jnp.float32), 'ln_beta': jnp.zeros((HC,), jnp.float32), 'res_W': jax.random.normal(ks[5], (IN, HC), jnp.float32) * s, 'res_b': jnp.zeros((HC,), jnp.float32), 'bnres_gamma': jnp.ones((HC,), jnp.float32), 'bnres_beta': jnp.zeros((HC,), jnp.float32)}
    _L3_gnn_all = _L3_gnn_setup()
    _L3_gnn_in = {k: v for k, v in _L3_gnn_all.items() if k in ('W', 'att_src', 'att_dst', 'bias', 'bn_gamma', 'bn_beta', 'ln_gamma', 'ln_beta', 'res_W', 'res_b', 'bnres_gamma', 'bnres_beta')}
    del _L3_gnn_all
    return {'x': x, 'src': src, 'dst': dst, 'edge_attr_64': edge_attr_64, 'edge_type_100': edge_type_100, 'L0_gnn_W': _L0_gnn_in['W'], 'L0_gnn_b': _L0_gnn_in['b'], 'L1_gnn_W_edge': _L1_gnn_in['W_edge'], 'L1_gnn_b_edge': _L1_gnn_in['b_edge'], 'L1_gnn_W_mlp': _L1_gnn_in['W_mlp'], 'L1_gnn_b_mlp': _L1_gnn_in['b_mlp'], 'L2_gnn_basis_weights': _L2_gnn_in['basis_weights'], 'L2_gnn_coefficients': _L2_gnn_in['coefficients'], 'L2_gnn_loop_weight': _L2_gnn_in['loop_weight'], 'L3_gnn_W': _L3_gnn_in['W'], 'L3_gnn_att_src': _L3_gnn_in['att_src'], 'L3_gnn_att_dst': _L3_gnn_in['att_dst'], 'L3_gnn_bias': _L3_gnn_in['bias'], 'L3_gnn_bn_gamma': _L3_gnn_in['bn_gamma'], 'L3_gnn_bn_beta': _L3_gnn_in['bn_beta'], 'L3_gnn_ln_gamma': _L3_gnn_in['ln_gamma'], 'L3_gnn_ln_beta': _L3_gnn_in['ln_beta'], 'L3_gnn_res_W': _L3_gnn_in['res_W'], 'L3_gnn_res_b': _L3_gnn_in['res_b'], 'L3_gnn_bnres_gamma': _L3_gnn_in['bnres_gamma'], 'L3_gnn_bnres_beta': _L3_gnn_in['bnres_beta']}

def reference(x, src, dst, edge_attr_64, edge_type_100, L0_gnn_W, L0_gnn_b, L1_gnn_W_edge, L1_gnn_b_edge, L1_gnn_W_mlp, L1_gnn_b_mlp, L2_gnn_basis_weights, L2_gnn_coefficients, L2_gnn_loop_weight, L3_gnn_W, L3_gnn_att_src, L3_gnn_att_dst, L3_gnn_bias, L3_gnn_bn_gamma, L3_gnn_bn_beta, L3_gnn_ln_gamma, L3_gnn_ln_beta, L3_gnn_res_W, L3_gnn_res_b, L3_gnn_bnres_gamma, L3_gnn_bnres_beta):
    import jax
    import jax.numpy as jnp

    def _L0_gnn_ref(x, edge_index, W, b):
        import jax, jax.numpy as jnp
        import numpy as np
        N_NODES = 50000
        N_EDGES = 25000
        IN_CH = 128
        OUT_CH = 128
        src, dst = (edge_index[0], edge_index[1])
        n = x.shape[0]
        neigh = jax.ops.segment_sum(x[src], dst, num_segments=n)
        deg = jax.ops.segment_sum(jnp.ones((dst.shape[0],), dtype=x.dtype), dst, num_segments=n)
        neigh = neigh / jnp.maximum(deg, 1.0)[:, None]
        h = jnp.concatenate([x, neigh], axis=-1)
        out = h @ W.T + b
        norm = jnp.linalg.norm(out, axis=-1, keepdims=True)
        return out / jnp.maximum(norm, 1e-12)

    def _L1_gnn_ref(x, e, e_feat, W_edge, b_edge, W_mlp, b_mlp):
        import jax, jax.numpy as jnp
        import numpy as np
        N = 3125
        E = 20000
        WIDTH = 128
        NUM_FEATURES = 64

        def _linear_relu(h, W, b):
            return jax.nn.relu(h @ W + b)
        src, dst = (e[0], e[1])
        diffs = x[dst] - x[src]
        ef = diffs + _linear_relu(jnp.concatenate([diffs, e_feat], axis=1), W_edge, b_edge)
        maxes = jax.ops.segment_max(ef, dst, num_segments=x.shape[0])
        maxes = jnp.where(jnp.isneginf(maxes), 0.0, maxes)
        return x + _linear_relu(jnp.concatenate([x, maxes], axis=1), W_mlp, b_mlp)

    def _L2_gnn_ref(h, norm, src, dst, rel_type, basis_weights, coefficients, loop_weight):
        import jax, jax.numpy as jnp
        import numpy as np
        N_NODES = 50000
        N_EDGES = 25000
        IN_DIM = 128
        OUT_DIM = 128
        NUM_RELS = 100
        NUM_BASES = 4
        n_nodes = h.shape[0]
        num_bases = basis_weights.shape[0]
        loop_message = h @ loop_weight
        hb = jnp.einsum('ni,bio->bno', h, basis_weights)
        c_e = coefficients[rel_type]
        msg = c_e[:, 0, None] * hb[0][src]
        for b in range(1, num_bases):
            msg = msg + c_e[:, b, None] * hb[b][src]
        agg = jax.ops.segment_sum(msg, dst, num_segments=n_nodes)
        node_repr = agg * norm
        node_repr = node_repr + loop_message
        return jax.nn.relu(node_repr)

    def _L3_gnn_ref(x, edge_index, W, att_src, att_dst, bias, bn_gamma, bn_beta, ln_gamma, ln_beta, res_W, res_b, bnres_gamma, bnres_beta):
        import jax, jax.numpy as jnp
        import numpy as np
        N, E, IN, H, C = (50000, 25000, 128, 4, 32)
        HC = H * C
        EPS = 1e-05
        NEG_SLOPE = 0.2

        def _bn(z, gamma, beta):
            mu = z.mean(0)
            var = z.var(0)
            return (z - mu) * jax.lax.rsqrt(var + EPS) * gamma + beta

        def _ln(z, gamma, beta):
            mu = z.mean(-1, keepdims=True)
            var = z.var(-1, keepdims=True)
            return (z - mu) * jax.lax.rsqrt(var + EPS) * gamma + beta
        n = x.shape[0]
        loops = jnp.tile(jnp.arange(n, dtype=edge_index.dtype), (2, 1))
        ei = jnp.concatenate([edge_index, loops], axis=1)
        src, dst = (ei[0], ei[1])
        h = (x @ W).reshape(n, H, C)
        a_src = (h * att_src).sum(-1)
        a_dst = (h * att_dst).sum(-1)
        alpha = a_src[src] + a_dst[dst]
        alpha = jnp.where(alpha >= 0, alpha, NEG_SLOPE * alpha)
        m = jax.ops.segment_max(alpha, dst, num_segments=n)
        ex = jnp.exp(alpha - m[dst])
        denom = jax.ops.segment_sum(ex, dst, num_segments=n)
        alpha = ex / denom[dst]
        msg = h[src] * alpha[..., None]
        out = jax.ops.segment_sum(msg, dst, num_segments=n).reshape(n, HC) + bias
        out = _bn(out, bn_gamma, bn_beta)
        out = _ln(out, ln_gamma, ln_beta)
        identity = _bn(x @ res_W + res_b, bnres_gamma, bnres_beta)
        return jax.nn.relu(out + identity)
    edge_index = jnp.stack([src, dst])
    deg = jnp.maximum(jax.ops.segment_sum(jnp.ones(dst.shape, jnp.float32), dst, num_segments=50000), 1.0)
    deg_isqrt = deg ** (-0.5)
    x = _layernorm(x + _L0_gnn_ref(x, edge_index, L0_gnn_W, L0_gnn_b), axis=-1)
    x = _layernorm(x + _L1_gnn_ref(x, edge_index, edge_attr_64, L1_gnn_W_edge, L1_gnn_b_edge, L1_gnn_W_mlp, L1_gnn_b_mlp), axis=-1)
    x = _layernorm(x + _L2_gnn_ref(x, deg_isqrt[:, None], src, dst, edge_type_100, L2_gnn_basis_weights, L2_gnn_coefficients, L2_gnn_loop_weight), axis=-1)
    x = _layernorm(x + _L3_gnn_ref(x, edge_index, L3_gnn_W, L3_gnn_att_src, L3_gnn_att_dst, L3_gnn_bias, L3_gnn_bn_gamma, L3_gnn_bn_beta, L3_gnn_ln_gamma, L3_gnn_ln_beta, L3_gnn_res_W, L3_gnn_res_b, L3_gnn_bnres_gamma, L3_gnn_bnres_beta), axis=-1)
    return x

_drawn_inputs = setup_inputs


def setup_inputs(seed=0):
    import zlib

    import numpy as np

    out = dict(_drawn_inputs(seed))
    spreads = {'L3_gnn_bias': (0.0, 0.8),
     'L3_gnn_bn_gamma': (1.0, 0.2),
     'L3_gnn_bn_beta': (0.0, 0.1),
     'L3_gnn_ln_gamma': (1.0, 0.2),
     'L3_gnn_ln_beta': (0.0, 0.1),
     'L3_gnn_res_b': (0.0, 0.8),
     'L3_gnn_bnres_gamma': (1.0, 0.2),
     'L3_gnn_bnres_beta': (0.0, 0.1)}
    factors = {'L0_gnn_b': 8.0, 'L1_gnn_b_edge': 8.0, 'L1_gnn_b_mlp': 4.044}
    for name, (base, spread) in spreads.items():
        noise = np.random.default_rng([zlib.crc32(name.encode()), seed]).standard_normal(out[name].shape)
        drawn = base * np.exp(spread * noise) if base else spread * noise
        out[name] = jnp.asarray(drawn.astype(out[name].dtype))
    for name, factor in factors.items():
        out[name] = (out[name] * factor).astype(out[name].dtype)
    return out
```

```python
import concourse.bass as bass
from concourse import mybir
from contextlib import ExitStack

N = 50000
F = 128
P = 128
K = 4
CH = P * K
NCH = -(-N // CH)
NP = NCH * CH
LAST = N - (NCH - 1) * CH
LO = 512
HI = NP // LO
H = 4
HC = F // H
W3 = F + 2 * H
NREL = 100
NBASE = 4
EF = 64
SLOTS = 4
EPS = 1e-5
BIG = 1e38

fp32 = mybir.dt.float32
bf16 = mybir.dt.bfloat16
fp16 = mybir.dt.float16
i32 = mybir.dt.int32
ALU = mybir.AluOpType
ACT = mybir.ActivationFunctionType
AX = mybir.AxisListType


def run_chunks(eng, *stages):
    most = max(lag for _, lag in stages)
    head = 1 + -(-most // SLOTS)
    whole = NCH // SLOTS

    def steps(ts):
        for t in ts:
            for work, lag in stages:
                c = t - lag
                if 0 <= c < NCH:
                    work(c, c // SLOTS, c % SLOTS)

    steps(range(head * SLOTS))
    with eng.Fori(head, whole) as i:
        for v in range(SLOTS):
            for work, lag in stages:
                q = i + (v - lag) // SLOTS
                work(i * SLOTS + (v - lag), q, (v - lag) % SLOTS)
    steps(range(whole * SLOTS, NCH + most))


def reused(c, n):
    return not (isinstance(c, int) and c < n)


class Room:

    def __init__(self, nc, ctx, tag):
        self.nc, self.ctx, self.tag = nc, ctx, tag
        self.used = []

    def sb(self, name, shape, dt=fp32):
        return self.ctx.enter_context(self.nc.sbuf_tensor(f"{self.tag}_{name}", shape, dt))

    def ps(self, name, shape=(P, 512)):
        return self.ctx.enter_context(self.nc.psum_tensor(f"{self.tag}_ps_{name}", list(shape), fp32))

    def sem(self, name):
        self.used.append(self.nc.alloc_semaphore(f"{self.tag}_{name}"))
        return self.used[-1]

    def close(self):
        self.nc.clear_and_free_semaphores(self.used)
        self.nc.all_engine_barrier()

    def sems(self, name, n=SLOTS):
        return [self.sem(f"{name}{i}") for i in range(n)]


def rows(dram, c, n=CH):
    return dram[bass.ds(c * CH, CH), :].rearrange("(p k) f -> p (k f)", k=K)


def vec(dram, c):
    return dram[bass.ds(c * CH, CH)].rearrange("(p k) -> p k", k=K)


def spread(dram, c, parts):
    return dram[bass.ds(c * CH, CH)].unsqueeze(0).to_broadcast([parts, CH])


def gather(pool, ready, out, width, table, index):
    pool.nop(nofuse=True)
    for k in range(K):
        pool.indirect_dma_start(out[:, k * width:(k + 1) * width], None, table,
                                bass.IndirectOffsetOnAxis(ap=index[:, k:k + 1], axis=0)).then_inc(ready, 16)


def prepare(nc, D, S):
    with ExitStack() as ctx:
        r = Room(nc, ctx, "prep")
        cols = NP // P
        dst = r.sb("dst", [P, cols], i32)
        prev = r.sb("prev", [P, cols], i32)
        rel = r.sb("rel", [P, cols], i32)
        keep = r.sb("keep", [P, cols], bf16)
        gate = r.sb("gate", [P, cols], bf16)
        relb = r.sb("relb", [P, cols], bf16)
        hi = r.sb("hi", [P, cols], i32)
        lo = r.sb("lo", [P, cols], i32)
        neutral = r.sb("neutral", [1, 2 * W3])
        s_load = r.sem("load")
        s_rel = r.sem("rel")
        s_keep = r.sem("keep")
        s_digit = r.sem("digit")
        s_neutral = r.sem("neutral")
        s_store = r.sem("store")
        s_id = r.sem("id")
        ctx.callback(r.close)
        block = ctx.enter_context(nc.Block())

        @block.sync
        def _(sp):
            sp.dma_start(dst[:, :], D["dst"][1:NP + 1].rearrange("(p j) -> p j", p=P)).then_inc(s_load, 16)
            sp.dma_start(prev[:, :], D["dst"][0:NP].rearrange("(p j) -> p j", p=P)).then_inc(s_load, 16)
            sp.dma_start(rel[:, :], D["edge_type_100"].rearrange("(p j) -> p j", p=P)).then_inc(s_rel, 16)
            sp.wait_ge(s_keep, 1)
            sp.dma_start(D["keep"].rearrange("(p j) -> p j", p=P), keep[:, :]).then_inc(s_store, 16)
            sp.wait_ge(s_keep, 2)
            sp.dma_start(D["gate"].rearrange("(p j) -> p j", p=P), gate[:, :]).then_inc(s_store, 16)
            sp.wait_ge(s_keep, 3)
            sp.dma_start(D["rel"].rearrange("(p j) -> p j", p=P), relb[:, :]).then_inc(s_store, 16)
            sp.wait_ge(s_neutral, 2)
            sp.dma_start(D["agg"][NP:NP + 1, :], neutral[:, 0:F]).then_inc(s_store, 16)
            sp.dma_start(D["att"][NP:NP + 1, :], neutral[:, W3:2 * W3]).then_inc(s_store, 16)
            sp.wait_ge(s_store, 80)

        @block.vector
        def _(dve):
            dve.wait_ge(s_load, 32)
            dve.tensor_tensor(keep[:, :], dst[:, :], prev[:, :], ALU.is_equal).then_inc(s_keep, 1)
            dve.wait_ge(s_keep, 1)
            dve.tensor_scalar(gate[:, :], keep[:, :], -1.0, BIG, ALU.add, ALU.mult).then_inc(s_keep, 1)
            dve.wait_ge(s_rel, 16)
            dve.tensor_copy(relb[:, :], rel[:, :]).then_inc(s_keep, 1)
            dve.tensor_scalar(hi[:, :], dst[:, :], LO.bit_length() - 1, None, ALU.arith_shift_right).then_inc(s_digit, 1)
            dve.tensor_scalar(lo[:, :], dst[:, :], LO - 1, None, ALU.bitwise_and).then_inc(s_digit, 1)
            dve.wait_ge(s_digit, 2)
            dve.tensor_copy(S["hi"][:, :], hi[:, :]).then_inc(s_digit, 1)
            dve.tensor_copy(S["lo"][:, :], lo[:, :]).then_inc(s_digit, 1)
            dve.memset(neutral[:, :], 0.0).then_inc(s_neutral, 1)
            dve.wait_ge(s_neutral, 1)
            dve.memset(neutral[:, 2 * W3 - H:2 * W3], -BIG).then_inc(s_neutral, 1)

        @block.gpsimd
        def _(pool):
            pool.iota(S["iota"][:, :], pattern=[[1, LO]], base=0, channel_multiplier=0,
                      allow_small_or_imprecise_dtypes=True).then_inc(s_id, 1)
            pool.iota(S["iota_p"][:, :], pattern=[[0, 1]], base=0, channel_multiplier=1,
                      allow_small_or_imprecise_dtypes=True).then_inc(s_id, 1)
            pool.memset(S["ones"][:, :], 1.0).then_inc(s_id, 1)
            pool.memset(S["eps"][:, :], EPS).then_inc(s_id, 1)
            pool.memset(S["ident"][:, :], 0.0).then_inc(s_id, 1)
            pool.wait_ge(s_id, 5)
            pool.affine_select(out=S["ident"][:, :], in_=S["ident"][:, :], compare_op=ALU.not_equal, fill=1.0,
                               base=0, pattern=[[-1, P]], channel_multiplier=1).then_inc(s_id, 1)
            pool.affine_select(out=S["head"][:, :], in_=S["ones"][:, 0:H], compare_op=ALU.is_ge, fill=0.0,
                               base=0, pattern=[[-HC, H]], channel_multiplier=1).then_inc(s_id, 1)
            pool.affine_select(out=S["head_first"][:, :], in_=S["ones"][:, 0:H], compare_op=ALU.is_equal, fill=0.0,
                               base=0, pattern=[[-HC, H]], channel_multiplier=1).then_inc(s_id, 1)
            pool.wait_ge(s_id, 8)
            pool.affine_select(out=S["head"][:, :], in_=S["head"][:, :], compare_op=ALU.is_ge, fill=0.0,
                               base=HC - 1, pattern=[[HC, H]], channel_multiplier=-1).then_inc(s_id, 1)
            pool.affine_select(out=S["before"][:, :], in_=S["ones"][:, 0:P], compare_op=ALU.is_gt, fill=0.0,
                               base=0, pattern=[[1, P]], channel_multiplier=-1).then_inc(s_id, 1)


def edge_sum_rows(nc, D, S):
    with ExitStack() as ctx:
        r = Room(nc, ctx, "e0")
        idx = r.sb("idx", [P, SLOTS, K], i32)
        keep = r.sb("keep", [P, SLOTS, CH], bf16)
        src = r.sb("src", [P, SLOTS, CH])
        run = r.sb("run", [P, SLOTS, CH])
        out = r.sb("out", [P, SLOTS, CH])
        hot_hi = r.sb("hot_hi", [P, 2, K, HI], bf16)
        hot_lo = r.sb("hot_lo", [P, 2, K, LO], bf16)
        count = r.sb("count", [HI, LO])
        cum = r.sb("cum", [HI, LO])
        has = r.sb("has", [HI, LO])
        last = r.sb("last", [HI, LO])
        before_me = r.sb("before_me", [HI, 1])
        index = r.sb("index", [HI, LO], i32)
        deg = r.sb("deg", [HI, LO])
        ps_src = [r.ps(f"src{i}") for i in range(2)]
        ps_out = [r.ps(f"out{i}") for i in range(2)]
        ps_count = r.ps("count")
        ps_off = r.ps("off")
        s_idx = r.sems("idx")
        s_keep = r.sems("keep")
        s_src = r.sems("src")
        s_store = r.sems("store")
        s_turned = r.sem("turned")
        s_scan = r.sem("scan")
        s_back = r.sem("back")
        s_out = r.sem("out")
        s_hot = r.sem("hot")
        s_counted = r.sem("counted")
        s_cnt = r.sem("cnt")
        s_off = r.sem("off")
        s_deg = r.sem("deg")
        ctx.callback(r.close)
        block = ctx.enter_context(nc.Block())

        @block.sync
        def _(sp):
            def load_idx(c, q, u):
                if reused(c, SLOTS):
                    sp.wait_ge(s_src[u], 16 * K * q)
                sp.nop(nofuse=True)
                sp.dma_start(idx[:, u, :], vec(D["src"], c)).then_inc(s_idx[u], 16)

            def load_keep(c, q, u):
                if reused(c, SLOTS):
                    sp.wait_ge(s_scan, c - SLOTS + 1)
                sp.nop(nofuse=True)
                sp.dma_start(keep[:, u, :], spread(D["keep"], c, P)).then_inc(s_keep[u], 16)

            def store(c, q, u):
                sp.wait_ge(s_out, c + 1)
                sp.nop(nofuse=True)
                sp.dma_start(rows(D["agg"], c), out[:, u, :]).then_inc(s_store[u], 16)

            run_chunks(sp, (load_idx, 0), (load_keep, 1), (store, 5))
            for u in range(SLOTS):
                sp.wait_ge(s_store[u], 16 * len(range(u, NCH, SLOTS)))
            sp.wait_ge(s_deg, 2)
            sp.dma_start(D["last"].rearrange("(h l) -> h l", l=LO), index[:, :]).then_inc(s_idx[0], 16)
            sp.dma_start(D["deg"].rearrange("(h l) -> h l", l=LO), deg[:, :]).then_inc(s_idx[0], 16)
            sp.wait_ge(s_idx[0], 16 * (len(range(0, NCH, SLOTS)) + 2))

        @block.gpsimd
        def _(pool):
            def fetch(c, q, u):
                pool.wait_ge(s_idx[u], 16 * (q + 1))
                if reused(c, SLOTS):
                    pool.wait_ge(s_turned, c - SLOTS + 1)
                gather(pool, s_src[u], src[:, u, :], F, D["x0"], idx[:, u, :])

            run_chunks(pool, (fetch, 0))

        @block.tensor
        def _(pe):
            def turn(c, q, u):
                pe.wait_ge(s_src[u], 16 * K * (q + 1))
                if reused(c, 2):
                    pe.wait_ge(s_scan, c - 1)
                bank = ps_src[u % 2][:, :].rearrange("f (p k) -> f k p", k=K)
                for k in range(K):
                    ins = pe.transpose(bank[:, k, :], src[:, u, k * F:(k + 1) * F], S["ident"][:, :])
                ins.then_inc(s_turned, 1)

            def tally(c, q, u):
                pe.wait_ge(s_hot, c + 1)
                for k in range(K):
                    first = isinstance(c, int) and c == 0 and k == 0
                    final = isinstance(c, int) and c == NCH - 1 and k == K - 1
                    ins = pe.matmul(ps_count[0:HI, :], hot_hi[:, u % 2, k, :], hot_lo[:, u % 2, k, :],
                                    start=first, stop=final)
                ins.then_inc(s_counted, 1)

            def back(c, q, u):
                pe.wait_ge(s_scan, c + 1)
                if reused(c, 2):
                    pe.wait_ge(s_out, c - 1)
                cols = run[:, u, :].rearrange("f (p k) -> f k p", k=K)
                for k in range(K):
                    ins = pe.transpose(ps_out[u % 2][:, k * F:(k + 1) * F], cols[:, k, :], S["ident"][:, :])
                ins.then_inc(s_back, 1)

            run_chunks(pe, (turn, 0), (tally, 1), (back, 1))
            pe.wait_ge(s_cnt, 2)
            pe.matmul(ps_off[0:HI, 0:1], S["before"][0:HI, 0:HI], cum[:, LO - 1:LO], start=True, stop=True).then_inc(s_off, 1)

        @block.vector
        def _(dve):
            def hot(c, q, u):
                if reused(c, 2):
                    dve.wait_ge(s_counted, c - 1)
                for k in range(K):
                    j = c * K + k
                    dve.tensor_scalar(hot_hi[:, u % 2, k, :], S["iota"][:, 0:HI], S["hi"][:, bass.ds(j, 1)], None, ALU.is_equal)
                    ins = dve.tensor_scalar(hot_lo[:, u % 2, k, :], S["iota"][:, :], S["lo"][:, bass.ds(j, 1)], None, ALU.is_equal)
                ins.then_inc(s_hot, 1)

            def scan(c, q, u):
                dve.wait_ge(s_turned, c + 1)
                dve.wait_ge(s_keep[u], 16 * (q + 1))
                if reused(c, SLOTS):
                    dve.wait_ge(s_back, c - SLOTS + 1)
                carry = 0.0
                if reused(c, 1):
                    dve.wait_ge(s_scan, c)
                    carry = run[:, (u - 1) % SLOTS, CH - 1:CH]
                dve.tensor_tensor_scan(run[:, u, :], keep[:, u, :], ps_src[u % 2][:, :], carry, ALU.mult, ALU.add).then_inc(s_scan, 1)

            run_chunks(dve, (hot, 0), (scan, 0))
            dve.wait_ge(s_counted, NCH)
            dve.tensor_copy(count[:, :], ps_count[0:HI, :]).then_inc(s_cnt, 1)
            dve.wait_ge(s_cnt, 1)
            dve.tensor_tensor_scan(cum[:, :], S["ones"][0:HI, :], count[:, :], 0.0, ALU.mult, ALU.add).then_inc(s_cnt, 1)
            dve.tensor_scalar(deg[:, :], count[:, :], 1.0, None, ALU.max).then_inc(s_deg, 1)
            dve.tensor_scalar(has[:, :], count[:, :], 0.0, None, ALU.is_gt).then_inc(s_cnt, 1)
            dve.wait_ge(s_off, 1)
            dve.tensor_copy(before_me[:, :], ps_off[0:HI, 0:1]).then_inc(s_cnt, 1)
            dve.wait_ge(s_cnt, 4)
            dve.tensor_scalar(last[:, :], cum[:, :], before_me[:, 0:1], -1.0 - NP, ALU.add, ALU.add).then_inc(s_cnt, 1)
            dve.wait_ge(s_cnt, 5)
            dve.tensor_tensor(cum[:, :], last[:, :], has[:, :], ALU.mult).then_inc(s_cnt, 1)
            dve.wait_ge(s_cnt, 6)
            dve.tensor_scalar(index[:, :], cum[:, :], float(NP), None, ALU.add).then_inc(s_deg, 1)

        @block.scalar
        def _(act):
            def leave(c, q, u):
                act.wait_ge(s_back, c + 1)
                if reused(c, SLOTS):
                    act.wait_ge(s_store[u], 16 * q)
                act.activation(out[:, u, :], ps_out[u % 2][:, :], ACT.Copy).then_inc(s_out, 1)

            run_chunks(act, (leave, 0))


def layer_norm_ready(dve, x, stats, mv, done, seen):
    for k in range(K):
        ins = dve.bn_stats(stats[:, k * 6:(k + 1) * 6], x[:, k * F:(k + 1) * F])
    ins.then_inc(done, 1)
    dve.wait_ge(done, seen)
    dve.nop(nofuse=True)
    for k in range(K):
        ins = dve.bn_aggr(mv[:, k, :], stats[:, k * 6:(k + 1) * 6])
    return ins


def node_mean(nc, D, S):
    with ExitStack() as ctx:
        r = Room(nc, ctx, "n0")
        w = r.sb("w", [P, 2 * F])
        wt = r.sb("wt", [P, 2 * F])
        b = r.sb("b", [1, F])
        idx = r.sb("idx", [P, SLOTS, K], i32)
        deg = r.sb("deg", [P, SLOTS, K])
        rdeg = r.sb("rdeg", [P, SLOTS, K])
        agg = r.sb("agg", [P, SLOTS, CH])
        mean = r.sb("mean", [P, 2, CH])
        x = r.sb("x", [P, SLOTS, CH])
        xT = r.sb("xT", [P, 2, CH])
        mT = r.sb("mT", [P, 2, CH])
        junk = r.sb("junk", [P, CH])
        ss = r.sb("ss", [P, SLOTS, K])
        nrm = r.sb("nrm", [P, SLOTS, K])
        rn = r.sb("rn", [P, SLOTS, K])
        y = r.sb("y", [P, SLOTS, CH])
        stats = r.sb("stats", [P, SLOTS, K * 6])
        mv = r.sb("mv", [P, SLOTS, K, 2])
        sd = r.sb("sd", [P, SLOTS, K])
        rs = r.sb("rs", [P, SLOTS, K])
        out = r.sb("out", [P, SLOTS, CH])
        ps_x = [r.ps(f"x{i}") for i in range(2)]
        ps_m = [r.ps(f"m{i}") for i in range(2)]
        ps_o = [r.ps(f"o{i}") for i in range(2)]
        s_w = r.sem("w")
        s_wps = r.sem("wps")
        s_wt = r.sem("wt")
        s_idx = r.sems("idx")
        s_x = r.sems("x")
        s_deg = r.sems("deg")
        s_agg = r.sems("agg")
        s_store = r.sems("store")
        s_rd = r.sem("rd")
        s_mean = r.sem("mean")
        s_turned = r.sem("turned")
        s_T = r.sem("T")
        s_mm = r.sem("mm")
        s_sq = r.sem("sq")
        s_nrm = r.sem("nrm")
        s_rn = r.sem("rn")
        s_y = r.sem("y")
        s_st = r.sem("st")
        s_mv = r.sem("mv")
        s_sd = r.sem("sd")
        s_rs = r.sem("rs")
        s_out = r.sem("out")
        ctx.callback(r.close)
        block = ctx.enter_context(nc.Block())

        @block.sync
        def _(sp):
            sp.dma_start(w[:, :], D["L0_gnn_W"]).then_inc(s_w, 16)
            sp.dma_start(b[:, :], D["L0_gnn_b"].unsqueeze(0)).then_inc(s_w, 16)

            def load_idx(c, q, u):
                if reused(c, SLOTS):
                    sp.wait_ge(s_agg[u], 16 * K * q)
                sp.nop(nofuse=True)
                sp.dma_start(idx[:, u, :], vec(D["last"], c)).then_inc(s_idx[u], 16)

            def load_x(c, q, u):
                if reused(c, SLOTS):
                    sp.wait_ge(s_y, c - SLOTS + 1)
                sp.nop(nofuse=True)
                sp.dma_start(x[:, u, :], rows(D["x0"], c)).then_inc(s_x[u], 16)
                if reused(c, SLOTS):
                    sp.wait_ge(s_rd, c - SLOTS + 1)
                sp.nop(nofuse=True)
                sp.dma_start(deg[:, u, :], vec(D["deg"], c)).then_inc(s_deg[u], 16)

            def store(c, q, u):
                sp.wait_ge(s_out, c + 1)
                sp.nop(nofuse=True)
                sp.dma_start(rows(D["x1"], c), out[:, u, :]).then_inc(s_store[u], 16)

            run_chunks(sp, (load_idx, 0), (load_x, 2), (store, 7))
            for u in range(SLOTS):
                sp.wait_ge(s_store[u], 16 * len(range(u, NCH, SLOTS)))

        @block.gpsimd
        def _(pool):
            def fetch(c, q, u):
                pool.wait_ge(s_idx[u], 16 * (q + 1))
                if reused(c, SLOTS):
                    pool.wait_ge(s_mean, c - SLOTS + 1)
                gather(pool, s_agg[u], agg[:, u, :], F, D["agg"], idx[:, u, :])

            run_chunks(pool, (fetch, 0))

        @block.tensor
        def _(pe):
            pe.wait_ge(s_w, 32)
            for h in range(2):
                ins = pe.transpose(ps_x[0][:, h * F:(h + 1) * F], w[:, h * F:(h + 1) * F], S["ident"][:, :])
            ins.then_inc(s_wps, 1)

            def turn(c, q, u):
                if not reused(c, 1):
                    pe.wait_ge(s_wt, 1)
                pe.wait_ge(s_x[u], 16 * (q + 1))
                if reused(c, 2):
                    pe.wait_ge(s_T, c - 1)
                for k in range(K):
                    pe.transpose(ps_x[u % 2][:, k * P:(k + 1) * P], x[:, u, k * F:(k + 1) * F], S["ident"][:, :])
                pe.wait_ge(s_mean, c + 1)
                for k in range(K):
                    ins = pe.transpose(ps_m[u % 2][:, k * P:(k + 1) * P], mean[:, u % 2, k * F:(k + 1) * F], S["ident"][:, :])
                ins.then_inc(s_turned, 1)

            def multiply(c, q, u):
                pe.wait_ge(s_T, c + 1)
                if reused(c, 2):
                    pe.wait_ge(s_y, c - 1)
                for k in range(K):
                    o = ps_o[u % 2][:, k * F:(k + 1) * F]
                    pe.matmul(o, xT[:, u % 2, k * P:(k + 1) * P], wt[:, 0:F], start=True, stop=False)
                    pe.matmul(o, mT[:, u % 2, k * P:(k + 1) * P], wt[:, F:2 * F], start=False, stop=False)
                    ins = pe.matmul(o, S["ones"][0:1, 0:P], b[0:1, :], start=False, stop=True)
                ins.then_inc(s_mm, 1)

            run_chunks(pe, (turn, 0), (multiply, 1))

        @block.scalar
        def _(act):
            act.wait_ge(s_wps, 1)
            act.activation(wt[:, :], ps_x[0][:, 0:2 * F], ACT.Copy).then_inc(s_wt, 1)

            def copy(c, q, u):
                act.wait_ge(s_turned, c + 1)
                if reused(c, 2):
                    act.wait_ge(s_mm, c - 1)
                act.activation(xT[:, u % 2, :], ps_x[u % 2][:, :], ACT.Copy)
                act.activation(mT[:, u % 2, :], ps_m[u % 2][:, :], ACT.Copy).then_inc(s_T, 1)

            def squares(c, q, u):
                act.wait_ge(s_mm, c + 1)
                for k in range(K):
                    ins = act.activation(junk[:, k * F:(k + 1) * F], ps_o[u % 2][:, k * F:(k + 1) * F], ACT.Square,
                                         accum_out=ss[:, u, k:k + 1])
                ins.then_inc(s_sq, 1)
                act.wait_ge(s_sq, c + 1)
                act.activation(nrm[:, u, :], ss[:, u, :], ACT.Sqrt).then_inc(s_nrm, 1)

            def deviation(c, q, u):
                act.wait_ge(s_mv, c + 1)
                act.activation(sd[:, u, :], mv[:, u, :, 1], ACT.Sqrt, bias=S["eps"][:, 0:1]).then_inc(s_sd, 1)

            run_chunks(act, (deviation, 3), (copy, 0), (squares, 1))

        @block.vector
        def _(dve):
            def scale(c, q, u):
                dve.wait_ge(s_deg[u], 16 * (q + 1))
                dve.reciprocal(rdeg[:, u, :], deg[:, u, :]).then_inc(s_rd, 1)
                dve.wait_ge(s_rd, c + 1)
                dve.wait_ge(s_agg[u], 16 * K * (q + 1))
                if reused(c, 2):
                    dve.wait_ge(s_turned, c - 1)
                for k in range(K):
                    ins = dve.tensor_scalar(mean[:, u % 2, k * F:(k + 1) * F], agg[:, u, k * F:(k + 1) * F],
                                            rdeg[:, u, k:k + 1], None, ALU.mult)
                ins.then_inc(s_mean, 1)

            def residual(c, q, u):
                dve.wait_ge(s_nrm, c + 1)
                dve.tensor_scalar(nrm[:, u, :], nrm[:, u, :], 1e-12, None, ALU.max).then_inc(s_rn, 1)
                dve.wait_ge(s_rn, 2 * c + 1)
                dve.reciprocal(rn[:, u, :], nrm[:, u, :]).then_inc(s_rn, 1)
                dve.wait_ge(s_rn, 2 * c + 2)
                for k in range(K):
                    f = slice(k * F, (k + 1) * F)
                    ins = dve.scalar_tensor_tensor(y[:, u, f], ps_o[u % 2][:, f], rn[:, u, k:k + 1], x[:, u, f], ALU.mult, ALU.add)
                ins.then_inc(s_y, 1)
                dve.wait_ge(s_y, c + 1)
                layer_norm_ready(dve, y[:, u, :], stats[:, u, :], mv[:, u, :, :], s_st, c + 1).then_inc(s_mv, 1)

            def normalise(c, q, u):
                dve.wait_ge(s_sd, c + 1)
                dve.reciprocal(rs[:, u, :], sd[:, u, :]).then_inc(s_rs, 1)
                dve.wait_ge(s_rs, c + 1)
                if reused(c, SLOTS):
                    dve.wait_ge(s_store[u], 16 * q)
                for k in range(K):
                    f = slice(k * F, (k + 1) * F)
                    ins = dve.tensor_scalar(out[:, u, f], y[:, u, f], mv[:, u, k, 0:1], rs[:, u, k:k + 1], ALU.subtract, ALU.mult)
                ins.then_inc(s_out, 1)

            run_chunks(dve, (scale, 0), (residual, 2), (normalise, 3))


def edge_max(nc, D, S):
    with ExitStack() as ctx:
        r = Room(nc, ctx, "e1")
        wd = r.sb("wd", [P, F])
        we = r.sb("we", [EF, F])
        b = r.sb("b", [P, 1])
        idx = r.sb("idx", [P, SLOTS, 2 * K], i32)
        gate = r.sb("gate", [P, SLOTS, CH], bf16)
        feat = r.sb("feat", [P, SLOTS, K * EF])
        src = r.sb("src", [P, SLOTS, CH])
        dst = r.sb("dst", [P, SLOTS, CH])
        diff = r.sb("diff", [P, 2, CH])
        dT = r.sb("dT", [P, SLOTS, CH])
        fT = r.sb("fT", [EF, 2, CH])
        hid = r.sb("hid", [P, 2, CH])
        ef = r.sb("ef", [P, 2, CH])
        run = r.sb("run", [P, SLOTS, CH])
        out = r.sb("out", [P, SLOTS, CH])
        ps_d = [r.ps(f"d{i}") for i in range(2)]
        ps_f = [r.ps(f"f{i}") for i in range(2)]
        ps_h = [r.ps(f"h{i}") for i in range(2)]
        ps_o = [r.ps(f"o{i}") for i in range(2)]
        s_w = r.sem("w")
        s_idx = r.sems("idx")
        s_gate = r.sems("gate")
        s_feat = r.sems("feat")
        s_rows = r.sems("rows")
        s_store = r.sems("store")
        s_diff = r.sem("diff")
        s_turned = r.sem("turned")
        s_T = r.sem("T")
        s_mm = r.sem("mm")
        s_hid = r.sem("hid")
        s_ef = r.sem("ef")
        s_scan = r.sem("scan")
        s_back = r.sem("back")
        s_out = r.sem("out")
        ctx.callback(r.close)
        block = ctx.enter_context(nc.Block())

        @block.sync
        def _(sp):
            sp.dma_start(wd[:, :], D["L1_gnn_W_edge"][0:F, :]).then_inc(s_w, 16)
            sp.dma_start(we[:, :], D["L1_gnn_W_edge"][F:F + EF, :]).then_inc(s_w, 16)
            sp.dma_start(b[:, :], D["L1_gnn_b_edge"].unsqueeze(1)).then_inc(s_w, 16)

            def load_idx(c, q, u):
                if reused(c, SLOTS):
                    sp.wait_ge(s_rows[u], 16 * 2 * K * q)
                sp.nop(nofuse=True)
                sp.dma_start(idx[:, u, 0:K], vec(D["src"], c)).then_inc(s_idx[u], 16)
                sp.dma_start(idx[:, u, K:2 * K], vec(D["dst"][1:NP + 1], c)).then_inc(s_idx[u], 16)

            def load_rest(c, q, u):
                if reused(c, SLOTS):
                    sp.wait_ge(s_turned, c - SLOTS + 1)
                sp.nop(nofuse=True)
                sp.dma_start(feat[:, u, :], rows(D["edge_attr_64"], c)).then_inc(s_feat[u], 16)
                if reused(c, SLOTS):
                    sp.wait_ge(s_scan, c - SLOTS + 1)
                sp.nop(nofuse=True)
                sp.dma_start(gate[:, u, :], spread(D["gate"], c, P)).then_inc(s_gate[u], 16)

            def store(c, q, u):
                sp.wait_ge(s_out, c + 1)
                sp.nop(nofuse=True)
                sp.dma_start(rows(D["agg"], c), out[:, u, :]).then_inc(s_store[u], 16)

            run_chunks(sp, (load_idx, 0), (load_rest, 1), (store, 5))
            for u in range(SLOTS):
                sp.wait_ge(s_store[u], 16 * len(range(u, NCH, SLOTS)))

        @block.gpsimd
        def _(pool):
            def fetch(c, q, u):
                pool.wait_ge(s_idx[u], 32 * (q + 1))
                if reused(c, SLOTS):
                    pool.wait_ge(s_diff, c - SLOTS + 1)
                gather(pool, s_rows[u], src[:, u, :], F, D["x1"], idx[:, u, 0:K])
                gather(pool, s_rows[u], dst[:, u, :], F, D["x1"], idx[:, u, K:2 * K])

            run_chunks(pool, (fetch, 0))

        @block.vector
        def _(dve):
            def differ(c, q, u):
                dve.wait_ge(s_rows[u], 16 * 2 * K * (q + 1))
                if reused(c, 2):
                    dve.wait_ge(s_turned, c - 1)
                dve.tensor_tensor(diff[:, u % 2, :], dst[:, u, :], src[:, u, :], ALU.subtract).then_inc(s_diff, 1)

            def scan(c, q, u):
                dve.wait_ge(s_hid, c + 1)
                dve.tensor_tensor(ef[:, u % 2, :], dT[:, u, :], hid[:, u % 2, :], ALU.add).then_inc(s_ef, 1)
                dve.wait_ge(s_ef, c + 1)
                dve.wait_ge(s_gate[u], 16 * (q + 1))
                if reused(c, SLOTS):
                    dve.wait_ge(s_back, c - SLOTS + 1)
                carry = 0.0
                if reused(c, 1):
                    dve.wait_ge(s_scan, c)
                    carry = run[:, (u - 1) % SLOTS, CH - 1:CH]
                dve.tensor_tensor_scan(run[:, u, :], gate[:, u, :], ef[:, u % 2, :], carry, ALU.add, ALU.max).then_inc(s_scan, 1)

            run_chunks(dve, (differ, 0), (scan, 1))

        @block.tensor
        def _(pe):
            pe.wait_ge(s_w, 48)

            def turn(c, q, u):
                pe.wait_ge(s_feat[u], 16 * (q + 1))
                pe.wait_ge(s_diff, c + 1)
                if reused(c, 2):
                    pe.wait_ge(s_T, c - 1)
                bank = ps_d[u % 2][:, :].rearrange("f (p k) -> f k p", k=K)
                for k in range(K):
                    pe.transpose(bank[:, k, :], diff[:, u % 2, k * F:(k + 1) * F], S["ident"][:, :])
                bank = ps_f[u % 2][0:EF, :].rearrange("f (p k) -> f k p", k=K)
                for k in range(K):
                    ins = pe.transpose(bank[:, k, :], feat[:, u, k * EF:(k + 1) * EF], S["ident"][:, :])
                ins.then_inc(s_turned, 1)

            def multiply(c, q, u):
                pe.wait_ge(s_T, c + 1)
                if reused(c, 2):
                    pe.wait_ge(s_hid, c - 1)
                pe.matmul(ps_h[u % 2][:, :], wd[:, :], dT[:, u, :], start=True, stop=False)
                pe.matmul(ps_h[u % 2][:, :], we[:, :], fT[:, u % 2, :], start=False, stop=True).then_inc(s_mm, 1)

            def back(c, q, u):
                pe.wait_ge(s_scan, c + 1)
                if reused(c, 2):
                    pe.wait_ge(s_out, c - 1)
                cols = run[:, u, :].rearrange("f (p k) -> f k p", k=K)
                for k in range(K):
                    ins = pe.transpose(ps_o[u % 2][:, k * F:(k + 1) * F], cols[:, k, :], S["ident"][:, :])
                ins.then_inc(s_back, 1)

            run_chunks(pe, (turn, 0), (multiply, 1), (back, 2))

        @block.scalar
        def _(act):
            act.wait_ge(s_w, 48)

            def copy(c, q, u):
                act.wait_ge(s_turned, c + 1)
                if reused(c, SLOTS):
                    act.wait_ge(s_ef, c - SLOTS + 1)
                if reused(c, 2):
                    act.wait_ge(s_mm, c - 1)
                act.activation(fT[:, u % 2, :], ps_f[u % 2][0:EF, :], ACT.Copy)
                act.activation(dT[:, u, :], ps_d[u % 2][:, :], ACT.Copy).then_inc(s_T, 1)

            def hidden(c, q, u):
                act.wait_ge(s_mm, c + 1)
                if reused(c, 2):
                    act.wait_ge(s_ef, c - 1)
                act.activation(hid[:, u % 2, :], ps_h[u % 2][:, :], ACT.Relu, bias=b[:, 0:1]).then_inc(s_hid, 1)

            def leave(c, q, u):
                act.wait_ge(s_back, c + 1)
                if reused(c, SLOTS):
                    act.wait_ge(s_store[u], 16 * q)
                act.activation(out[:, u, :], ps_o[u % 2][:, :], ACT.Copy).then_inc(s_out, 1)

            run_chunks(act, (copy, 0), (hidden, 1), (leave, 2))


def node_mlp(nc, D, S):
    with ExitStack() as ctx:
        r = Room(nc, ctx, "n1")
        w = r.sb("w", [P, 2 * F])
        b = r.sb("b", [1, F])
        idx = r.sb("idx", [P, SLOTS, K], i32)
        agg = r.sb("agg", [P, SLOTS, CH])
        x = r.sb("x", [P, SLOTS, CH])
        xT = r.sb("xT", [P, 2, CH])
        mT = r.sb("mT", [P, 2, CH])
        hid = r.sb("hid", [P, 2, CH])
        y = r.sb("y", [P, SLOTS, CH])
        stats = r.sb("stats", [P, SLOTS, K * 6])
        mv = r.sb("mv", [P, SLOTS, K, 2])
        sd = r.sb("sd", [P, SLOTS, K])
        rs = r.sb("rs", [P, SLOTS, K])
        out = r.sb("out", [P, SLOTS, CH])
        ps_x = [r.ps(f"x{i}") for i in range(2)]
        ps_m = [r.ps(f"m{i}") for i in range(2)]
        ps_o = [r.ps(f"o{i}") for i in range(2)]
        s_w = r.sem("w")
        s_idx = r.sems("idx")
        s_x = r.sems("x")
        s_agg = r.sems("agg")
        s_store = r.sems("store")
        s_turned = r.sem("turned")
        s_T = r.sem("T")
        s_mm = r.sem("mm")
        s_hid = r.sem("hid")
        s_y = r.sem("y")
        s_st = r.sem("st")
        s_mv = r.sem("mv")
        s_sd = r.sem("sd")
        s_rs = r.sem("rs")
        s_out = r.sem("out")
        ctx.callback(r.close)
        block = ctx.enter_context(nc.Block())

        @block.sync
        def _(sp):
            for h in range(2):
                sp.dma_start(w[:, h * F:(h + 1) * F], D["L1_gnn_W_mlp"][h * F:(h + 1) * F, :]).then_inc(s_w, 16)
            sp.dma_start(b[:, :], D["L1_gnn_b_mlp"].unsqueeze(0)).then_inc(s_w, 16)

            def load_idx(c, q, u):
                if reused(c, SLOTS):
                    sp.wait_ge(s_agg[u], 16 * K * q)
                sp.nop(nofuse=True)
                sp.dma_start(idx[:, u, :], vec(D["last"], c)).then_inc(s_idx[u], 16)

            def load_x(c, q, u):
                if reused(c, SLOTS):
                    sp.wait_ge(s_y, c - SLOTS + 1)
                sp.nop(nofuse=True)
                sp.dma_start(x[:, u, :], rows(D["x1"], c)).then_inc(s_x[u], 16)

            def store(c, q, u):
                sp.wait_ge(s_out, c + 1)
                sp.nop(nofuse=True)
                sp.dma_start(rows(D["x2"], c), out[:, u, :]).then_inc(s_store[u], 16)

            run_chunks(sp, (load_idx, 0), (load_x, 2), (store, 7))
            for u in range(SLOTS):
                sp.wait_ge(s_store[u], 16 * len(range(u, NCH, SLOTS)))

        @block.gpsimd
        def _(pool):
            def fetch(c, q, u):
                pool.wait_ge(s_idx[u], 16 * (q + 1))
                if reused(c, SLOTS):
                    pool.wait_ge(s_turned, c - SLOTS + 1)
                gather(pool, s_agg[u], agg[:, u, :], F, D["agg"], idx[:, u, :])

            run_chunks(pool, (fetch, 0))

        @block.tensor
        def _(pe):
            pe.wait_ge(s_w, 48)

            def turn(c, q, u):
                pe.wait_ge(s_x[u], 16 * (q + 1))
                if reused(c, 2):
                    pe.wait_ge(s_T, c - 1)
                for k in range(K):
                    pe.transpose(ps_x[u % 2][:, k * P:(k + 1) * P], x[:, u, k * F:(k + 1) * F], S["ident"][:, :])
                pe.wait_ge(s_agg[u], 16 * K * (q + 1))
                for k in range(K):
                    ins = pe.transpose(ps_m[u % 2][:, k * P:(k + 1) * P], agg[:, u, k * F:(k + 1) * F], S["ident"][:, :])
                ins.then_inc(s_turned, 1)

            def multiply(c, q, u):
                pe.wait_ge(s_T, c + 1)
                if reused(c, 2):
                    pe.wait_ge(s_hid, c - 1)
                for k in range(K):
                    o = ps_o[u % 2][:, k * F:(k + 1) * F]
                    pe.matmul(o, xT[:, u % 2, k * P:(k + 1) * P], w[:, 0:F], start=True, stop=False)
                    pe.matmul(o, mT[:, u % 2, k * P:(k + 1) * P], w[:, F:2 * F], start=False, stop=False)
                    ins = pe.matmul(o, S["ones"][0:1, 0:P], b[0:1, :], start=False, stop=True)
                ins.then_inc(s_mm, 1)

            run_chunks(pe, (turn, 0), (multiply, 1))

        @block.scalar
        def _(act):
            def copy(c, q, u):
                act.wait_ge(s_turned, c + 1)
                if reused(c, 2):
                    act.wait_ge(s_mm, c - 1)
                act.activation(xT[:, u % 2, :], ps_x[u % 2][:, :], ACT.Copy)
                act.activation(mT[:, u % 2, :], ps_m[u % 2][:, :], ACT.Copy).then_inc(s_T, 1)

            def hidden(c, q, u):
                act.wait_ge(s_mm, c + 1)
                if reused(c, 2):
                    act.wait_ge(s_y, c - 1)
                act.activation(hid[:, u % 2, :], ps_o[u % 2][:, :], ACT.Relu).then_inc(s_hid, 1)

            def deviation(c, q, u):
                act.wait_ge(s_mv, c + 1)
                act.activation(sd[:, u, :], mv[:, u, :, 1], ACT.Sqrt, bias=S["eps"][:, 0:1]).then_inc(s_sd, 1)

            run_chunks(act, (deviation, 3), (copy, 0), (hidden, 1))

        @block.vector
        def _(dve):
            def residual(c, q, u):
                dve.wait_ge(s_hid, c + 1)
                dve.wait_ge(s_x[u], 16 * (q + 1))
                dve.scalar_tensor_tensor(y[:, u, :], x[:, u, :], 2.0, hid[:, u % 2, :], ALU.mult, ALU.add).then_inc(s_y, 1)
                dve.wait_ge(s_y, c + 1)
                layer_norm_ready(dve, y[:, u, :], stats[:, u, :], mv[:, u, :, :], s_st, c + 1).then_inc(s_mv, 1)

            def normalise(c, q, u):
                dve.wait_ge(s_sd, c + 1)
                dve.reciprocal(rs[:, u, :], sd[:, u, :]).then_inc(s_rs, 1)
                dve.wait_ge(s_rs, c + 1)
                if reused(c, SLOTS):
                    dve.wait_ge(s_store[u], 16 * q)
                for k in range(K):
                    f = slice(k * F, (k + 1) * F)
                    ins = dve.tensor_scalar(out[:, u, f], y[:, u, f], mv[:, u, k, 0:1], rs[:, u, k:k + 1], ALU.subtract, ALU.mult)
                ins.then_inc(s_out, 1)

            run_chunks(dve, (residual, 2), (normalise, 3))


def edge_relations(nc, D, S):
    with ExitStack() as ctx:
        r = Room(nc, ctx, "e2")
        basis = r.sb("basis", [P, NBASE, F])
        coef = r.sb("coef", [NREL, NBASE])
        idx = r.sb("idx", [P, SLOTS, K], i32)
        keep = r.sb("keep", [P, SLOTS, CH], bf16)
        rel = r.sb("rel", [NREL, SLOTS, CH], bf16)
        src = r.sb("src", [P, SLOTS, CH])
        hot = r.sb("hot", [NREL, 2, CH])
        scaled = r.sb("scaled", [P, 2, K, NBASE, F])
        sT = r.sb("sT", [P, 2, NBASE, CH])
        run = r.sb("run", [P, SLOTS, CH])
        out = r.sb("out", [P, SLOTS, CH])
        ps_c = r.ps("c")
        ps_s = [r.ps(f"s{b}") for b in range(NBASE)]
        ps_m = r.ps("m")
        ps_o = [r.ps(f"o{i}") for i in range(2)]
        s_w = r.sem("w")
        s_idx = r.sems("idx")
        s_keep = r.sems("keep")
        s_rel = r.sems("rel")
        s_src = r.sems("src")
        s_store = r.sems("store")
        s_hot = r.sem("hot")
        s_coef = r.sem("coef")
        s_scaled = r.sem("scaled")
        s_half = r.sem("half")
        s_turned = r.sem("turned")
        s_T = r.sem("T")
        s_mm = r.sem("mm")
        s_scan = r.sem("scan")
        s_back = r.sem("back")
        s_out = r.sem("out")
        ctx.callback(r.close)
        block = ctx.enter_context(nc.Block())

        @block.sync
        def _(sp):
            for b in range(NBASE):
                sp.dma_start(basis[:, b, :], D["L2_gnn_basis_weights"][b, :, :]).then_inc(s_w, 16)
            sp.dma_start(coef[:, :], D["L2_gnn_coefficients"]).then_inc(s_w, 16)

            def load_idx(c, q, u):
                if reused(c, SLOTS):
                    sp.wait_ge(s_src[u], 16 * K * q)
                sp.nop(nofuse=True)
                sp.dma_start(idx[:, u, :], vec(D["src"], c)).then_inc(s_idx[u], 16)

            def load_rest(c, q, u):
                if reused(c, SLOTS):
                    sp.wait_ge(s_hot, c - SLOTS + 1)
                sp.nop(nofuse=True)
                sp.dma_start(rel[:, u, :], spread(D["rel"], c, NREL)).then_inc(s_rel[u], 16)
                if reused(c, SLOTS):
                    sp.wait_ge(s_scan, c - SLOTS + 1)
                sp.nop(nofuse=True)
                sp.dma_start(keep[:, u, :], spread(D["keep"], c, P)).then_inc(s_keep[u], 16)

            def store(c, q, u):
                sp.wait_ge(s_out, c + 1)
                sp.nop(nofuse=True)
                sp.dma_start(rows(D["agg"], c), out[:, u, :]).then_inc(s_store[u], 16)

            run_chunks(sp, (load_idx, 0), (load_rest, 1), (store, 6))
            for u in range(SLOTS):
                sp.wait_ge(s_store[u], 16 * len(range(u, NCH, SLOTS)))

        @block.gpsimd
        def _(pool):
            def fetch(c, q, u):
                pool.wait_ge(s_idx[u], 16 * (q + 1))
                if reused(c, SLOTS):
                    pool.wait_ge(s_scaled, c - SLOTS + 1)
                gather(pool, s_src[u], src[:, u, :], F, D["x2"], idx[:, u, :])

            run_chunks(pool, (fetch, 0))

        @block.vector
        def _(dve):
            def types(c, q, u):
                dve.wait_ge(s_rel[u], 16 * (q + 1))
                if reused(c, 2):
                    dve.wait_ge(s_coef, c - 1)
                dve.tensor_scalar(hot[:, u % 2, :], rel[:, u, :], S["iota_p"][0:NREL, 0:1], None, ALU.is_equal).then_inc(s_hot, 1)

            def scale(c, q, u):
                dve.wait_ge(s_coef, c + 1)
                dve.wait_ge(s_src[u], 16 * K * (q + 1))
                if reused(c, 2):
                    dve.wait_ge(s_turned, c - 1)
                row = src[:, u, :].rearrange("p (k f) -> p k f", k=K)
                c4 = ps_c[:, 0:K * NBASE].rearrange("p (k b) -> p k b", k=K)
                dve.tensor_tensor(scaled[:, u % 2, :, :, :], row.unsqueeze(2).to_broadcast([P, K, NBASE, F]),
                                  c4.unsqueeze(3).to_broadcast([P, K, NBASE, F]), ALU.mult).then_inc(s_scaled, 1)

            def scan(c, q, u):
                dve.wait_ge(s_mm, c + 1)
                dve.wait_ge(s_keep[u], 16 * (q + 1))
                if reused(c, SLOTS):
                    dve.wait_ge(s_back, c - SLOTS + 1)
                carry = 0.0
                if reused(c, 1):
                    dve.wait_ge(s_scan, c)
                    carry = run[:, (u - 1) % SLOTS, CH - 1:CH]
                dve.tensor_tensor_scan(run[:, u, :], keep[:, u, :], ps_m[:, :], carry, ALU.mult, ALU.add).then_inc(s_scan, 1)

            run_chunks(dve, (types, 0), (scale, 1), (scan, 3))

        @block.tensor
        def _(pe):
            pe.wait_ge(s_w, 16 * (NBASE + 1))

            def coefficients(c, q, u):
                pe.wait_ge(s_hot, c + 1)
                if reused(c, 1):
                    pe.wait_ge(s_scaled, c)
                cols = hot[:, u % 2, :].rearrange("t (p k) -> t k p", k=K)
                for k in range(K):
                    ins = pe.matmul(ps_c[:, k * NBASE:(k + 1) * NBASE], cols[:, k, :], coef[:, :], start=True, stop=True)
                ins.then_inc(s_coef, 1)

            def turn(c, q, u):
                pe.wait_ge(s_scaled, c + 1)
                for b in range(NBASE):
                    if reused(c, 1):
                        pe.wait_ge(s_T, NBASE * (c - 1) + b + 1)
                    bank = ps_s[b][:, :].rearrange("f (p k) -> f k p", k=K)
                    for k in range(K):
                        ins = pe.transpose(bank[:, k, :], scaled[:, u % 2, k, b, :], S["ident"][:, :])
                    if b < NBASE - 1:
                        ins.then_inc(s_half, 1)
                ins.then_inc(s_turned, 1)

            def multiply(c, q, u):
                pe.wait_ge(s_T, NBASE * (c + 1))
                if reused(c, 1):
                    pe.wait_ge(s_scan, c)
                for b in range(NBASE):
                    ins = pe.matmul(ps_m[:, :], basis[:, b, :], sT[:, u % 2, b, :], start=(b == 0), stop=(b == NBASE - 1))
                ins.then_inc(s_mm, 1)

            def back(c, q, u):
                pe.wait_ge(s_scan, c + 1)
                if reused(c, 2):
                    pe.wait_ge(s_out, c - 1)
                cols = run[:, u, :].rearrange("f (p k) -> f k p", k=K)
                for k in range(K):
                    ins = pe.transpose(ps_o[u % 2][:, k * F:(k + 1) * F], cols[:, k, :], S["ident"][:, :])
                ins.then_inc(s_back, 1)

            run_chunks(pe, (coefficients, 0), (turn, 1), (multiply, 2), (back, 3))

        @block.scalar
        def _(act):
            def copy(c, q, u):
                if reused(c, 2):
                    act.wait_ge(s_mm, c - 1)
                for b in range(NBASE):
                    if b < NBASE - 1:
                        act.wait_ge(s_half, (NBASE - 1) * c + b + 1)
                    else:
                        act.wait_ge(s_turned, c + 1)
                    act.activation(sT[:, u % 2, b, :], ps_s[b][:, :], ACT.Copy).then_inc(s_T, 1)

            def leave(c, q, u):
                act.wait_ge(s_back, c + 1)
                if reused(c, SLOTS):
                    act.wait_ge(s_store[u], 16 * q)
                act.activation(out[:, u, :], ps_o[u % 2][:, :], ACT.Copy).then_inc(s_out, 1)

            run_chunks(act, (copy, 1), (leave, 3))


def node_relations(nc, D, S):
    with ExitStack() as ctx:
        r = Room(nc, ctx, "n2")
        loop = r.sb("loop", [P, F])
        w = r.sb("w", [P, F])
        wT = r.sb("wT", [P, F])
        att = r.sb("att", [P, 2])
        heads = r.sb("heads", [P, 2 * H])
        wcat = r.sb("wcat", [P, W3])
        idx = r.sb("idx", [P, SLOTS, K], i32)
        deg = r.sb("deg", [P, SLOTS, K])
        sdeg = r.sb("sdeg", [P, SLOTS, K])
        rdeg = r.sb("rdeg", [P, SLOTS, K])
        agg = r.sb("agg", [P, SLOTS, CH])
        x = r.sb("x", [P, SLOTS, CH])
        xT = r.sb("xT", [P, 2, CH])
        pre = r.sb("pre", [P, 2, CH])
        y = r.sb("y", [P, SLOTS, CH])
        stats = r.sb("stats", [P, SLOTS, K * 6])
        mv = r.sb("mv", [P, SLOTS, K, 2])
        sd = r.sb("sd", [P, SLOTS, K])
        rs = r.sb("rs", [P, SLOTS, K])
        out = r.sb("out", [P, SLOTS, CH])
        oT = r.sb("oT", [P, 2, CH])
        tab = r.sb("tab", [P, SLOTS, K * W3])
        ps_x = [r.ps(f"x{i}") for i in range(2)]
        ps_o = [r.ps(f"o{i}") for i in range(2)]
        ps_y = r.ps("y")
        ps_h = [r.ps(f"h{i}") for i in range(2)]
        ps_r = r.ps("r")
        s_w = r.sem("w")
        s_heads = r.sem("heads")
        s_wps = r.sem("wps")
        s_wT = r.sem("wT")
        s_wps2 = r.sem("wps2")
        s_wcat = r.sem("wcat")
        s_idx = r.sems("idx")
        s_x = r.sems("x")
        s_deg = r.sems("deg")
        s_agg = r.sems("agg")
        s_store = r.sems("store")
        s_tab_store = r.sems("tab_store")
        s_sdeg = r.sem("sdeg")
        s_rdeg = r.sem("rdeg")
        s_turned = r.sem("turned")
        s_T = r.sem("T")
        s_mm = r.sem("mm")
        s_pre = r.sem("pre")
        s_y = r.sem("y")
        s_st = r.sem("st")
        s_mv = r.sem("mv")
        s_sd = r.sem("sd")
        s_rs = r.sem("rs")
        s_out = r.sem("out")
        s_yturned = r.sem("yturned")
        s_yT = r.sem("yT")
        s_tab = r.sem("tab")
        s_tabbed = r.sem("tabbed")
        s_rst = r.sem("rst")
        ctx.callback(r.close)
        block = ctx.enter_context(nc.Block())

        @block.sync
        def _(sp):
            sp.dma_start(loop[:, :], D["L2_gnn_loop_weight"]).then_inc(s_w, 16)
            sp.dma_start(w[:, :], D["L3_gnn_W"]).then_inc(s_w, 16)
            sp.dma_start(S["res_w"][:, :], D["L3_gnn_res_W"]).then_inc(s_w, 16)
            sp.dma_start(att[:, 0:1], D["L3_gnn_att_src"].rearrange("h c -> (h c)").unsqueeze(1)).then_inc(s_w, 16)
            sp.dma_start(att[:, 1:2], D["L3_gnn_att_dst"].rearrange("h c -> (h c)").unsqueeze(1)).then_inc(s_w, 16)

            def load_idx(c, q, u):
                if reused(c, SLOTS):
                    sp.wait_ge(s_agg[u], 16 * K * q)
                sp.nop(nofuse=True)
                sp.dma_start(idx[:, u, :], vec(D["last"], c)).then_inc(s_idx[u], 16)

            def load_x(c, q, u):
                if reused(c, SLOTS):
                    sp.wait_ge(s_y, c - SLOTS + 1)
                sp.nop(nofuse=True)
                sp.dma_start(x[:, u, :], rows(D["x2"], c)).then_inc(s_x[u], 16)
                if reused(c, SLOTS):
                    sp.wait_ge(s_sdeg, c - SLOTS + 1)
                sp.nop(nofuse=True)
                sp.dma_start(deg[:, u, :], vec(D["deg"], c)).then_inc(s_deg[u], 16)

            def store(c, q, u):
                sp.wait_ge(s_out, c + 1)
                sp.nop(nofuse=True)
                sp.dma_start(rows(D["x3"], c), out[:, u, :]).then_inc(s_store[u], 16)

            def store_table(c, q, u):
                sp.wait_ge(s_tabbed, 2 * (c + 1))
                sp.nop(nofuse=True)
                sp.dma_start(rows(D["table"], c), tab[:, u, :]).then_inc(s_tab_store[u], 16)
                four = tab[:, u, :].rearrange("p (k f) -> p k f", k=K)[:, :, F + H:W3]
                sp.dma_start(rows(D["a_dst"], c).rearrange("p (k h) -> p k h", k=K), four).then_inc(s_tab_store[u], 16)

            run_chunks(sp, (load_idx, 0), (load_x, 2), (store, 7), (store_table, 9))
            for u in range(SLOTS):
                sp.wait_ge(s_store[u], 16 * len(range(u, NCH, SLOTS)))
                sp.wait_ge(s_tab_store[u], 32 * len(range(u, NCH, SLOTS)))

        @block.gpsimd
        def _(pool):
            def fetch(c, q, u):
                pool.wait_ge(s_idx[u], 16 * (q + 1))
                if reused(c, SLOTS):
                    pool.wait_ge(s_pre, c - SLOTS + 1)
                gather(pool, s_agg[u], agg[:, u, :], F, D["agg"], idx[:, u, :])

            run_chunks(pool, (fetch, 0))

        @block.tensor
        def _(pe):
            pe.wait_ge(s_w, 80)
            pe.transpose(ps_h[0][:, 0:P], w[:, :], S["ident"][:, :]).then_inc(s_wps, 1)
            pe.wait_ge(s_wT, 1)
            pe.wait_ge(s_heads, 2)
            pe.matmul(ps_h[1][:, 0:2 * H], wT[:, :], heads[:, :], start=True, stop=True).then_inc(s_wps2, 1)

            def turn(c, q, u):
                pe.wait_ge(s_x[u], 16 * (q + 1))
                if reused(c, 2):
                    pe.wait_ge(s_T, c - 1)
                for k in range(K):
                    ins = pe.transpose(ps_x[u % 2][:, k * P:(k + 1) * P], x[:, u, k * F:(k + 1) * F], S["ident"][:, :])
                ins.then_inc(s_turned, 1)

            def multiply(c, q, u):
                pe.wait_ge(s_T, c + 1)
                if reused(c, 2):
                    pe.wait_ge(s_pre, c - 1)
                for k in range(K):
                    ins = pe.matmul(ps_o[u % 2][:, k * F:(k + 1) * F], xT[:, u % 2, k * P:(k + 1) * P], loop[:, :],
                                    start=True, stop=True)
                ins.then_inc(s_mm, 1)

            def turn_out(c, q, u):
                pe.wait_ge(s_out, c + 1)
                if reused(c, 1):
                    pe.wait_ge(s_yT, c)
                for k in range(K):
                    ins = pe.transpose(ps_y[:, k * P:(k + 1) * P], out[:, u, k * F:(k + 1) * F], S["ident"][:, :])
                ins.then_inc(s_yturned, 1)

            def table(c, q, u):
                pe.wait_ge(s_yT, c + 1)
                if not reused(c, 1):
                    pe.wait_ge(s_wcat, 2)
                for half in range(2):
                    if reused(c, 1):
                        pe.wait_ge(s_tabbed, 2 * c - 1 + half)
                    for k in (2 * half, 2 * half + 1):
                        ins = pe.matmul(ps_h[half][:, (k % 2) * W3:(k % 2 + 1) * W3], oT[:, u % 2, k * P:(k + 1) * P],
                                        wcat[:, :], start=True, stop=True)
                    if half == 0:
                        ins.then_inc(s_tab, 1)
                ins.then_inc(s_tab, 1)
                if reused(c, 1):
                    pe.wait_ge(s_rst, c)
                pe.matmul(ps_r[:, :], S["res_w"][:, :], oT[:, u % 2, :], start=True, stop=True).then_inc(s_tab, 1)

            run_chunks(pe, (turn, 0), (multiply, 1), (turn_out, 4), (table, 5))

        @block.scalar
        def _(act):
            act.wait_ge(s_wps, 1)
            act.activation(wT[:, :], ps_h[0][:, 0:P], ACT.Copy).then_inc(s_wT, 1)
            act.wait_ge(s_w, 80)
            act.activation(wcat[:, 0:F], w[:, :], ACT.Copy).then_inc(s_wcat, 1)
            act.wait_ge(s_wps2, 1)
            act.activation(wcat[:, F:W3], ps_h[1][:, 0:2 * H], ACT.Copy).then_inc(s_wcat, 1)

            def root(c, q, u):
                act.wait_ge(s_deg[u], 16 * (q + 1))
                if reused(c, SLOTS):
                    act.wait_ge(s_rdeg, c - SLOTS + 1)
                act.activation(sdeg[:, u, :], deg[:, u, :], ACT.Sqrt).then_inc(s_sdeg, 1)

            def copy(c, q, u):
                act.wait_ge(s_turned, c + 1)
                if reused(c, 2):
                    act.wait_ge(s_mm, c - 1)
                act.activation(xT[:, u % 2, :], ps_x[u % 2][:, :], ACT.Copy).then_inc(s_T, 1)

            def deviation(c, q, u):
                act.wait_ge(s_mv, c + 1)
                act.activation(sd[:, u, :], mv[:, u, :, 1], ACT.Sqrt, bias=S["eps"][:, 0:1]).then_inc(s_sd, 1)

            def copy_out(c, q, u):
                act.wait_ge(s_yturned, c + 1)
                if reused(c, 2):
                    act.wait_ge(s_tab, 3 * (c - 1))
                act.activation(oT[:, u % 2, :], ps_y[:, :], ACT.Copy).then_inc(s_yT, 1)

            def copy_table(c, q, u):
                if reused(c, SLOTS):
                    act.wait_ge(s_tab_store[u], 32 * q)
                for half in range(2):
                    act.wait_ge(s_tab, 3 * c + 1 + half)
                    act.activation(tab[:, u, half * 2 * W3:(half + 1) * 2 * W3], ps_h[half][:, 0:2 * W3],
                                   ACT.Copy).then_inc(s_tabbed, 1)

            run_chunks(act, (deviation, 3), (root, 0), (copy, 0), (copy_out, 4), (copy_table, 5))

        @block.vector
        def _(dve):
            dve.wait_ge(s_w, 80)
            for j in range(2):
                dve.tensor_scalar(heads[:, j * H:(j + 1) * H], S["head"][:, :], att[:, j:j + 1], None, ALU.mult).then_inc(s_heads, 1)

            def invert(c, q, u):
                dve.wait_ge(s_sdeg, c + 1)
                if reused(c, SLOTS):
                    dve.wait_ge(s_pre, c - SLOTS + 1)
                dve.reciprocal(rdeg[:, u, :], sdeg[:, u, :]).then_inc(s_rdeg, 1)

            def residual(c, q, u):
                dve.wait_ge(s_mm, c + 1)
                dve.wait_ge(s_rdeg, c + 1)
                dve.wait_ge(s_agg[u], 16 * K * (q + 1))
                for k in range(K):
                    f = slice(k * F, (k + 1) * F)
                    ins = dve.scalar_tensor_tensor(pre[:, u % 2, f], agg[:, u, f], rdeg[:, u, k:k + 1], ps_o[u % 2][:, f], ALU.mult, ALU.add)
                ins.then_inc(s_pre, 1)
                dve.wait_ge(s_pre, c + 1)
                dve.scalar_tensor_tensor(y[:, u, :], pre[:, u % 2, :], 0.0, x[:, u, :], ALU.max, ALU.add).then_inc(s_y, 1)
                dve.wait_ge(s_y, c + 1)
                layer_norm_ready(dve, y[:, u, :], stats[:, u, :], mv[:, u, :, :], s_st, c + 1).then_inc(s_mv, 1)

            def normalise(c, q, u):
                dve.wait_ge(s_sd, c + 1)
                dve.reciprocal(rs[:, u, :], sd[:, u, :]).then_inc(s_rs, 1)
                dve.wait_ge(s_rs, c + 1)
                if reused(c, SLOTS):
                    dve.wait_ge(s_store[u], 16 * q)
                    dve.wait_ge(s_yturned, c - SLOTS + 1)
                for k in range(K):
                    f = slice(k * F, (k + 1) * F)
                    ins = dve.tensor_scalar(out[:, u, f], y[:, u, f], mv[:, u, k, 0:1], rs[:, u, k:k + 1], ALU.subtract, ALU.mult)
                ins.then_inc(s_out, 1)

            def statistics(c, q, u):
                dve.wait_ge(s_tab, 3 * (c + 1))
                real = isinstance(c, int) and c == NCH - 1
                seen = ps_r[:, :].rearrange("f (k p) -> f k p", k=K)[:, :, 0:LAST // K] if real else ps_r[:, :]
                dve.nop(nofuse=True)
                dve.bn_stats(S["res_stats"][:, bass.ds(c * 6, 6)], seen).then_inc(s_rst, 1)

            run_chunks(dve, (invert, 0), (residual, 2), (normalise, 3), (statistics, 6))


def edge_attention(nc, D, S):
    with ExitStack() as ctx:
        r = Room(nc, ctx, "e3")
        idx = r.sb("idx", [P, SLOTS, 2 * K], i32)
        gate = r.sb("gate", [P, SLOTS, CH], bf16)
        src = r.sb("src", [P, SLOTS, K * W3])
        dst = r.sb("dst", [P, SLOTS, K * H])
        lin = r.sb("lin", [P, 2, K, H])
        logit = r.sb("logit", [P, 2, K, H])
        wide = r.sb("wide", [P, 2, K, F])
        top = r.sb("top", [P, SLOTS, 1 + CH])
        moved = r.sb("moved", [P, 2, CH])
        decay = r.sb("decay", [P, 2, 2, CH])
        grow = r.sb("grow", [P, 2, 2, CH])
        wrow = r.sb("wrow", [P, 2, CH])
        den = r.sb("den", [P, SLOTS, CH])
        num = r.sb("num", [P, SLOTS, CH])
        out = r.sb("out", [P, SLOTS, K * W3])
        ps_h = [r.ps(f"h{i}") for i in range(2)]
        ps_a = [r.ps(f"a{i}") for i in range(2)]
        ps_o = [r.ps(f"o{i}") for i in range(2)]
        ps_d = [r.ps(f"d{i}") for i in range(2)]
        s_idx = r.sems("idx")
        s_gate = r.sems("gate")
        s_rows = r.sems("rows")
        s_store = r.sems("store")
        s_first = r.sem("first")
        s_lin = r.sem("lin")
        s_logit = r.sem("logit")
        s_wide = r.sem("wide")
        s_turned = r.sem("turned")
        s_top = r.sem("top")
        s_moved = r.sem("moved")
        s_diff = r.sem("diff")
        s_exp = r.sem("exp")
        s_wrow = r.sem("wrow")
        s_scan = r.sem("scan")
        s_back = r.sem("back")
        s_out = r.sem("out")
        ctx.callback(r.close)
        block = ctx.enter_context(nc.Block())

        @block.sync
        def _(sp):
            def load_idx(c, q, u):
                if reused(c, SLOTS):
                    sp.wait_ge(s_rows[u], 16 * 2 * K * q)
                sp.nop(nofuse=True)
                sp.dma_start(idx[:, u, 0:K], vec(D["src"], c)).then_inc(s_idx[u], 16)
                sp.dma_start(idx[:, u, K:2 * K], vec(D["dst"][1:NP + 1], c)).then_inc(s_idx[u], 16)

            def load_gate(c, q, u):
                if reused(c, SLOTS):
                    sp.wait_ge(s_moved, c - SLOTS + 1)
                sp.nop(nofuse=True)
                sp.dma_start(gate[:, u, :], spread(D["gate"], c, P)).then_inc(s_gate[u], 16)

            def store(c, q, u):
                sp.wait_ge(s_out, c + 1)
                sp.nop(nofuse=True)
                sp.dma_start(rows(D["att"], c), out[:, u, :]).then_inc(s_store[u], 16)

            run_chunks(sp, (load_idx, 0), (load_gate, 1), (store, 5))
            for u in range(SLOTS):
                sp.wait_ge(s_store[u], 16 * len(range(u, NCH, SLOTS)))

        @block.gpsimd
        def _(pool):
            def fetch(c, q, u):
                pool.wait_ge(s_idx[u], 32 * (q + 1))
                if reused(c, SLOTS):
                    pool.wait_ge(s_lin, c - SLOTS + 1)
                    pool.wait_ge(s_turned, c - SLOTS + 1)
                gather(pool, s_rows[u], src[:, u, :], W3, D["table"], idx[:, u, 0:K])
                gather(pool, s_rows[u], dst[:, u, :], H, D["a_dst"], idx[:, u, K:2 * K])

            run_chunks(pool, (fetch, 0))

        @block.vector
        def _(dve):
            dve.memset(top[:, 0, 0:1], -BIG).then_inc(s_first, 1)

            def logits(c, q, u):
                dve.wait_ge(s_rows[u], 16 * 2 * K * (q + 1))
                a_src = src[:, u, :].rearrange("p (k f) -> p k f", k=K)[:, :, F:F + H]
                a_dst = dst[:, u, :].rearrange("p (k h) -> p k h", k=K)
                dve.tensor_tensor(lin[:, u % 2, :, :], a_src, a_dst, ALU.add).then_inc(s_lin, 1)
                dve.wait_ge(s_lin, c + 1)
                dve.scalar_tensor_tensor(logit[:, u % 2, :, :], lin[:, u % 2, :, :], 0.2, lin[:, u % 2, :, :], ALU.mult, ALU.max).then_inc(s_logit, 1)

            def maximum(c, q, u):
                dve.wait_ge(s_turned, c + 1)
                dve.wait_ge(s_gate[u], 16 * (q + 1))
                if reused(c, 1):
                    if reused(c, SLOTS):
                        dve.wait_ge(s_back, c - SLOTS + 1)
                    dve.wait_ge(s_top, c)
                    dve.tensor_copy(top[:, u, 0:1], top[:, (u - 1) % SLOTS, CH:CH + 1]).then_inc(s_first, 1)
                dve.wait_ge(s_first, c + 1)
                dve.tensor_tensor_scan(top[:, u, 1:CH + 1], gate[:, u, :], ps_a[u % 2][:, :], top[:, u, 0:1], ALU.add, ALU.max).then_inc(s_top, 1)
                dve.wait_ge(s_top, c + 1)
                if reused(c, 2):
                    dve.wait_ge(s_exp, c - 1)
                dve.tensor_tensor(moved[:, u % 2, :], top[:, u, 0:CH], gate[:, u, :], ALU.add).then_inc(s_moved, 1)
                dve.tensor_tensor(grow[:, u % 2, 0, :], ps_a[u % 2][:, :], top[:, u, 1:CH + 1], ALU.subtract)
                dve.wait_ge(s_moved, c + 1)
                dve.tensor_tensor(decay[:, u % 2, 0, :], moved[:, u % 2, :], top[:, u, 1:CH + 1], ALU.subtract).then_inc(s_diff, 1)

            def sums(c, q, u):
                dve.wait_ge(s_exp, c + 1)
                dve.tensor_tensor(wrow[:, u % 2, :], grow[:, u % 2, 1, :], ps_h[u % 2][:, :], ALU.mult).then_inc(s_wrow, 1)
                if reused(c, SLOTS):
                    dve.wait_ge(s_back, c - SLOTS + 1)
                first, second = 0.0, 0.0
                if reused(c, 1):
                    dve.wait_ge(s_scan, 2 * c)
                    first = den[:, (u - 1) % SLOTS, CH - 1:CH]
                    second = num[:, (u - 1) % SLOTS, CH - 1:CH]
                dve.tensor_tensor_scan(den[:, u, :], decay[:, u % 2, 1, :], grow[:, u % 2, 1, :], first, ALU.mult, ALU.add).then_inc(s_scan, 1)
                dve.wait_ge(s_wrow, c + 1)
                dve.tensor_tensor_scan(num[:, u, :], decay[:, u % 2, 1, :], wrow[:, u % 2, :], second, ALU.mult, ALU.add).then_inc(s_scan, 1)

            run_chunks(dve, (logits, 0), (maximum, 1), (sums, 2))

        @block.tensor
        def _(pe):
            def turn(c, q, u):
                pe.wait_ge(s_wide, c + 1)
                if reused(c, 2):
                    pe.wait_ge(s_wrow, c - 1)
                    pe.wait_ge(s_diff, c - 1)
                bank = ps_h[u % 2][:, :].rearrange("f (p k) -> f k p", k=K)
                for k in range(K):
                    pe.transpose(bank[:, k, :], src[:, u, k * W3:k * W3 + F], S["ident"][:, :])
                bank = ps_a[u % 2][:, :].rearrange("f (p k) -> f k p", k=K)
                for k in range(K):
                    ins = pe.transpose(bank[:, k, :], wide[:, u % 2, k, :], S["ident"][:, :])
                ins.then_inc(s_turned, 1)

            def back(c, q, u):
                pe.wait_ge(s_scan, 2 * (c + 1))
                if reused(c, 2):
                    pe.wait_ge(s_out, c - 1)
                cols = num[:, u, :].rearrange("f (p k) -> f k p", k=K)
                for k in range(K):
                    pe.transpose(ps_o[u % 2][:, k * F:(k + 1) * F], cols[:, k, :], S["ident"][:, :])
                cols = [t.rearrange("f (p k) -> f k p", k=K) for t in (den[:, u, :], top[:, u, 1:CH + 1])]
                for k in range(K):
                    for j in range(2):
                        at = (2 * k + j) * H
                        ins = pe.matmul(ps_d[u % 2][:, at:at + H], cols[j][:, k, :], S["head_first"][:, :], start=True, stop=True)
                ins.then_inc(s_back, 1)

            run_chunks(pe, (turn, 0), (back, 3))

        @block.scalar
        def _(act):
            def widen(c, q, u):
                act.wait_ge(s_logit, c + 1)
                if reused(c, 2):
                    act.wait_ge(s_turned, c - 1)
                flat = logit[:, u % 2, :, :].rearrange("p k h -> p (k h)")
                act.activation(wide[:, u % 2, :, :].rearrange("p k (h c) -> p (k h) c", h=H),
                               flat.unsqueeze(2).to_broadcast([P, K * H, HC]), ACT.Copy).then_inc(s_wide, 1)

            def exponentials(c, q, u):
                act.wait_ge(s_diff, c + 1)
                if reused(c, 2):
                    act.wait_ge(s_scan, 2 * (c - 1))
                act.activation(grow[:, u % 2, 1, :], grow[:, u % 2, 0, :], ACT.Exp)
                act.activation(decay[:, u % 2, 1, :], decay[:, u % 2, 0, :], ACT.Exp).then_inc(s_exp, 1)

            def leave(c, q, u):
                act.wait_ge(s_back, c + 1)
                if reused(c, SLOTS):
                    act.wait_ge(s_store[u], 16 * q)
                row = out[:, u, :].rearrange("p (k f) -> p k f", k=K)
                act.activation(row[:, :, 0:F], ps_o[u % 2][:, :].rearrange("p (k f) -> p k f", k=K), ACT.Copy)
                act.activation(row[:, :, F:W3], ps_d[u % 2][:, 0:K * 2 * H].rearrange("p (k f) -> p k f", k=K),
                               ACT.Copy).then_inc(s_out, 1)

            run_chunks(act, (widen, 0), (exponentials, 1), (leave, 3))


def node_attention(nc, D, S):
    with ExitStack() as ctx:
        r = Room(nc, ctx, "n3")
        bias = r.sb("bias", [1, K, F])
        idx = r.sb("idx", [P, SLOTS, K], i32)
        agg = r.sb("agg", [P, SLOTS, K * W3])
        own = r.sb("own", [P, SLOTS, K * W3])
        t = {n: r.sb(n, [P, 2, K, H]) for n in ("lin", "logit", "top", "den", "rden")}
        ex = r.sb("ex", [P, 2, 2, K * H])
        wgt = r.sb("wgt", [P, 2, 2, K * H])
        part = r.sb("part", [P, 2, 2, CH])
        out = r.sb("out", [P, SLOTS, CH])
        ps_o = [r.ps(f"o{i}") for i in range(2)]
        ps_t = [r.ps(f"t{i}") for i in range(2)]
        s_bias = r.sem("bias")
        s_idx = r.sems("idx")
        s_agg = r.sems("agg")
        s_own = r.sems("own")
        s_store = r.sems("store")
        s_step = r.sem("step")
        s_fold = r.sem("fold")
        s_arg = r.sem("arg")
        s_exp = r.sem("exp")
        s_wgt = r.sem("wgt")
        s_part = r.sem("part")
        s_mm = r.sem("mm")
        s_out = r.sem("out")
        s_turned = r.sem("turned")
        s_stats = r.sem("stats")
        ctx.callback(r.close)
        block = ctx.enter_context(nc.Block())

        @block.sync
        def _(sp):
            for k in range(K):
                sp.dma_start(bias[:, k, :], D["L3_gnn_bias"].unsqueeze(0)).then_inc(s_bias, 16)

            def load_idx(c, q, u):
                if reused(c, SLOTS):
                    sp.wait_ge(s_agg[u], 16 * K * q)
                sp.nop(nofuse=True)
                sp.dma_start(idx[:, u, :], vec(D["last"], c)).then_inc(s_idx[u], 16)

            def load_own(c, q, u):
                if reused(c, SLOTS):
                    sp.wait_ge(s_part, c - SLOTS + 1)
                sp.nop(nofuse=True)
                sp.dma_start(own[:, u, :], rows(D["table"], c)).then_inc(s_own[u], 16)

            def store(c, q, u):
                sp.wait_ge(s_out, c + 1)
                sp.nop(nofuse=True)
                sp.dma_start(rows(D["gat"], c), out[:, u, :]).then_inc(s_store[u], 16)

            run_chunks(sp, (load_idx, 0), (load_own, 2), (store, 6))
            for u in range(SLOTS):
                sp.wait_ge(s_store[u], 16 * len(range(u, NCH, SLOTS)))

        @block.gpsimd
        def _(pool):
            def fetch(c, q, u):
                pool.wait_ge(s_idx[u], 16 * (q + 1))
                if reused(c, SLOTS):
                    pool.wait_ge(s_part, c - SLOTS + 1)
                gather(pool, s_agg[u], agg[:, u, :], W3, D["att"], idx[:, u, :])

            run_chunks(pool, (fetch, 0))

        @block.vector
        def _(dve):
            def cut(buf, u, a, b):
                return buf[:, u, :].rearrange("p (k f) -> p k f", k=K)[:, :, a:b]

            def four(name, v):
                return t[name][:, v, :, :]

            def exponents(c, q, u):
                v = u % 2
                dve.wait_ge(s_own[u], 16 * (q + 1))
                dve.wait_ge(s_agg[u], 16 * K * (q + 1))
                dve.tensor_tensor(four("lin", v), cut(own, u, F, F + H), cut(own, u, F + H, W3), ALU.add).then_inc(s_step, 1)
                dve.wait_ge(s_step, 3 * c + 1)
                dve.scalar_tensor_tensor(four("logit", v), four("lin", v), 0.2, four("lin", v), ALU.mult, ALU.max).then_inc(s_step, 1)
                dve.wait_ge(s_step, 3 * c + 2)
                dve.tensor_tensor(four("top", v), cut(agg, u, F + H, W3), four("logit", v), ALU.max).then_inc(s_step, 1)
                dve.wait_ge(s_step, 3 * c + 3)
                pair = ex[:, v, :, :].rearrange("p j (k h) -> p j k h", k=K)
                dve.tensor_tensor(pair[:, 0, :, :], cut(agg, u, F + H, W3), four("top", v), ALU.subtract)
                dve.tensor_tensor(pair[:, 1, :, :], four("logit", v), four("top", v), ALU.subtract).then_inc(s_arg, 1)

            def weigh(c, q, u):
                v = u % 2
                dve.wait_ge(s_exp, c + 1)
                pair = ex[:, v, :, :].rearrange("p j (k h) -> p j k h", k=K)
                dve.tensor_tensor(four("den", v), cut(agg, u, F, F + H), pair[:, 0, :, :], ALU.mult).then_inc(s_fold, 1)
                dve.wait_ge(s_fold, 3 * c + 1)
                dve.tensor_tensor(four("den", v), four("den", v), pair[:, 1, :, :], ALU.add).then_inc(s_fold, 1)
                dve.wait_ge(s_fold, 3 * c + 2)
                dve.reciprocal(four("rden", v), four("den", v)).then_inc(s_fold, 1)
                dve.wait_ge(s_fold, 3 * c + 3)
                flat = four("rden", v).rearrange("p k h -> p (k h)")
                for j in range(2):
                    ins = dve.tensor_tensor(wgt[:, v, j, :], ex[:, v, j, :], flat, ALU.mult)
                ins.then_inc(s_wgt, 1)
                dve.wait_ge(s_wgt, c + 1)
                if reused(c, 2):
                    dve.wait_ge(s_mm, c - 1)
                for j, rows_ in ((0, agg), (1, own)):
                    w4 = wgt[:, v, j, :].rearrange("p (k h) -> p k h", k=K).unsqueeze(3).to_broadcast([P, K, H, HC])
                    ins = dve.tensor_tensor(part[:, v, j, :].rearrange("p (k h c) -> p k h c", k=K, h=H),
                                            cut(rows_, u, 0, F).rearrange("p k (h c) -> p k h c", h=H), w4, ALU.mult)
                ins.then_inc(s_part, 1)

            def statistics(c, q, u):
                dve.wait_ge(s_turned, c + 1)
                bank = ps_t[u % 2]
                real = isinstance(c, int) and c == NCH - 1
                seen = bank[:, :].rearrange("f (k p) -> f k p", k=K)[:, :, 0:LAST // K] if real else bank[:, :]
                dve.nop(nofuse=True)
                dve.bn_stats(S["gat_stats"][:, bass.ds(c * 6, 6)], seen).then_inc(s_stats, 1)

            run_chunks(dve, (exponents, 0), (weigh, 1), (statistics, 4))

        @block.scalar
        def _(act):
            def exponentials(c, q, u):
                act.wait_ge(s_arg, c + 1)
                both = ex[:, u % 2, :, :].rearrange("p j k -> p (j k)")
                act.activation(both, both, ACT.Exp).then_inc(s_exp, 1)

            def leave(c, q, u):
                act.wait_ge(s_mm, c + 1)
                if reused(c, SLOTS):
                    act.wait_ge(s_store[u], 16 * q)
                    act.wait_ge(s_turned, c - SLOTS + 1)
                act.activation(out[:, u, :], ps_o[u % 2][:, :], ACT.Copy).then_inc(s_out, 1)

            run_chunks(act, (exponentials, 0), (leave, 2))

        @block.tensor
        def _(pe):
            pe.wait_ge(s_bias, 16 * K)

            def add(c, q, u):
                pe.wait_ge(s_part, c + 1)
                if reused(c, 2):
                    pe.wait_ge(s_out, c - 1)
                pe.matmul(ps_o[u % 2][:, :], S["ident"][:, :], part[:, u % 2, 0, :], start=True, stop=False)
                pe.matmul(ps_o[u % 2][:, :], S["ident"][:, :], part[:, u % 2, 1, :], start=False, stop=False)
                pe.matmul(ps_o[u % 2][:, :], S["ones"][0:1, 0:P], bias[:, :, :].rearrange("p k f -> p (k f)"),
                          start=False, stop=True).then_inc(s_mm, 1)

            def turn(c, q, u):
                pe.wait_ge(s_out, c + 1)
                if reused(c, 2):
                    pe.wait_ge(s_stats, c - 1)
                for k in range(K):
                    ins = pe.transpose(ps_t[u % 2][:, k * P:(k + 1) * P], out[:, u, k * F:(k + 1) * F], S["ident"][:, :])
                ins.then_inc(s_turned, 1)

            run_chunks(pe, (add, 1), (turn, 3))


def finish(nc, D, S):
    with ExitStack() as ctx:
        r = Room(nc, ctx, "fin")
        NC = 7
        cols = r.sb("cols", [P, NC])
        GAM, BET, LG, LB, RB, RG, RBET = range(NC)
        mvs = r.sb("mvs", [P, 2, 2])
        dev = r.sb("dev", [P, 2])
        inv = r.sb("inv", [P, 2])
        mu = r.sb("mu", [P, 1])
        tmp = r.sb("tmp", [P, 3])
        vecs = r.sb("vecs", [P, 5])
        diag = r.sb("diag", [P, 5, P])
        scale_row = r.sb("scale_row", [P, CH])
        shift_row = r.sb("shift_row", [P, CH])
        gamma_row = r.sb("gamma_row", [P, CH])
        wres = r.sb("wres", [P, F])
        tres = r.sb("tres", [1, F])
        g = r.sb("g", [P, SLOTS, CH])
        x = r.sb("x", [P, SLOTS, CH])
        z0 = r.sb("z0", [P, 2, CH])
        z = r.sb("z", [P, SLOTS, CH])
        zn = r.sb("zn", [P, 2, CH])
        zg = r.sb("zg", [P, 2, CH])
        xT = r.sb("xT", [P, 2, CH])
        sumv = r.sb("sumv", [P, 2, CH])
        y = r.sb("y", [P, SLOTS, CH])
        act_row = r.sb("act_row", [P, 2, CH])
        out = r.sb("out", [P, SLOTS, CH])
        st = [r.sb(f"st{i}", [P, SLOTS, K * 6]) for i in range(2)]
        mv = [r.sb(f"mv{i}", [P, SLOTS, K, 2]) for i in range(2)]
        sd = [r.sb(f"sd{i}", [P, SLOTS, K]) for i in range(2)]
        rs = [r.sb(f"rs{i}", [P, SLOTS, K]) for i in range(2)]
        ps_x = [r.ps(f"x{i}") for i in range(2)]
        ps_i = [r.ps(f"i{i}") for i in range(2)]
        ps_row = [r.ps(f"row{i}") for i in range(3)]
        s_cols = r.sem("cols")
        s_aggr = r.sem("aggr")
        s_dev = r.sem("dev")
        s_vec = r.sem("vec")
        s_diag = r.sem("diag")
        s_row = r.sem("row")
        s_ready = r.sem("ready")
        s_g = r.sems("g")
        s_x = r.sems("x")
        s_store = r.sems("store")
        s_z0 = r.sem("z0")
        s_z = r.sem("z")
        s_st = [r.sem(f"st{i}") for i in range(2)]
        s_mv = [r.sem(f"mv{i}") for i in range(2)]
        s_sd = [r.sem(f"sd{i}") for i in range(2)]
        s_rs = [r.sem(f"rs{i}") for i in range(2)]
        s_zn = r.sem("zn")
        s_zg = r.sem("zg")
        s_turned = r.sem("turned")
        s_T = r.sem("T")
        s_mm = r.sem("mm")
        s_sum = r.sem("sum")
        s_relu = r.sem("relu")
        s_y = r.sem("y")
        s_out = r.sem("out")
        ctx.callback(r.close)
        block = ctx.enter_context(nc.Block())

        @block.sync
        def _(sp):
            for j, name in enumerate(("bn_gamma", "bn_beta", "ln_gamma", "ln_beta", "res_b", "bnres_gamma", "bnres_beta")):
                sp.dma_start(cols[:, j:j + 1], D[f"L3_gnn_{name}"].unsqueeze(1)).then_inc(s_cols, 16)

            def load_g(c, q, u):
                if reused(c, SLOTS):
                    sp.wait_ge(s_z0, c - SLOTS + 1)
                sp.nop(nofuse=True)
                sp.dma_start(g[:, u, :], rows(D["gat"], c)).then_inc(s_g[u], 16)

            def load_x(c, q, u):
                if reused(c, SLOTS):
                    sp.wait_ge(s_y, c - SLOTS + 1)
                sp.nop(nofuse=True)
                sp.dma_start(x[:, u, :], rows(D["x3"], c)).then_inc(s_x[u], 16)

            def store(c, q, u):
                sp.wait_ge(s_out, c + 1)
                sp.nop(nofuse=True)
                sp.dma_start(rows(D["x4"], c), out[:, u, :]).then_inc(s_store[u], 16)

            run_chunks(sp, (load_g, 0), (load_x, 2), (store, 7))
            for u in range(SLOTS):
                sp.wait_ge(s_store[u], 16 * len(range(u, NCH, SLOTS)))

        @block.gpsimd
        def _(pool):
            pool.wait_ge(s_ready, 5)

            def affine(c, q, u):
                pool.wait_ge(s_g[u], 16 * (q + 1))
                if reused(c, 2):
                    pool.wait_ge(s_z, c - 1)
                pool.tensor_tensor(z0[:, u % 2, :], g[:, u, :], scale_row[:, :], ALU.mult).then_inc(s_z0, 1)
                pool.wait_ge(s_z0, c + 1)
                if reused(c, SLOTS):
                    pool.wait_ge(s_zn, c - SLOTS + 1)
                pool.tensor_tensor(z[:, u, :], z0[:, u % 2, :], shift_row[:, :], ALU.add).then_inc(s_z, 1)

            def gamma(c, q, u):
                pool.wait_ge(s_zn, c + 1)
                if reused(c, 2):
                    pool.wait_ge(s_sum, c - 1)
                pool.tensor_tensor(zg[:, u % 2, :], zn[:, u % 2, :], gamma_row[:, :], ALU.mult).then_inc(s_zg, 1)

            def residual(c, q, u):
                pool.wait_ge(s_relu, c + 1)
                if reused(c, SLOTS):
                    pool.wait_ge(s_out, c - SLOTS + 1)
                pool.tensor_tensor(y[:, u, :], act_row[:, u % 2, :], x[:, u, :], ALU.add).then_inc(s_y, 1)

            run_chunks(pool, (affine, 0), (gamma, 2), (residual, 3))

        @block.vector
        def _(dve):
            chain = [0]

            def link(ins):
                chain[0] += 1
                ins.then_inc(s_vec, 1)
                dve.wait_ge(s_vec, chain[0])

            dve.bn_aggr(mvs[:, 0, :], S["gat_stats"][:, :])
            dve.bn_aggr(mvs[:, 1, :], S["res_stats"][:, :]).then_inc(s_aggr, 1)
            dve.wait_ge(s_dev, 1)
            dve.wait_ge(s_cols, 16 * NC)
            link(dve.reciprocal(inv[:, :], dev[:, :]))
            link(dve.tensor_tensor(vecs[:, 0:1], cols[:, GAM:GAM + 1], inv[:, 0:1], ALU.mult))
            link(dve.tensor_tensor(tmp[:, 0:1], mvs[:, 0, 0:1], vecs[:, 0:1], ALU.mult))
            link(dve.tensor_tensor(vecs[:, 1:2], cols[:, BET:BET + 1], tmp[:, 0:1], ALU.subtract))
            link(dve.tensor_copy(vecs[:, 2:3], cols[:, LG:LG + 1]))
            link(dve.tensor_tensor(vecs[:, 3:4], cols[:, RG:RG + 1], inv[:, 1:2], ALU.mult))
            link(dve.tensor_tensor(mu[:, :], mvs[:, 1, 0:1], cols[:, RB:RB + 1], ALU.add))
            link(dve.tensor_tensor(tmp[:, 1:2], cols[:, RB:RB + 1], mu[:, :], ALU.subtract))
            link(dve.tensor_tensor(tmp[:, 2:3], tmp[:, 1:2], vecs[:, 3:4], ALU.mult))
            link(dve.tensor_tensor(vecs[:, 4:5], tmp[:, 2:3], cols[:, RBET:RBET + 1], ALU.add))
            link(dve.tensor_tensor(vecs[:, 4:5], vecs[:, 4:5], cols[:, LB:LB + 1], ALU.add))
            for j in range(5):
                dve.tensor_scalar(diag[:, j, :], S["ident"][:, :], vecs[:, j:j + 1], None, ALU.mult).then_inc(s_diag, 1)
            dve.wait_ge(s_row, 3)
            for j, row in enumerate((scale_row, shift_row, gamma_row)):
                dve.tensor_copy(row[:, :], ps_row[j][:, :]).then_inc(s_ready, 1)
            dve.wait_ge(s_row, 5)
            dve.tensor_tensor(wres[:, :], S["res_w"][:, :], ps_x[0][:, 0:F], ALU.mult).then_inc(s_ready, 1)
            dve.tensor_copy(tres[:, :], ps_x[1][0:1, 0:F]).then_inc(s_ready, 1)

            def first_norm(c, q, u):
                dve.wait_ge(s_z, c + 1)
                dve.nop(nofuse=True)
                layer_norm_ready(dve, z[:, u, :], st[0][:, u, :], mv[0][:, u, :, :], s_st[0], c + 1).then_inc(s_mv[0], 1)

            def apply_first(c, q, u):
                dve.wait_ge(s_sd[0], c + 1)
                dve.reciprocal(rs[0][:, u, :], sd[0][:, u, :]).then_inc(s_rs[0], 1)
                dve.wait_ge(s_rs[0], c + 1)
                if reused(c, 2):
                    dve.wait_ge(s_zg, c - 1)
                for k in range(K):
                    f = slice(k * F, (k + 1) * F)
                    ins = dve.tensor_scalar(zn[:, u % 2, f], z[:, u, f], mv[0][:, u, k, 0:1], rs[0][:, u, k:k + 1], ALU.subtract, ALU.mult)
                ins.then_inc(s_zn, 1)

            def total(c, q, u):
                dve.wait_ge(s_zg, c + 1)
                dve.wait_ge(s_mm, c + 1)
                if reused(c, 2):
                    dve.wait_ge(s_relu, c - 1)
                dve.tensor_tensor(sumv[:, u % 2, :], zg[:, u % 2, :], ps_i[u % 2][:, :], ALU.add).then_inc(s_sum, 1)

            def second_norm(c, q, u):
                dve.wait_ge(s_y, c + 1)
                dve.nop(nofuse=True)
                layer_norm_ready(dve, y[:, u, :], st[1][:, u, :], mv[1][:, u, :, :], s_st[1], c + 1).then_inc(s_mv[1], 1)

            def apply_second(c, q, u):
                dve.wait_ge(s_sd[1], c + 1)
                dve.reciprocal(rs[1][:, u, :], sd[1][:, u, :]).then_inc(s_rs[1], 1)
                dve.wait_ge(s_rs[1], c + 1)
                if reused(c, SLOTS):
                    dve.wait_ge(s_store[u], 16 * q)
                for k in range(K):
                    f = slice(k * F, (k + 1) * F)
                    ins = dve.tensor_scalar(out[:, u, f], y[:, u, f], mv[1][:, u, k, 0:1], rs[1][:, u, k:k + 1], ALU.subtract, ALU.mult)
                ins.then_inc(s_out, 1)

            run_chunks(dve, (first_norm, 0), (apply_first, 1), (total, 2), (second_norm, 4), (apply_second, 5))

        @block.scalar
        def _(act):
            act.wait_ge(s_aggr, 1)
            act.activation(dev[:, :], mvs[:, :, 1], ACT.Sqrt, bias=S["eps"][:, 0:1]).then_inc(s_dev, 1)

            def deviation(i):
                def work(c, q, u):
                    act.wait_ge(s_mv[i], c + 1)
                    act.activation(sd[i][:, u, :], mv[i][:, u, :, 1], ACT.Sqrt, bias=S["eps"][:, 0:1]).then_inc(s_sd[i], 1)
                return work

            def copy(c, q, u):
                act.wait_ge(s_turned, c + 1)
                if reused(c, 2):
                    act.wait_ge(s_mm, c - 1)
                act.activation(xT[:, u % 2, :], ps_x[u % 2][:, :], ACT.Copy).then_inc(s_T, 1)

            def relu(c, q, u):
                act.wait_ge(s_sum, c + 1)
                if reused(c, 2):
                    act.wait_ge(s_y, c - 1)
                act.activation(act_row[:, u % 2, :], sumv[:, u % 2, :], ACT.Relu).then_inc(s_relu, 1)

            run_chunks(act, (deviation(0), 0), (copy, 0), (relu, 2), (deviation(1), 4))

        @block.tensor
        def _(pe):
            for j in range(3):
                pe.wait_ge(s_diag, j + 1)
                for k in range(K):
                    ins = pe.matmul(ps_row[j][:, k * F:(k + 1) * F], S["ones"][:, 0:P], diag[:, j, :], start=True, stop=True)
                ins.then_inc(s_row, 1)
            for j in range(2):
                pe.wait_ge(s_diag, 4 + j)
                pe.matmul(ps_x[j][:, 0:F], S["ones"][:, 0:P], diag[:, 3 + j, :], start=True, stop=True).then_inc(s_row, 1)
            pe.wait_ge(s_ready, 5)

            def turn(c, q, u):
                pe.wait_ge(s_x[u], 16 * (q + 1))
                if reused(c, 2):
                    pe.wait_ge(s_T, c - 1)
                for k in range(K):
                    ins = pe.transpose(ps_x[u % 2][:, k * P:(k + 1) * P], x[:, u, k * F:(k + 1) * F], S["ident"][:, :])
                ins.then_inc(s_turned, 1)

            def multiply(c, q, u):
                pe.wait_ge(s_T, c + 1)
                if reused(c, 2):
                    pe.wait_ge(s_sum, c - 1)
                for k in range(K):
                    o = ps_i[u % 2][:, k * F:(k + 1) * F]
                    pe.matmul(o, xT[:, u % 2, k * P:(k + 1) * P], wres[:, :], start=True, stop=False)
                    ins = pe.matmul(o, S["ones"][0:1, 0:P], tres[:, :], start=False, stop=True)
                ins.then_inc(s_mm, 1)

            run_chunks(pe, (turn, 0), (multiply, 1))


SCRATCH = [("keep", (NP,), bf16), ("gate", (NP,), bf16), ("rel", (NP,), bf16), ("last", (NP,), i32), ("deg", (NP,), fp32),
           ("agg", (NP + 1, F), fp32), ("att", (NP + 1, W3), fp32),
           ("x1", (NP, F), fp32), ("x2", (NP, F), fp32), ("x3", (NP, F), fp32),
           ("table", (NP, W3), fp32), ("a_dst", (NP, H), fp32), ("gat", (NP, F), fp32)]


def build(nc, D):
    with ExitStack() as ctx:
        r = Room(nc, ctx, "all")
        S = {"iota": r.sb("iota", [P, LO], fp16), "iota_p": r.sb("iota_p", [P, 1]), "ones": r.sb("ones", [P, LO]),
             "eps": r.sb("eps", [P, 1]), "ident": r.sb("ident", [P, P]), "before": r.sb("before", [P, P]),
             "hi": r.sb("hi", [P, NP // P]), "lo": r.sb("lo", [P, NP // P]),
             "head": r.sb("head", [P, H]), "head_first": r.sb("head_first", [P, H]),
             "res_w": r.sb("res_w", [P, F]),
             "res_stats": r.sb("res_stats", [P, 6 * NCH]), "gat_stats": r.sb("gat_stats", [P, 6 * NCH])}
        prepare(nc, D, S)
        edge_sum_rows(nc, D, S)
        node_mean(nc, D, S)
        edge_max(nc, D, S)
        node_mlp(nc, D, S)
        edge_relations(nc, D, S)
        node_relations(nc, D, S)
        edge_attention(nc, D, S)
        node_attention(nc, D, S)
        finish(nc, D, S)


_FLOATS = ["L0_gnn_W", "L0_gnn_b", "L1_gnn_W_edge", "L1_gnn_b_edge", "L1_gnn_W_mlp", "L1_gnn_b_mlp",
           "L2_gnn_basis_weights", "L2_gnn_coefficients", "L2_gnn_loop_weight",
           "L3_gnn_W", "L3_gnn_att_src", "L3_gnn_att_dst", "L3_gnn_bias", "L3_gnn_bn_gamma", "L3_gnn_bn_beta",
           "L3_gnn_ln_gamma", "L3_gnn_ln_beta", "L3_gnn_res_W", "L3_gnn_res_b", "L3_gnn_bnres_gamma", "L3_gnn_bnres_beta"]


def kernel(**inputs):
    import numpy as _np
    import concourse.bacc as _bacc
    from concourse.bass_utils import run_bass_kernel_spmd as _run

    def padded(a, fill=0, front=0):
        a = _np.asarray(a)
        out = _np.full((front + NP,) + a.shape[1:], fill, a.dtype)
        out[front:front + N] = a
        return out

    dst = padded(inputs["dst"], N, 1)
    dst[0] = -1
    arrays = {"x0": padded(inputs["x"]), "src": padded(inputs["src"]), "dst": dst,
              "edge_attr_64": padded(inputs["edge_attr_64"]), "edge_type_100": padded(inputs["edge_type_100"])}
    for name in _FLOATS:
        arrays[name] = _np.ascontiguousarray(inputs[name])
    nc = _bacc.Bacc("TRN2", target_bir_lowering=False, num_devices=1)
    D = {n: nc.dram_tensor(f"in_{n}", a.shape, mybir.dt.from_np(a.dtype), kind="ExternalInput").ap()
         for n, a in arrays.items()}
    D["x4"] = nc.dram_tensor("out_x4", (NP, F), fp32, kind="ExternalOutput").ap()
    for name, shape, dt in SCRATCH:
        D[name] = nc.dram_tensor(f"tmp_{name}", shape, dt, kind="Internal").ap()
    build(nc, D)
    r = _run(nc, [{f"in_{n}": a for n, a in arrays.items()}], core_ids=[0])
    return r.results[0]["out_x4"][:N]
```

```python
import concourse.bass as bass
from concourse import mybir
from contextlib import ExitStack

N = 50000
F = 128
P = 128
K = 4
CH = P * K
NCH = -(-N // CH)
NP = NCH * CH
LAST = N - (NCH - 1) * CH
LO = 512
HI = NP // LO
H = 4
HC = F // H
W3 = F + 2 * H
NREL = 100
NBASE = 4
EF = 64
SLOTS = 8
EPS = 1e-5
BIG = 1e38

fp32 = mybir.dt.float32
bf16 = mybir.dt.bfloat16
fp16 = mybir.dt.float16
i32 = mybir.dt.int32
ALU = mybir.AluOpType
ACT = mybir.ActivationFunctionType
AX = mybir.AxisListType


def run_chunks(eng, *stages):
    most = max(lag for _, lag in stages)
    head = 1 + -(-most // SLOTS)
    whole = NCH // SLOTS

    def steps(ts):
        for t in ts:
            for work, lag in stages:
                c = t - lag
                if 0 <= c < NCH:
                    work(c, c // SLOTS, c % SLOTS)

    steps(range(head * SLOTS))
    with eng.Fori(head, whole) as i:
        for v in range(SLOTS):
            for work, lag in stages:
                q = i + (v - lag) // SLOTS
                work(i * SLOTS + (v - lag), q, (v - lag) % SLOTS)
    steps(range(whole * SLOTS, NCH + most))


def reused(c, n):
    return not (isinstance(c, int) and c < n)


class Room:

    def __init__(self, nc, ctx, tag):
        self.nc, self.ctx, self.tag = nc, ctx, tag
        self.used = []

    def sb(self, name, shape, dt=fp32):
        return self.ctx.enter_context(self.nc.sbuf_tensor(f"{self.tag}_{name}", shape, dt))

    def ps(self, name, shape=(P, 512)):
        return self.ctx.enter_context(self.nc.psum_tensor(f"{self.tag}_ps_{name}", list(shape), fp32))

    def sem(self, name):
        self.used.append(self.nc.alloc_semaphore(f"{self.tag}_{name}"))
        return self.used[-1]

    def close(self):
        self.nc.clear_and_free_semaphores(self.used)
        self.nc.all_engine_barrier()

    def sems(self, name, n=SLOTS):
        return [self.sem(f"{name}{i}") for i in range(n)]


def rows(dram, c, n=CH):
    return dram[bass.ds(c * CH, CH), :].rearrange("(p k) f -> p (k f)", k=K)


def vec(dram, c):
    return dram[bass.ds(c * CH, CH)].rearrange("(p k) -> p k", k=K)


def spread(dram, c, parts):
    return dram[bass.ds(c * CH, CH)].unsqueeze(0).to_broadcast([parts, CH])


def gather(pool, ready, out, width, table, index):
    pool.nop(nofuse=True)
    for k in range(K):
        pool.indirect_dma_start(out[:, k * width:(k + 1) * width], None, table,
                                bass.IndirectOffsetOnAxis(ap=index[:, k:k + 1], axis=0)).then_inc(ready, 16)


def prepare(nc, D, S):
    with ExitStack() as ctx:
        r = Room(nc, ctx, "prep")
        cols = NP // P
        dst = r.sb("dst", [P, cols], i32)
        prev = r.sb("prev", [P, cols], i32)
        rel = r.sb("rel", [P, cols], i32)
        keep = r.sb("keep", [P, cols], bf16)
        gate = r.sb("gate", [P, cols], bf16)
        relb = r.sb("relb", [P, cols], bf16)
        hi = r.sb("hi", [P, cols], i32)
        lo = r.sb("lo", [P, cols], i32)
        neutral = r.sb("neutral", [1, 2 * W3])
        s_load = r.sem("load")
        s_rel = r.sem("rel")
        s_keep = r.sem("keep")
        s_digit = r.sem("digit")
        s_neutral = r.sem("neutral")
        s_store = r.sem("store")
        s_id = r.sem("id")
        ctx.callback(r.close)
        block = ctx.enter_context(nc.Block())

        @block.sync
        def _(sp):
            sp.dma_start(dst[:, :], D["dst"][1:NP + 1].rearrange("(p j) -> p j", p=P)).then_inc(s_load, 16)
            sp.dma_start(prev[:, :], D["dst"][0:NP].rearrange("(p j) -> p j", p=P)).then_inc(s_load, 16)
            sp.dma_start(rel[:, :], D["edge_type_100"].rearrange("(p j) -> p j", p=P)).then_inc(s_rel, 16)
            sp.wait_ge(s_keep, 1)
            sp.dma_start(D["keep"].rearrange("(p j) -> p j", p=P), keep[:, :]).then_inc(s_store, 16)
            sp.wait_ge(s_keep, 2)
            sp.dma_start(D["gate"].rearrange("(p j) -> p j", p=P), gate[:, :]).then_inc(s_store, 16)
            sp.wait_ge(s_keep, 3)
            sp.dma_start(D["rel"].rearrange("(p j) -> p j", p=P), relb[:, :]).then_inc(s_store, 16)
            sp.wait_ge(s_neutral, 2)
            sp.dma_start(D["agg"][NP:NP + 1, :], neutral[:, 0:F]).then_inc(s_store, 16)
            sp.dma_start(D["att"][NP:NP + 1, :], neutral[:, W3:2 * W3]).then_inc(s_store, 16)
            sp.wait_ge(s_store, 80)

        @block.vector
        def _(dve):
            dve.wait_ge(s_load, 32)
            dve.tensor_tensor(keep[:, :], dst[:, :], prev[:, :], ALU.is_equal).then_inc(s_keep, 1)
            dve.wait_ge(s_keep, 1)
            dve.tensor_scalar(gate[:, :], keep[:, :], -1.0, BIG, ALU.add, ALU.mult).then_inc(s_keep, 1)
            dve.wait_ge(s_rel, 16)
            dve.tensor_copy(relb[:, :], rel[:, :]).then_inc(s_keep, 1)
            dve.tensor_scalar(hi[:, :], dst[:, :], LO.bit_length() - 1, None, ALU.arith_shift_right).then_inc(s_digit, 1)
            dve.tensor_scalar(lo[:, :], dst[:, :], LO - 1, None, ALU.bitwise_and).then_inc(s_digit, 1)
            dve.wait_ge(s_digit, 2)
            dve.tensor_copy(S["hi"][:, :], hi[:, :]).then_inc(s_digit, 1)
            dve.tensor_copy(S["lo"][:, :], lo[:, :]).then_inc(s_digit, 1)
            dve.memset(neutral[:, :], 0.0).then_inc(s_neutral, 1)
            dve.wait_ge(s_neutral, 1)
            dve.memset(neutral[:, 2 * W3 - H:2 * W3], -BIG).then_inc(s_neutral, 1)

        @block.gpsimd
        def _(pool):
            pool.iota(S["iota"][:, :], pattern=[[1, LO]], base=0, channel_multiplier=0,
                      allow_small_or_imprecise_dtypes=True).then_inc(s_id, 1)
            pool.iota(S["iota_p"][:, :], pattern=[[0, 1]], base=0, channel_multiplier=1,
                      allow_small_or_imprecise_dtypes=True).then_inc(s_id, 1)
            pool.memset(S["ones"][:, :], 1.0).then_inc(s_id, 1)
            pool.memset(S["eps"][:, :], EPS).then_inc(s_id, 1)
            pool.memset(S["ident"][:, :], 0.0).then_inc(s_id, 1)
            pool.wait_ge(s_id, 5)
            pool.affine_select(out=S["ident"][:, :], in_=S["ident"][:, :], compare_op=ALU.not_equal, fill=1.0,
                               base=0, pattern=[[-1, P]], channel_multiplier=1).then_inc(s_id, 1)
            pool.affine_select(out=S["head"][:, :], in_=S["ones"][:, 0:H], compare_op=ALU.is_ge, fill=0.0,
                               base=0, pattern=[[-HC, H]], channel_multiplier=1).then_inc(s_id, 1)
            pool.affine_select(out=S["head_first"][:, :], in_=S["ones"][:, 0:H], compare_op=ALU.is_equal, fill=0.0,
                               base=0, pattern=[[-HC, H]], channel_multiplier=1).then_inc(s_id, 1)
            pool.wait_ge(s_id, 8)
            pool.affine_select(out=S["head"][:, :], in_=S["head"][:, :], compare_op=ALU.is_ge, fill=0.0,
                               base=HC - 1, pattern=[[HC, H]], channel_multiplier=-1).then_inc(s_id, 1)
            pool.affine_select(out=S["before"][:, :], in_=S["ones"][:, 0:P], compare_op=ALU.is_gt, fill=0.0,
                               base=0, pattern=[[1, P]], channel_multiplier=-1).then_inc(s_id, 1)


def edge_sum_rows(nc, D, S):
    with ExitStack() as ctx:
        r = Room(nc, ctx, "e0")
        idx = r.sb("idx", [P, SLOTS, K], i32)
        keep = r.sb("keep", [P, SLOTS, CH], bf16)
        src = r.sb("src", [P, SLOTS, CH])
        run = r.sb("run", [P, SLOTS, CH])
        out = r.sb("out", [P, SLOTS, CH])
        hot_hi = r.sb("hot_hi", [P, 2, K, HI], bf16)
        hot_lo = r.sb("hot_lo", [P, 2, K, LO], bf16)
        count = r.sb("count", [HI, LO])
        cum = r.sb("cum", [HI, LO])
        has = r.sb("has", [HI, LO])
        last = r.sb("last", [HI, LO])
        before_me = r.sb("before_me", [HI, 1])
        index = r.sb("index", [HI, LO], i32)
        deg = r.sb("deg", [HI, LO])
        ps_src = [r.ps(f"src{i}") for i in range(2)]
        ps_out = [r.ps(f"out{i}") for i in range(2)]
        ps_count = r.ps("count")
        ps_off = r.ps("off")
        s_idx = r.sems("idx")
        s_keep = r.sems("keep")
        s_src = r.sems("src")
        s_store = r.sems("store")
        s_turned = r.sem("turned")
        s_scan = r.sem("scan")
        s_back = r.sem("back")
        s_out = r.sem("out")
        s_hot = r.sem("hot")
        s_counted = r.sem("counted")
        s_cnt = r.sem("cnt")
        s_off = r.sem("off")
        s_deg = r.sem("deg")
        ctx.callback(r.close)
        block = ctx.enter_context(nc.Block())

        @block.sync
        def _(sp):
            def load_idx(c, q, u):
                if reused(c, SLOTS):
                    sp.wait_ge(s_src[u], 16 * K * q)
                sp.nop(nofuse=True)
                sp.dma_start(idx[:, u, :], vec(D["src"], c)).then_inc(s_idx[u], 16)

            def load_keep(c, q, u):
                if reused(c, SLOTS):
                    sp.wait_ge(s_scan, c - SLOTS + 1)
                sp.nop(nofuse=True)
                sp.dma_start(keep[:, u, :], spread(D["keep"], c, P)).then_inc(s_keep[u], 16)

            def store(c, q, u):
                sp.wait_ge(s_out, c + 1)
                sp.nop(nofuse=True)
                sp.dma_start(rows(D["agg"], c), out[:, u, :]).then_inc(s_store[u], 16)

            run_chunks(sp, (load_idx, 0), (load_keep, 1), (store, 5))
            for u in range(SLOTS):
                sp.wait_ge(s_store[u], 16 * len(range(u, NCH, SLOTS)))
            sp.wait_ge(s_deg, 2)
            sp.dma_start(D["last"].rearrange("(h l) -> h l", l=LO), index[:, :]).then_inc(s_idx[0], 16)
            sp.dma_start(D["deg"].rearrange("(h l) -> h l", l=LO), deg[:, :]).then_inc(s_idx[0], 16)
            sp.wait_ge(s_idx[0], 16 * (len(range(0, NCH, SLOTS)) + 2))

        @block.gpsimd
        def _(pool):
            def fetch(c, q, u):
                pool.wait_ge(s_idx[u], 16 * (q + 1))
                if reused(c, SLOTS):
                    pool.wait_ge(s_turned, c - SLOTS + 1)
                gather(pool, s_src[u], src[:, u, :], F, D["x0"], idx[:, u, :])

            run_chunks(pool, (fetch, 0))

        @block.tensor
        def _(pe):
            def turn(c, q, u):
                pe.wait_ge(s_src[u], 16 * K * (q + 1))
                if reused(c, 2):
                    pe.wait_ge(s_scan, c - 1)
                bank = ps_src[u % 2][:, :].rearrange("f (p k) -> f k p", k=K)
                for k in range(K):
                    ins = pe.transpose(bank[:, k, :], src[:, u, k * F:(k + 1) * F], S["ident"][:, :])
                ins.then_inc(s_turned, 1)

            def tally(c, q, u):
                pe.wait_ge(s_hot, c + 1)
                for k in range(K):
                    first = isinstance(c, int) and c == 0 and k == 0
                    final = isinstance(c, int) and c == NCH - 1 and k == K - 1
                    ins = pe.matmul(ps_count[0:HI, :], hot_hi[:, u % 2, k, :], hot_lo[:, u % 2, k, :],
                                    start=first, stop=final)
                ins.then_inc(s_counted, 1)

            def back(c, q, u):
                pe.wait_ge(s_scan, c + 1)
                if reused(c, 2):
                    pe.wait_ge(s_out, c - 1)
                cols = run[:, u, :].rearrange("f (p k) -> f k p", k=K)
                for k in range(K):
                    ins = pe.transpose(ps_out[u % 2][:, k * F:(k + 1) * F], cols[:, k, :], S["ident"][:, :])
                ins.then_inc(s_back, 1)

            run_chunks(pe, (turn, 0), (tally, 1), (back, 1))
            pe.wait_ge(s_cnt, 2)
            pe.matmul(ps_off[0:HI, 0:1], S["before"][0:HI, 0:HI], cum[:, LO - 1:LO], start=True, stop=True).then_inc(s_off, 1)

        @block.vector
        def _(dve):
            def hot(c, q, u):
                if reused(c, 2):
                    dve.wait_ge(s_counted, c - 1)
                for k in range(K):
                    j = c * K + k
                    dve.tensor_scalar(hot_hi[:, u % 2, k, :], S["iota"][:, 0:HI], S["hi"][:, bass.ds(j, 1)], None, ALU.is_equal)
                    ins = dve.tensor_scalar(hot_lo[:, u % 2, k, :], S["iota"][:, :], S["lo"][:, bass.ds(j, 1)], None, ALU.is_equal)
                ins.then_inc(s_hot, 1)

            def scan(c, q, u):
                dve.wait_ge(s_turned, c + 1)
                dve.wait_ge(s_keep[u], 16 * (q + 1))
                if reused(c, SLOTS):
                    dve.wait_ge(s_back, c - SLOTS + 1)
                carry = 0.0
                if reused(c, 1):
                    dve.wait_ge(s_scan, c)
                    carry = run[:, (u - 1) % SLOTS, CH - 1:CH]
                dve.tensor_tensor_scan(run[:, u, :], keep[:, u, :], ps_src[u % 2][:, :], carry, ALU.mult, ALU.add).then_inc(s_scan, 1)

            run_chunks(dve, (hot, 0), (scan, 0))
            dve.wait_ge(s_counted, NCH)
            dve.tensor_copy(count[:, :], ps_count[0:HI, :]).then_inc(s_cnt, 1)
            dve.wait_ge(s_cnt, 1)
            dve.tensor_tensor_scan(cum[:, :], S["ones"][0:HI, :], count[:, :], 0.0, ALU.mult, ALU.add).then_inc(s_cnt, 1)
            dve.tensor_scalar(deg[:, :], count[:, :], 1.0, None, ALU.max).then_inc(s_deg, 1)
            dve.tensor_scalar(has[:, :], count[:, :], 0.0, None, ALU.is_gt).then_inc(s_cnt, 1)
            dve.wait_ge(s_off, 1)
            dve.tensor_copy(before_me[:, :], ps_off[0:HI, 0:1]).then_inc(s_cnt, 1)
            dve.wait_ge(s_cnt, 4)
            dve.tensor_scalar(last[:, :], cum[:, :], before_me[:, 0:1], -1.0 - NP, ALU.add, ALU.add).then_inc(s_cnt, 1)
            dve.wait_ge(s_cnt, 5)
            dve.tensor_tensor(cum[:, :], last[:, :], has[:, :], ALU.mult).then_inc(s_cnt, 1)
            dve.wait_ge(s_cnt, 6)
            dve.tensor_scalar(index[:, :], cum[:, :], float(NP), None, ALU.add).then_inc(s_deg, 1)

        @block.scalar
        def _(act):
            def leave(c, q, u):
                act.wait_ge(s_back, c + 1)
                if reused(c, SLOTS):
                    act.wait_ge(s_store[u], 16 * q)
                act.activation(out[:, u, :], ps_out[u % 2][:, :], ACT.Copy).then_inc(s_out, 1)

            run_chunks(act, (leave, 0))


def row_stats(dve, x, stats):
    for k in range(K):
        ins = dve.bn_stats(stats[:, k * 6:(k + 1) * 6], x[:, k * F:(k + 1) * F])
    return ins


def row_moments(dve, stats, mv):
    dve.nop(nofuse=True)
    for k in range(K):
        ins = dve.bn_aggr(mv[:, k, :], stats[:, k * 6:(k + 1) * 6])
    return ins


def row_affine(act, out, x, scale, shift):
    for k in range(K):
        ins = act.activation(out[:, k * F:(k + 1) * F], x[:, k * F:(k + 1) * F], ACT.Identity,
                             bias=shift[:, k:k + 1], scale=scale[:, k:k + 1])
    return ins


def node_mean(nc, D, S):
    with ExitStack() as ctx:
        r = Room(nc, ctx, "n0")
        w = r.sb("w", [P, 2 * F])
        wt = r.sb("wt", [P, 2 * F])
        b = r.sb("b", [1, F])
        idx = r.sb("idx", [P, SLOTS, K], i32)
        deg = r.sb("deg", [P, SLOTS, K])
        agg = r.sb("agg", [P, SLOTS, CH])
        mean = r.sb("mean", [P, 2, CH])
        x = r.sb("x", [P, SLOTS, CH])
        xT = r.sb("xT", [P, 2, CH])
        mT = r.sb("mT", [P, 2, CH])
        junk = r.sb("junk", [P, CH])
        ss = r.sb("ss", [P, SLOTS, K])
        nrm = r.sb("nrm", [P, SLOTS, K])
        rn = r.sb("rn", [P, SLOTS, K])
        y = r.sb("y", [P, SLOTS, CH])
        stats = r.sb("stats", [P, SLOTS, K * 6])
        mv = r.sb("mv", [P, SLOTS, K, 2])
        sd = r.sb("sd", [P, SLOTS, K])
        rs = r.sb("rs", [P, SLOTS, K])
        shift = r.sb("shift", [P, SLOTS, K])
        out = r.sb("out", [P, SLOTS, CH])
        ps_rdeg = r.ps("rdeg")
        ps_x = [r.ps(f"x{i}") for i in range(2)]
        ps_m = [r.ps(f"m{i}") for i in range(2)]
        ps_o = [r.ps(f"o{i}") for i in range(2)]
        s_w = r.sem("w")
        s_wps = r.sem("wps")
        s_wt = r.sem("wt")
        s_idx = r.sems("idx")
        s_x = r.sems("x")
        s_deg = r.sems("deg")
        s_agg = r.sems("agg")
        s_store = r.sems("store")
        s_rd = r.sem("rd")
        s_mean = r.sem("mean")
        s_turned = r.sem("turned")
        s_T = r.sem("T")
        s_mm = r.sem("mm")
        s_sq = r.sem("sq")
        s_nrm = r.sem("nrm")
        s_rn = r.sem("rn")
        s_y = r.sem("y")
        s_st = r.sem("st")
        s_mv = r.sem("mv")
        s_sd = r.sem("sd")
        s_rs = r.sem("rs")
        s_shift = r.sem("shift")
        s_out = r.sem("out")
        ctx.callback(r.close)
        block = ctx.enter_context(nc.Block())

        @block.sync
        def _(sp):
            def load_idx(c, q, u):
                if reused(c, SLOTS):
                    sp.wait_ge(s_agg[u], 16 * K * q)
                sp.nop(nofuse=True)
                sp.dma_start(idx[:, u, :], vec(D["last"], c)).then_inc(s_idx[u], 16)

            def load_x(c, q, u):
                if reused(c, SLOTS):
                    sp.wait_ge(s_y, c - SLOTS + 1)
                sp.nop(nofuse=True)
                sp.dma_start(x[:, u, :], rows(D["x0"], c)).then_inc(s_x[u], 16)
                if reused(c, SLOTS):
                    sp.wait_ge(s_rd, c - SLOTS + 1)
                sp.nop(nofuse=True)
                sp.dma_start(deg[:, u, :], vec(D["deg"], c)).then_inc(s_deg[u], 16)

            def store(c, q, u):
                sp.wait_ge(s_out, c + 1)
                sp.nop(nofuse=True)
                sp.dma_start(rows(D["x1"], c), out[:, u, :]).then_inc(s_store[u], 16)

            run_chunks(sp, (load_idx, 0), (load_x, 0), (store, 9))
            for u in range(SLOTS):
                sp.wait_ge(s_store[u], 16 * len(range(u, NCH, SLOTS)))

        @block.gpsimd
        def _(pool):
            def fetch(c, q, u):
                pool.wait_ge(s_idx[u], 16 * (q + 1))
                if reused(c, SLOTS):
                    pool.wait_ge(s_mean, c - SLOTS + 1)
                gather(pool, s_agg[u], agg[:, u, :], F, D["agg"], idx[:, u, :])

            run_chunks(pool, (fetch, 0))

        @block.tensor
        def _(pe):
            pe.wait_ge(s_w, 32)
            for h in range(2):
                ins = pe.transpose(ps_x[0][:, h * F:(h + 1) * F], w[:, h * F:(h + 1) * F], S["ident"][:, :])
            ins.then_inc(s_wps, 1)

            def turn(c, q, u):
                if not reused(c, 1):
                    pe.wait_ge(s_wt, 1)
                pe.wait_ge(s_x[u], 16 * (q + 1))
                if reused(c, 2):
                    pe.wait_ge(s_T, c - 1)
                for k in range(K):
                    pe.transpose(ps_x[u % 2][:, k * P:(k + 1) * P], x[:, u, k * F:(k + 1) * F], S["ident"][:, :])
                pe.wait_ge(s_mean, c + 1)
                for k in range(K):
                    ins = pe.transpose(ps_m[u % 2][:, k * P:(k + 1) * P], mean[:, u % 2, k * F:(k + 1) * F], S["ident"][:, :])
                ins.then_inc(s_turned, 1)

            def multiply(c, q, u):
                pe.wait_ge(s_T, c + 1)
                if reused(c, 2):
                    pe.wait_ge(s_y, c - 1)
                for k in range(K):
                    o = ps_o[u % 2][:, k * F:(k + 1) * F]
                    pe.matmul(o, xT[:, u % 2, k * P:(k + 1) * P], wt[:, 0:F], start=True, stop=False)
                    pe.matmul(o, mT[:, u % 2, k * P:(k + 1) * P], wt[:, F:2 * F], start=False, stop=False)
                    ins = pe.matmul(o, S["ones"][0:1, 0:P], b[0:1, :], start=False, stop=True)
                ins.then_inc(s_mm, 1)

            run_chunks(pe, (turn, 0), (multiply, 1))

        @block.scalar
        def _(act):
            act.dma_start(w[:, :], D["L0_gnn_W"]).then_inc(s_w, 16)
            act.dma_start(b[:, :], D["L0_gnn_b"].unsqueeze(0)).then_inc(s_w, 16)

            act.wait_ge(s_wps, 1)
            act.activation(wt[:, :], ps_x[0][:, 0:2 * F], ACT.Copy).then_inc(s_wt, 1)

            def copy(c, q, u):
                act.wait_ge(s_turned, c + 1)
                if reused(c, 2):
                    act.wait_ge(s_mm, c - 1)
                act.activation(xT[:, u % 2, :], ps_x[u % 2][:, :], ACT.Copy)
                act.activation(mT[:, u % 2, :], ps_m[u % 2][:, :], ACT.Copy).then_inc(s_T, 1)

            def squares(c, q, u):
                act.wait_ge(s_mm, c + 1)
                for k in range(K):
                    ins = act.activation(junk[:, k * F:(k + 1) * F], ps_o[u % 2][:, k * F:(k + 1) * F], ACT.Square,
                                         accum_out=ss[:, u, k:k + 1])
                ins.then_inc(s_sq, 1)
                act.wait_ge(s_sq, c + 1)
                act.activation(nrm[:, u, :], ss[:, u, :], ACT.Sqrt).then_inc(s_nrm, 1)

            def deviation(c, q, u):
                act.wait_ge(s_mv, c + 1)
                act.activation(sd[:, u, :], mv[:, u, :, 1], ACT.Sqrt, bias=S["eps"][:, 0:1]).then_inc(s_sd, 1)

            def normalise(c, q, u):
                act.wait_ge(s_shift, c + 1)
                if reused(c, SLOTS):
                    act.wait_ge(s_store[u], 16 * q)
                row_affine(act, out[:, u, :], y[:, u, :], rs[:, u, :], shift[:, u, :]).then_inc(s_out, 1)

            run_chunks(act, (deviation, 4), (copy, 0), (squares, 1), (normalise, 5))

        @block.vector
        def _(dve):
            def invert(c, q, u):
                dve.wait_ge(s_deg[u], 16 * (q + 1))
                if reused(c, SLOTS):
                    dve.wait_ge(s_mean, c - SLOTS + 1)
                dve.reciprocal(ps_rdeg[:, u * K:(u + 1) * K], deg[:, u, :]).then_inc(s_rd, 1)

            def clamp(c, q, u):
                dve.wait_ge(s_nrm, c + 1)
                dve.tensor_scalar(nrm[:, u, :], nrm[:, u, :], 1e-12, None, ALU.max).then_inc(s_rn, 1)

            def scale(c, q, u):
                dve.wait_ge(s_rd, c + 1)
                dve.wait_ge(s_agg[u], 16 * K * (q + 1))
                if reused(c, 2):
                    dve.wait_ge(s_turned, c - 1)
                dve.tensor_tensor(mean[:, u % 2, :].rearrange("p (k f) -> p k f", k=K),
                                  agg[:, u, :].rearrange("p (k f) -> p k f", k=K),
                                  ps_rdeg[:, u * K:(u + 1) * K].unsqueeze(2).to_broadcast([P, K, F]),
                                  ALU.mult).then_inc(s_mean, 1)

            def norm_inverse(c, q, u):
                dve.wait_ge(s_rn, 2 * c + 1)
                dve.reciprocal(rn[:, u, :], nrm[:, u, :]).then_inc(s_rn, 1)

            def inverse(c, q, u):
                dve.wait_ge(s_sd, c + 1)
                dve.reciprocal(rs[:, u, :], sd[:, u, :]).then_inc(s_rs, 1)

            def residual(c, q, u):
                dve.wait_ge(s_rn, 2 * c + 2)
                if reused(c, SLOTS):
                    dve.wait_ge(s_out, c - SLOTS + 1)
                for k in range(K):
                    f = slice(k * F, (k + 1) * F)
                    ins = dve.scalar_tensor_tensor(y[:, u, f], ps_o[u % 2][:, f], rn[:, u, k:k + 1], x[:, u, f], ALU.mult, ALU.add)
                ins.then_inc(s_y, 1)

            def shifts(c, q, u):
                dve.wait_ge(s_rs, c + 1)
                dve.scalar_tensor_tensor(shift[:, u, :], mv[:, u, :, 0], -1.0, rs[:, u, :], ALU.mult, ALU.mult).then_inc(s_shift, 1)

            def statistics(c, q, u):
                dve.wait_ge(s_y, c + 1)
                row_stats(dve, y[:, u, :], stats[:, u, :]).then_inc(s_st, 1)

            def moments(c, q, u):
                dve.wait_ge(s_st, c + 1)
                row_moments(dve, stats[:, u, :], mv[:, u, :, :]).then_inc(s_mv, 1)

            run_chunks(dve, (invert, 0), (inverse, 5), (scale, 0), (shifts, 5), (clamp, 2), (statistics, 3),
                       (norm_inverse, 2), (moments, 3), (residual, 2))


def edge_max(nc, D, S):
    with ExitStack() as ctx:
        r = Room(nc, ctx, "e1")
        wd = r.sb("wd", [P, F])
        we = r.sb("we", [EF, F])
        b = r.sb("b", [P, 1])
        coef = r.sb("coef", [NREL, NBASE])
        rel = r.sb("rel", [NREL, SLOTS, CH], bf16)
        hot = r.sb("hot", [NREL, 2, CH])
        edge_coef = r.sb("edge_coef", [P, SLOTS, K * NBASE])
        idx = r.sb("idx", [P, SLOTS, 2 * K], i32)
        gate = r.sb("gate", [P, SLOTS, CH], bf16)
        feat = r.sb("feat", [P, SLOTS, K * EF])
        src = r.sb("src", [P, SLOTS, CH])
        dst = r.sb("dst", [P, SLOTS, CH])
        diff = r.sb("diff", [P, 2, CH])
        dT = r.sb("dT", [P, SLOTS, CH])
        fT = r.sb("fT", [EF, 2, CH])
        hid = r.sb("hid", [P, 2, CH])
        ef = r.sb("ef", [P, 2, CH])
        run = r.sb("run", [P, SLOTS, CH])
        out = r.sb("out", [P, SLOTS, CH])
        ps_d = [r.ps(f"d{i}") for i in range(2)]
        ps_f = [r.ps(f"f{i}") for i in range(2)]
        ps_h = [r.ps(f"h{i}") for i in range(2)]
        ps_o = r.ps("o")
        ps_c = r.ps("c")
        s_w = r.sem("w")
        s_idx = r.sems("idx")
        s_gate = r.sems("gate")
        s_feat = r.sems("feat")
        s_rows = r.sems("rows")
        s_store = r.sems("store")
        s_rel = r.sems("rel")
        s_coef_store = r.sems("coef_store")
        s_hot = r.sem("hot")
        s_coef = r.sem("coef")
        s_coef_out = r.sem("coef_out")
        s_diff = r.sem("diff")
        s_turned = r.sem("turned")
        s_T = r.sem("T")
        s_mm = r.sem("mm")
        s_hid = r.sem("hid")
        s_ef = r.sem("ef")
        s_scan = r.sem("scan")
        s_back = r.sem("back")
        s_out = r.sem("out")
        ctx.callback(r.close)
        block = ctx.enter_context(nc.Block())

        @block.sync
        def _(sp):
            def load_idx(c, q, u):
                if reused(c, SLOTS):
                    sp.wait_ge(s_rows[u], 16 * 2 * K * q)
                sp.nop(nofuse=True)
                sp.dma_start(idx[:, u, 0:K], vec(D["src"], c)).then_inc(s_idx[u], 16)
                sp.dma_start(idx[:, u, K:2 * K], vec(D["dst"][1:NP + 1], c)).then_inc(s_idx[u], 16)

            def load_rest(c, q, u):
                if reused(c, SLOTS):
                    sp.wait_ge(s_turned, c - SLOTS + 1)
                sp.nop(nofuse=True)
                sp.dma_start(feat[:, u, :], rows(D["edge_attr_64"], c)).then_inc(s_feat[u], 16)
                if reused(c, SLOTS):
                    sp.wait_ge(s_scan, c - SLOTS + 1)
                sp.nop(nofuse=True)
                sp.dma_start(gate[:, u, :], spread(D["gate"], c, P)).then_inc(s_gate[u], 16)
                if reused(c, SLOTS):
                    sp.wait_ge(s_hot, c - SLOTS + 1)
                sp.nop(nofuse=True)
                sp.dma_start(rel[:, u, :], spread(D["rel"], c, NREL)).then_inc(s_rel[u], 16)

            def store(c, q, u):
                sp.wait_ge(s_out, c + 1)
                sp.nop(nofuse=True)
                sp.dma_start(rows(D["agg"], c), out[:, u, :]).then_inc(s_store[u], 16)

            def store_coef(c, q, u):
                sp.wait_ge(s_coef_out, c + 1)
                sp.nop(nofuse=True)
                sp.dma_start(rows(D["edge_coef"], c), edge_coef[:, u, :]).then_inc(s_coef_store[u], 16)

            run_chunks(sp, (load_idx, 0), (load_rest, 1), (store_coef, 4), (store, 5))
            for u in range(SLOTS):
                sp.wait_ge(s_store[u], 16 * len(range(u, NCH, SLOTS)))
                sp.wait_ge(s_coef_store[u], 16 * len(range(u, NCH, SLOTS)))

        @block.gpsimd
        def _(pool):
            def fetch(c, q, u):
                pool.wait_ge(s_idx[u], 32 * (q + 1))
                if reused(c, SLOTS):
                    pool.wait_ge(s_diff, c - SLOTS + 1)
                gather(pool, s_rows[u], src[:, u, :], F, D["x1"], idx[:, u, 0:K])
                gather(pool, s_rows[u], dst[:, u, :], F, D["x1"], idx[:, u, K:2 * K])

            run_chunks(pool, (fetch, 0))

        @block.vector
        def _(dve):
            def differ(c, q, u):
                dve.wait_ge(s_rows[u], 16 * 2 * K * (q + 1))
                if reused(c, 2):
                    dve.wait_ge(s_turned, c - 1)
                dve.tensor_tensor(diff[:, u % 2, :], dst[:, u, :], src[:, u, :], ALU.subtract).then_inc(s_diff, 1)

            def scan(c, q, u):
                dve.wait_ge(s_hid, c + 1)
                dve.tensor_tensor(ef[:, u % 2, :], dT[:, u, :], hid[:, u % 2, :], ALU.add).then_inc(s_ef, 1)
                dve.wait_ge(s_ef, c + 1)
                dve.wait_ge(s_gate[u], 16 * (q + 1))
                if reused(c, SLOTS):
                    dve.wait_ge(s_back, c - SLOTS + 1)
                carry = 0.0
                if reused(c, 1):
                    dve.wait_ge(s_scan, c)
                    carry = run[:, (u - 1) % SLOTS, CH - 1:CH]
                dve.tensor_tensor_scan(run[:, u, :], gate[:, u, :], ef[:, u % 2, :], carry, ALU.add, ALU.max).then_inc(s_scan, 1)

            def types(c, q, u):
                dve.wait_ge(s_rel[u], 16 * (q + 1))
                if reused(c, 2):
                    dve.wait_ge(s_coef, c - 1)
                dve.tensor_scalar(hot[:, u % 2, :], rel[:, u, :], S["iota_p"][0:NREL, 0:1], None, ALU.is_equal).then_inc(s_hot, 1)

            run_chunks(dve, (differ, 0), (scan, 1), (types, 1))

        @block.tensor
        def _(pe):
            pe.wait_ge(s_w, 64)

            def turn(c, q, u):
                pe.wait_ge(s_feat[u], 16 * (q + 1))
                pe.wait_ge(s_diff, c + 1)
                if reused(c, 2):
                    pe.wait_ge(s_T, c - 1)
                bank = ps_d[u % 2][:, :].rearrange("f (p k) -> f k p", k=K)
                for k in range(K):
                    pe.transpose(bank[:, k, :], diff[:, u % 2, k * F:(k + 1) * F], S["ident"][:, :])
                bank = ps_f[u % 2][0:EF, :].rearrange("f (p k) -> f k p", k=K)
                for k in range(K):
                    ins = pe.transpose(bank[:, k, :], feat[:, u, k * EF:(k + 1) * EF], S["ident"][:, :])
                ins.then_inc(s_turned, 1)

            def multiply(c, q, u):
                pe.wait_ge(s_T, c + 1)
                if reused(c, 2):
                    pe.wait_ge(s_hid, c - 1)
                pe.matmul(ps_h[u % 2][:, :], wd[:, :], dT[:, u, :], start=True, stop=False)
                pe.matmul(ps_h[u % 2][:, :], we[:, :], fT[:, u % 2, :], start=False, stop=True).then_inc(s_mm, 1)

            def back(c, q, u):
                pe.wait_ge(s_scan, c + 1)
                if reused(c, 1):
                    pe.wait_ge(s_out, c)
                cols = run[:, u, :].rearrange("f (p k) -> f k p", k=K)
                for k in range(K):
                    ins = pe.transpose(ps_o[:, k * F:(k + 1) * F], cols[:, k, :], S["ident"][:, :])
                ins.then_inc(s_back, 1)

            def coefficients(c, q, u):
                pe.wait_ge(s_hot, c + 1)
                if reused(c, 1):
                    pe.wait_ge(s_coef_out, c)
                cols = hot[:, u % 2, :].rearrange("t (p k) -> t k p", k=K)
                for k in range(K):
                    ins = pe.matmul(ps_c[:, k * NBASE:(k + 1) * NBASE], cols[:, k, :], coef[:, :], start=True, stop=True)
                ins.then_inc(s_coef, 1)

            run_chunks(pe, (turn, 0), (multiply, 1), (back, 2), (coefficients, 2))

        @block.scalar
        def _(act):
            act.dma_start(wd[:, :], D["L1_gnn_W_edge"][0:F, :]).then_inc(s_w, 16)
            act.dma_start(we[:, :], D["L1_gnn_W_edge"][F:F + EF, :]).then_inc(s_w, 16)
            act.dma_start(b[:, :], D["L1_gnn_b_edge"].unsqueeze(1)).then_inc(s_w, 16)
            act.dma_start(coef[:, :], D["L2_gnn_coefficients"]).then_inc(s_w, 16)

            act.wait_ge(s_w, 64)

            def copy(c, q, u):
                act.wait_ge(s_turned, c + 1)
                if reused(c, SLOTS):
                    act.wait_ge(s_ef, c - SLOTS + 1)
                if reused(c, 2):
                    act.wait_ge(s_mm, c - 1)
                act.activation(fT[:, u % 2, :], ps_f[u % 2][0:EF, :], ACT.Copy)
                act.activation(dT[:, u, :], ps_d[u % 2][:, :], ACT.Copy).then_inc(s_T, 1)

            def hidden(c, q, u):
                act.wait_ge(s_mm, c + 1)
                if reused(c, 2):
                    act.wait_ge(s_ef, c - 1)
                act.activation(hid[:, u % 2, :], ps_h[u % 2][:, :], ACT.Relu, bias=b[:, 0:1]).then_inc(s_hid, 1)

            def leave(c, q, u):
                act.wait_ge(s_back, c + 1)
                if reused(c, SLOTS):
                    act.wait_ge(s_store[u], 16 * q)
                act.activation(out[:, u, :], ps_o[:, :], ACT.Copy).then_inc(s_out, 1)

            def leave_coef(c, q, u):
                act.wait_ge(s_coef, c + 1)
                if reused(c, SLOTS):
                    act.wait_ge(s_coef_store[u], 16 * q)
                act.activation(edge_coef[:, u, :], ps_c[:, 0:K * NBASE], ACT.Copy).then_inc(s_coef_out, 1)

            run_chunks(act, (copy, 0), (hidden, 1), (leave, 2), (leave_coef, 2))


def node_mlp(nc, D, S):
    with ExitStack() as ctx:
        r = Room(nc, ctx, "n1")
        w = r.sb("w", [P, 2 * F])
        b = r.sb("b", [1, F])
        idx = r.sb("idx", [P, SLOTS, K], i32)
        agg = r.sb("agg", [P, SLOTS, CH])
        x = r.sb("x", [P, SLOTS, CH])
        xT = r.sb("xT", [P, 2, CH])
        mT = r.sb("mT", [P, 2, CH])
        hid = r.sb("hid", [P, 2, CH])
        y = r.sb("y", [P, SLOTS, CH])
        stats = r.sb("stats", [P, SLOTS, K * 6])
        mv = r.sb("mv", [P, SLOTS, K, 2])
        sd = r.sb("sd", [P, SLOTS, K])
        rs = r.sb("rs", [P, SLOTS, K])
        out = r.sb("out", [P, SLOTS, CH])
        ps_x = [r.ps(f"x{i}") for i in range(2)]
        ps_m = [r.ps(f"m{i}") for i in range(2)]
        ps_o = [r.ps(f"o{i}") for i in range(2)]
        s_w = r.sem("w")
        s_idx = r.sems("idx")
        s_x = r.sems("x")
        s_agg = r.sems("agg")
        s_store = r.sems("store")
        s_turned = r.sem("turned")
        s_T = r.sem("T")
        s_mm = r.sem("mm")
        s_hid = r.sem("hid")
        s_y = r.sem("y")
        s_st = r.sem("st")
        s_mv = r.sem("mv")
        s_sd = r.sem("sd")
        s_rs = r.sem("rs")
        s_out = r.sem("out")
        ctx.callback(r.close)
        block = ctx.enter_context(nc.Block())

        @block.sync
        def _(sp):
            def load_idx(c, q, u):
                if reused(c, SLOTS):
                    sp.wait_ge(s_agg[u], 16 * K * q)
                sp.nop(nofuse=True)
                sp.dma_start(idx[:, u, :], vec(D["last"], c)).then_inc(s_idx[u], 16)

            def load_x(c, q, u):
                if reused(c, SLOTS):
                    sp.wait_ge(s_y, c - SLOTS + 1)
                sp.nop(nofuse=True)
                sp.dma_start(x[:, u, :], rows(D["x1"], c)).then_inc(s_x[u], 16)

            def store(c, q, u):
                sp.wait_ge(s_out, c + 1)
                sp.nop(nofuse=True)
                sp.dma_start(rows(D["x2"], c), out[:, u, :]).then_inc(s_store[u], 16)

            run_chunks(sp, (load_idx, 0), (load_x, 0), (store, 7))
            for u in range(SLOTS):
                sp.wait_ge(s_store[u], 16 * len(range(u, NCH, SLOTS)))

        @block.gpsimd
        def _(pool):
            def fetch(c, q, u):
                pool.wait_ge(s_idx[u], 16 * (q + 1))
                if reused(c, SLOTS):
                    pool.wait_ge(s_turned, c - SLOTS + 1)
                gather(pool, s_agg[u], agg[:, u, :], F, D["agg"], idx[:, u, :])

            run_chunks(pool, (fetch, 0))

        @block.tensor
        def _(pe):
            pe.wait_ge(s_w, 48)

            def turn(c, q, u):
                pe.wait_ge(s_x[u], 16 * (q + 1))
                if reused(c, 2):
                    pe.wait_ge(s_T, c - 1)
                for k in range(K):
                    pe.transpose(ps_x[u % 2][:, k * P:(k + 1) * P], x[:, u, k * F:(k + 1) * F], S["ident"][:, :])
                pe.wait_ge(s_agg[u], 16 * K * (q + 1))
                for k in range(K):
                    ins = pe.transpose(ps_m[u % 2][:, k * P:(k + 1) * P], agg[:, u, k * F:(k + 1) * F], S["ident"][:, :])
                ins.then_inc(s_turned, 1)

            def multiply(c, q, u):
                pe.wait_ge(s_T, c + 1)
                if reused(c, 2):
                    pe.wait_ge(s_hid, c - 1)
                for k in range(K):
                    o = ps_o[u % 2][:, k * F:(k + 1) * F]
                    pe.matmul(o, xT[:, u % 2, k * P:(k + 1) * P], w[:, 0:F], start=True, stop=False)
                    pe.matmul(o, mT[:, u % 2, k * P:(k + 1) * P], w[:, F:2 * F], start=False, stop=False)
                    ins = pe.matmul(o, S["ones"][0:1, 0:P], b[0:1, :], start=False, stop=True)
                ins.then_inc(s_mm, 1)

            run_chunks(pe, (turn, 0), (multiply, 1))

        @block.scalar
        def _(act):
            for h in range(2):
                act.dma_start(w[:, h * F:(h + 1) * F], D["L1_gnn_W_mlp"][h * F:(h + 1) * F, :]).then_inc(s_w, 16)
            act.dma_start(b[:, :], D["L1_gnn_b_mlp"].unsqueeze(0)).then_inc(s_w, 16)

            def copy(c, q, u):
                act.wait_ge(s_turned, c + 1)
                if reused(c, 2):
                    act.wait_ge(s_mm, c - 1)
                act.activation(xT[:, u % 2, :], ps_x[u % 2][:, :], ACT.Copy)
                act.activation(mT[:, u % 2, :], ps_m[u % 2][:, :], ACT.Copy).then_inc(s_T, 1)

            def hidden(c, q, u):
                act.wait_ge(s_mm, c + 1)
                if reused(c, 2):
                    act.wait_ge(s_y, c - 1)
                act.activation(hid[:, u % 2, :], ps_o[u % 2][:, :], ACT.Relu).then_inc(s_hid, 1)

            def deviation(c, q, u):
                act.wait_ge(s_mv, c + 1)
                act.activation(sd[:, u, :], mv[:, u, :, 1], ACT.Sqrt, bias=S["eps"][:, 0:1]).then_inc(s_sd, 1)

            run_chunks(act, (deviation, 3), (copy, 0), (hidden, 1))

        @block.vector
        def _(dve):
            def residual(c, q, u):
                dve.wait_ge(s_hid, c + 1)
                dve.wait_ge(s_x[u], 16 * (q + 1))
                dve.scalar_tensor_tensor(y[:, u, :], x[:, u, :], 2.0, hid[:, u % 2, :], ALU.mult, ALU.add).then_inc(s_y, 1)

            def statistics(c, q, u):
                dve.wait_ge(s_y, c + 1)
                row_stats(dve, y[:, u, :], stats[:, u, :]).then_inc(s_st, 1)

            def moments(c, q, u):
                dve.wait_ge(s_st, c + 1)
                row_moments(dve, stats[:, u, :], mv[:, u, :, :]).then_inc(s_mv, 1)

            def inverse(c, q, u):
                dve.wait_ge(s_sd, c + 1)
                dve.reciprocal(rs[:, u, :], sd[:, u, :]).then_inc(s_rs, 1)

            def normalise(c, q, u):
                dve.wait_ge(s_rs, c + 1)
                if reused(c, SLOTS):
                    dve.wait_ge(s_store[u], 16 * q)
                for k in range(K):
                    f = slice(k * F, (k + 1) * F)
                    ins = dve.tensor_scalar(out[:, u, f], y[:, u, f], mv[:, u, k, 0:1], rs[:, u, k:k + 1], ALU.subtract, ALU.mult)
                ins.then_inc(s_out, 1)

            run_chunks(dve, (residual, 2), (inverse, 3), (statistics, 2), (normalise, 3), (moments, 2))


def edge_relations(nc, D, S):
    with ExitStack() as ctx:
        r = Room(nc, ctx, "e2")
        basis = r.sb("basis", [P, NBASE * F])
        idx = r.sb("idx", [P, SLOTS, K], i32)
        keep = r.sb("keep", [P, SLOTS, CH], bf16)
        coef = r.sb("coef", [P, SLOTS, K * NBASE])
        src = r.sb("src", [P, SLOTS, CH])
        xT = r.sb("xT", [P, 2, CH])
        part = r.sb("part", [P, NBASE - 1, CH])
        msg = r.sb("msg", [P, 2, CH])
        run = r.sb("run", [P, SLOTS, CH])
        out = r.sb("out", [P, SLOTS, CH])
        ps_x = r.ps("x")
        ps_y = [r.ps(f"y{k}") for k in range(K)]
        ps_m = [r.ps(f"m{i}") for i in range(2)]
        ps_o = r.ps("o")
        s_w = r.sem("w")
        s_idx = r.sems("idx")
        s_keep = r.sems("keep")
        s_coef = r.sems("coef")
        s_src = r.sems("src")
        s_store = r.sems("store")
        s_turned = r.sem("turned")
        s_T = r.sem("T")
        s_mm = r.sem("mm")
        s_first = r.sem("first")
        s_part = r.sem("part")
        s_msg = r.sem("msg")
        s_mT = r.sem("mT")
        s_scan = r.sem("scan")
        s_back = r.sem("back")
        s_out = r.sem("out")
        ctx.callback(r.close)
        block = ctx.enter_context(nc.Block())

        @block.sync
        def _(sp):
            def load_idx(c, q, u):
                if reused(c, SLOTS):
                    sp.wait_ge(s_src[u], 16 * K * q)
                sp.nop(nofuse=True)
                sp.dma_start(idx[:, u, :], vec(D["src"], c)).then_inc(s_idx[u], 16)

            def load_rest(c, q, u):
                if reused(c, SLOTS):
                    sp.wait_ge(s_msg, K * (c - SLOTS + 1))
                sp.nop(nofuse=True)
                sp.dma_start(coef[:, u, :], rows(D["edge_coef"], c)).then_inc(s_coef[u], 16)
                if reused(c, SLOTS):
                    sp.wait_ge(s_scan, c - SLOTS + 1)
                sp.nop(nofuse=True)
                sp.dma_start(keep[:, u, :], spread(D["keep"], c, P)).then_inc(s_keep[u], 16)

            def store(c, q, u):
                sp.wait_ge(s_out, c + 1)
                sp.nop(nofuse=True)
                sp.dma_start(rows(D["agg"], c), out[:, u, :]).then_inc(s_store[u], 16)

            run_chunks(sp, (load_idx, 0), (load_rest, 1), (store, 7))
            for u in range(SLOTS):
                sp.wait_ge(s_store[u], 16 * len(range(u, NCH, SLOTS)))

        @block.gpsimd
        def _(pool):
            def fetch(c, q, u):
                pool.wait_ge(s_idx[u], 16 * (q + 1))
                if reused(c, SLOTS):
                    pool.wait_ge(s_turned, c - SLOTS + 1)
                gather(pool, s_src[u], src[:, u, :], F, D["x2"], idx[:, u, :])

            run_chunks(pool, (fetch, 0))

        @block.tensor
        def _(pe):
            pe.wait_ge(s_w, 16 * NBASE)

            def turn(c, q, u):
                pe.wait_ge(s_src[u], 16 * K * (q + 1))
                if reused(c, 1):
                    pe.wait_ge(s_T, c)
                for k in range(K):
                    ins = pe.transpose(ps_x[:, k * P:(k + 1) * P], src[:, u, k * F:(k + 1) * F], S["ident"][:, :])
                ins.then_inc(s_turned, 1)

            def multiply(c, q, u):
                pe.wait_ge(s_T, c + 1)
                for k in range(K):
                    if reused(c, 1):
                        pe.wait_ge(s_msg, K * (c - 1) + k + 1)
                    pe.matmul(ps_y[k][:, :], xT[:, u % 2, k * P:(k + 1) * P], basis[:, :], start=True, stop=True).then_inc(s_mm, 1)

            def turn_message(c, q, u):
                pe.wait_ge(s_msg, K * (c + 1))
                if reused(c, 2):
                    pe.wait_ge(s_scan, c - 1)
                bank = ps_m[u % 2][:, :].rearrange("f (p k) -> f k p", k=K)
                for k in range(K):
                    ins = pe.transpose(bank[:, k, :], msg[:, u % 2, k * F:(k + 1) * F], S["ident"][:, :])
                ins.then_inc(s_mT, 1)

            def back(c, q, u):
                pe.wait_ge(s_scan, c + 1)
                if reused(c, 1):
                    pe.wait_ge(s_out, c)
                cols = run[:, u, :].rearrange("f (p k) -> f k p", k=K)
                for k in range(K):
                    ins = pe.transpose(ps_o[:, k * F:(k + 1) * F], cols[:, k, :], S["ident"][:, :])
                ins.then_inc(s_back, 1)

            run_chunks(pe, (turn, 0), (multiply, 1), (turn_message, 2), (back, 4))

        @block.scalar
        def _(act):
            for b in range(NBASE):
                act.dma_start(basis[:, b * F:(b + 1) * F], D["L2_gnn_basis_weights"][b, :, :]).then_inc(s_w, 16)

            def copy(c, q, u):
                act.wait_ge(s_turned, c + 1)
                if reused(c, 2):
                    act.wait_ge(s_mm, K * (c - 1))
                act.activation(xT[:, u % 2, :], ps_x[:, :], ACT.Copy).then_inc(s_T, 1)

            def first(c, q, u):
                act.wait_ge(s_coef[u], 16 * (q + 1))
                for k in range(K):
                    act.wait_ge(s_mm, K * c + k + 1)
                    if reused(c, 1):
                        act.wait_ge(s_part, 2 * K * (c - 1) + 2 * (k // 2) * 2 + k % 2 + 1)
                    act.activation(part[:, 0, k * F:(k + 1) * F], ps_y[k][:, 0:F], ACT.Copy,
                                   scale=coef[:, u, k * NBASE:k * NBASE + 1]).then_inc(s_first, 1)

            def leave(c, q, u):
                act.wait_ge(s_back, c + 1)
                if reused(c, SLOTS):
                    act.wait_ge(s_store[u], 16 * q)
                act.activation(out[:, u, :], ps_o[:, :], ACT.Copy).then_inc(s_out, 1)

            run_chunks(act, (copy, 0), (first, 1), (leave, 4))

        @block.vector
        def _(dve):
            def combine(c, q, u):
                for pair in range(K // 2):
                    for b in range(1, NBASE):
                        for k in (2 * pair, 2 * pair + 1):
                            if b == 1:
                                dve.wait_ge(s_first, K * c + k + 1)
                            else:
                                dve.wait_ge(s_part, 2 * K * c + 4 * pair + 2 * (b - 2) + k % 2 + 1)
                            if b == NBASE - 1 and k == 0 and reused(c, 2):
                                dve.wait_ge(s_mT, c - 1)
                            f = slice(k * F, (k + 1) * F)
                            into = msg[:, u % 2, f] if b == NBASE - 1 else part[:, b, f]
                            ins = dve.scalar_tensor_tensor(into, ps_y[k][:, b * F:(b + 1) * F],
                                                           coef[:, u, k * NBASE + b:k * NBASE + b + 1],
                                                           part[:, b - 1, f], ALU.mult, ALU.add)
                            ins.then_inc(s_msg if b == NBASE - 1 else s_part, 1)

            def scan(c, q, u):
                dve.wait_ge(s_mT, c + 1)
                dve.wait_ge(s_keep[u], 16 * (q + 1))
                if reused(c, SLOTS):
                    dve.wait_ge(s_back, c - SLOTS + 1)
                carry = 0.0
                if reused(c, 1):
                    dve.wait_ge(s_scan, c)
                    carry = run[:, (u - 1) % SLOTS, CH - 1:CH]
                dve.tensor_tensor_scan(run[:, u, :], keep[:, u, :], ps_m[u % 2][:, :], carry, ALU.mult, ALU.add).then_inc(s_scan, 1)

            run_chunks(dve, (combine, 1), (scan, 3))


def node_relations(nc, D, S):
    with ExitStack() as ctx:
        r = Room(nc, ctx, "n2")
        loop = r.sb("loop", [P, F])
        w = r.sb("w", [P, F])
        wT = r.sb("wT", [P, F])
        att = r.sb("att", [P, 2])
        heads = r.sb("heads", [P, 2 * H])
        wcat = r.sb("wcat", [P, W3])
        idx = r.sb("idx", [P, SLOTS, K], i32)
        deg = r.sb("deg", [P, SLOTS, K])
        sdeg = r.sb("sdeg", [P, SLOTS, K])
        rdeg = r.sb("rdeg", [P, SLOTS, K])
        agg = r.sb("agg", [P, SLOTS, CH])
        x = r.sb("x", [P, SLOTS, CH])
        xT = r.sb("xT", [P, 2, CH])
        pre = r.sb("pre", [P, 2, CH])
        y = r.sb("y", [P, SLOTS, CH])
        stats = r.sb("stats", [P, SLOTS, K * 6])
        mv = r.sb("mv", [P, SLOTS, K, 2])
        sd = r.sb("sd", [P, SLOTS, K])
        rs = r.sb("rs", [P, SLOTS, K])
        shift = r.sb("shift", [P, SLOTS, K])
        out = r.sb("out", [P, SLOTS, CH])
        oT = r.sb("oT", [P, 4, CH])
        tab = r.sb("tab", [P, SLOTS, K * W3])
        ps_x = r.ps("x")
        ps_o = [r.ps(f"o{i}") for i in range(2)]
        ps_y = r.ps("y")
        ps_h = [r.ps(f"h{i}") for i in range(2)]
        ps_r = [r.ps(f"r{i}") for i in range(2)]
        s_w = r.sem("w")
        s_heads = r.sem("heads")
        s_wps = r.sem("wps")
        s_wT = r.sem("wT")
        s_wps2 = r.sem("wps2")
        s_wcat = r.sem("wcat")
        s_idx = r.sems("idx")
        s_x = r.sems("x")
        s_deg = r.sems("deg")
        s_agg = r.sems("agg")
        s_store = r.sems("store")
        s_tab_store = r.sems("tab_store")
        s_sdeg = r.sem("sdeg")
        s_rdeg = r.sem("rdeg")
        s_turned = r.sem("turned")
        s_T = r.sem("T")
        s_mm = r.sem("mm")
        s_pre = r.sem("pre")
        s_y = r.sem("y")
        s_st = r.sem("st")
        s_mv = r.sem("mv")
        s_sd = r.sem("sd")
        s_rs = r.sem("rs")
        s_shift = r.sem("shift")
        s_out = r.sem("out")
        s_yturned = r.sem("yturned")
        s_yT = r.sem("yT")
        s_tab = r.sem("tab")
        s_tabbed = r.sem("tabbed")
        s_res = r.sem("res")
        s_rst = r.sem("rst")
        ctx.callback(r.close)
        block = ctx.enter_context(nc.Block())

        @block.sync
        def _(sp):
            def load_idx(c, q, u):
                if reused(c, SLOTS):
                    sp.wait_ge(s_agg[u], 16 * K * q)
                sp.nop(nofuse=True)
                sp.dma_start(idx[:, u, :], vec(D["last"], c)).then_inc(s_idx[u], 16)

            def load_x(c, q, u):
                if reused(c, SLOTS):
                    sp.wait_ge(s_y, c - SLOTS + 1)
                sp.nop(nofuse=True)
                sp.dma_start(x[:, u, :], rows(D["x2"], c)).then_inc(s_x[u], 16)
                if reused(c, SLOTS):
                    sp.wait_ge(s_sdeg, c - SLOTS + 1)
                sp.nop(nofuse=True)
                sp.dma_start(deg[:, u, :], vec(D["deg"], c)).then_inc(s_deg[u], 16)

            def store(c, q, u):
                sp.wait_ge(s_out, c + 1)
                sp.nop(nofuse=True)
                sp.dma_start(rows(D["x3"], c), out[:, u, :]).then_inc(s_store[u], 16)

            def store_table(c, q, u):
                sp.wait_ge(s_tabbed, 2 * (c + 1))
                sp.nop(nofuse=True)
                sp.dma_start(rows(D["table"], c), tab[:, u, :]).then_inc(s_tab_store[u], 16)
                four = tab[:, u, :].rearrange("p (k f) -> p k f", k=K)[:, :, F + H:W3]
                sp.dma_start(rows(D["a_dst"], c).rearrange("p (k h) -> p k h", k=K), four).then_inc(s_tab_store[u], 16)

            run_chunks(sp, (load_idx, 0), (load_x, 0), (store, 9), (store_table, 11))
            for u in range(SLOTS):
                sp.wait_ge(s_store[u], 16 * len(range(u, NCH, SLOTS)))
                sp.wait_ge(s_tab_store[u], 32 * len(range(u, NCH, SLOTS)))

        @block.gpsimd
        def _(pool):
            def fetch(c, q, u):
                pool.wait_ge(s_idx[u], 16 * (q + 1))
                if reused(c, SLOTS):
                    pool.wait_ge(s_pre, c - SLOTS + 1)
                gather(pool, s_agg[u], agg[:, u, :], F, D["agg"], idx[:, u, :])

            run_chunks(pool, (fetch, 0))

        @block.tensor
        def _(pe):
            pe.wait_ge(s_w, 80)
            pe.transpose(ps_h[0][:, 0:P], w[:, :], S["ident"][:, :]).then_inc(s_wps, 1)
            pe.wait_ge(s_wT, 1)
            pe.wait_ge(s_heads, 2)
            pe.matmul(ps_h[1][:, 0:2 * H], wT[:, :], heads[:, :], start=True, stop=True).then_inc(s_wps2, 1)

            def turn(c, q, u):
                pe.wait_ge(s_x[u], 16 * (q + 1))
                if reused(c, 1):
                    pe.wait_ge(s_T, c)
                for k in range(K):
                    ins = pe.transpose(ps_x[:, k * P:(k + 1) * P], x[:, u, k * F:(k + 1) * F], S["ident"][:, :])
                ins.then_inc(s_turned, 1)

            def multiply(c, q, u):
                pe.wait_ge(s_T, c + 1)
                if reused(c, 2):
                    pe.wait_ge(s_pre, c - 1)
                for k in range(K):
                    ins = pe.matmul(ps_o[u % 2][:, k * F:(k + 1) * F], xT[:, u % 2, k * P:(k + 1) * P], loop[:, :],
                                    start=True, stop=True)
                ins.then_inc(s_mm, 1)

            def turn_out(c, q, u):
                pe.wait_ge(s_out, c + 1)
                if reused(c, 1):
                    pe.wait_ge(s_yT, c)
                for k in range(K):
                    ins = pe.transpose(ps_y[:, k * P:(k + 1) * P], out[:, u, k * F:(k + 1) * F], S["ident"][:, :])
                ins.then_inc(s_yturned, 1)

            def table(c, q, u):
                pe.wait_ge(s_yT, c + 1)
                if not reused(c, 1):
                    pe.wait_ge(s_wcat, 2)
                for half in range(2):
                    if reused(c, 1):
                        pe.wait_ge(s_tabbed, 2 * c - 1 + half)
                    for k in (2 * half, 2 * half + 1):
                        ins = pe.matmul(ps_h[half][:, (k % 2) * W3:(k % 2 + 1) * W3], oT[:, u % 4, k * P:(k + 1) * P],
                                        wcat[:, :], start=True, stop=True)
                    ins.then_inc(s_tab, 1)

            def project(c, q, u):
                pe.wait_ge(s_yT, c + 1)
                if reused(c, 2):
                    pe.wait_ge(s_rst, c - 1)
                pe.matmul(ps_r[u % 2][:, :], S["res_w"][:, :], oT[:, u % 4, :], start=True, stop=True).then_inc(s_res, 1)

            run_chunks(pe, (turn, 0), (multiply, 1), (turn_out, 7), (table, 8), (project, 9))

        @block.scalar
        def _(act):
            act.dma_start(loop[:, :], D["L2_gnn_loop_weight"]).then_inc(s_w, 16)
            act.dma_start(w[:, :], D["L3_gnn_W"]).then_inc(s_w, 16)
            act.dma_start(S["res_w"][:, :], D["L3_gnn_res_W"]).then_inc(s_w, 16)
            act.dma_start(att[:, 0:1], D["L3_gnn_att_src"].rearrange("h c -> (h c)").unsqueeze(1)).then_inc(s_w, 16)
            act.dma_start(att[:, 1:2], D["L3_gnn_att_dst"].rearrange("h c -> (h c)").unsqueeze(1)).then_inc(s_w, 16)

            act.wait_ge(s_wps, 1)
            act.activation(wT[:, :], ps_h[0][:, 0:P], ACT.Copy).then_inc(s_wT, 1)
            act.wait_ge(s_w, 80)
            act.activation(wcat[:, 0:F], w[:, :], ACT.Copy).then_inc(s_wcat, 1)
            act.wait_ge(s_wps2, 1)
            act.activation(wcat[:, F:W3], ps_h[1][:, 0:2 * H], ACT.Copy).then_inc(s_wcat, 1)

            def root(c, q, u):
                act.wait_ge(s_deg[u], 16 * (q + 1))
                if reused(c, SLOTS):
                    act.wait_ge(s_rdeg, c - SLOTS + 1)
                act.activation(sdeg[:, u, :], deg[:, u, :], ACT.Sqrt).then_inc(s_sdeg, 1)

            def copy(c, q, u):
                act.wait_ge(s_turned, c + 1)
                if reused(c, 2):
                    act.wait_ge(s_mm, c - 1)
                act.activation(xT[:, u % 2, :], ps_x[:, :], ACT.Copy).then_inc(s_T, 1)

            def deviation(c, q, u):
                act.wait_ge(s_mv, c + 1)
                act.activation(sd[:, u, :], mv[:, u, :, 1], ACT.Sqrt, bias=S["eps"][:, 0:1]).then_inc(s_sd, 1)

            def copy_out(c, q, u):
                act.wait_ge(s_yturned, c + 1)
                if reused(c, 4):
                    act.wait_ge(s_tab, 2 * (c - 3))
                    act.wait_ge(s_res, c - 3)
                act.activation(oT[:, u % 4, :], ps_y[:, :], ACT.Copy).then_inc(s_yT, 1)

            def copy_table(c, q, u):
                if reused(c, SLOTS):
                    act.wait_ge(s_tab_store[u], 32 * q)
                for half in range(2):
                    act.wait_ge(s_tab, 2 * c + 1 + half)
                    act.activation(tab[:, u, half * 2 * W3:(half + 1) * 2 * W3], ps_h[half][:, 0:2 * W3],
                                   ACT.Copy).then_inc(s_tabbed, 1)

            def normalise(c, q, u):
                act.wait_ge(s_shift, c + 1)
                if reused(c, SLOTS):
                    act.wait_ge(s_store[u], 16 * q)
                    act.wait_ge(s_yturned, c - SLOTS + 1)
                row_affine(act, out[:, u, :], y[:, u, :], rs[:, u, :], shift[:, u, :]).then_inc(s_out, 1)

            run_chunks(act, (deviation, 4), (root, 0), (copy, 0), (copy_out, 7), (normalise, 6), (copy_table, 8))

        @block.vector
        def _(dve):
            dve.wait_ge(s_w, 80)
            for j in range(2):
                dve.tensor_scalar(heads[:, j * H:(j + 1) * H], S["head"][:, :], att[:, j:j + 1], None, ALU.mult).then_inc(s_heads, 1)

            def invert(c, q, u):
                dve.wait_ge(s_sdeg, c + 1)
                if reused(c, SLOTS):
                    dve.wait_ge(s_pre, c - SLOTS + 1)
                dve.reciprocal(rdeg[:, u, :], sdeg[:, u, :]).then_inc(s_rdeg, 1)

            def residual(c, q, u):
                dve.wait_ge(s_mm, c + 1)
                dve.wait_ge(s_rdeg, c + 1)
                dve.wait_ge(s_agg[u], 16 * K * (q + 1))
                for k in range(K):
                    f = slice(k * F, (k + 1) * F)
                    ins = dve.scalar_tensor_tensor(pre[:, u % 2, f], agg[:, u, f], rdeg[:, u, k:k + 1], ps_o[u % 2][:, f], ALU.mult, ALU.add)
                ins.then_inc(s_pre, 1)

            def inverse(c, q, u):
                dve.wait_ge(s_sd, c + 1)
                dve.reciprocal(rs[:, u, :], sd[:, u, :]).then_inc(s_rs, 1)

            def relu_add(c, q, u):
                dve.wait_ge(s_pre, c + 1)
                if reused(c, SLOTS):
                    dve.wait_ge(s_out, c - SLOTS + 1)
                dve.scalar_tensor_tensor(y[:, u, :], pre[:, u % 2, :], 0.0, x[:, u, :], ALU.max, ALU.add).then_inc(s_y, 1)

            def shifts(c, q, u):
                dve.wait_ge(s_rs, c + 1)
                dve.scalar_tensor_tensor(shift[:, u, :], mv[:, u, :, 0], -1.0, rs[:, u, :], ALU.mult, ALU.mult).then_inc(s_shift, 1)

            def row_statistics(c, q, u):
                dve.wait_ge(s_y, c + 1)
                row_stats(dve, y[:, u, :], stats[:, u, :]).then_inc(s_st, 1)

            def moments(c, q, u):
                dve.wait_ge(s_st, c + 1)
                row_moments(dve, stats[:, u, :], mv[:, u, :, :]).then_inc(s_mv, 1)

            def statistics(c, q, u):
                dve.wait_ge(s_res, c + 1)
                short = isinstance(c, int) and c == NCH - 1
                bank = ps_r[u % 2][:, :]
                seen = bank.rearrange("f (k p) -> f k p", k=K)[:, :, 0:LAST // K] if short else bank
                dve.nop(nofuse=True)
                dve.bn_stats(S["res_stats"][:, bass.ds(c * 6, 6)], seen).then_inc(s_rst, 1)

            run_chunks(dve, (inverse, 5), (invert, 1), (residual, 2), (shifts, 5), (row_statistics, 3), (relu_add, 2),
                       (moments, 3), (statistics, 10))


def edge_attention(nc, D, S):
    with ExitStack() as ctx:
        r = Room(nc, ctx, "e3")
        idx = r.sb("idx", [P, SLOTS, 2 * K], i32)
        gate = r.sb("gate", [P, SLOTS, CH], bf16)
        src = r.sb("src", [P, SLOTS, K * W3])
        dst = r.sb("dst", [P, SLOTS, K * H])
        lin = r.sb("lin", [P, 2, K, H])
        logit = r.sb("logit", [P, 2, K, H])
        wide = r.sb("wide", [P, 2, K, F])
        top = r.sb("top", [P, SLOTS, 1 + CH])
        moved = r.sb("moved", [P, 2, CH])
        decay = r.sb("decay", [P, 2, 2, CH])
        grow = r.sb("grow", [P, 2, 2, CH])
        wrow = r.sb("wrow", [P, 2, CH])
        den = r.sb("den", [P, SLOTS, CH])
        num = r.sb("num", [P, SLOTS, CH])
        out = r.sb("out", [P, SLOTS, K * W3])
        ps_h = [r.ps(f"h{i}") for i in range(2)]
        ps_a = [r.ps(f"a{i}") for i in range(2)]
        ps_o = [r.ps(f"o{i}") for i in range(2)]
        ps_d = [r.ps(f"d{i}") for i in range(2)]
        s_idx = r.sems("idx")
        s_gate = r.sems("gate")
        s_rows = r.sems("rows")
        s_store = r.sems("store")
        s_first = r.sem("first")
        s_lin = r.sem("lin")
        s_logit = r.sem("logit")
        s_wide = r.sem("wide")
        s_turned = r.sem("turned")
        s_top = r.sem("top")
        s_moved = r.sem("moved")
        s_diff = r.sem("diff")
        s_exp = r.sem("exp")
        s_wrow = r.sem("wrow")
        s_scan = r.sem("scan")
        s_back = r.sem("back")
        s_out = r.sem("out")
        ctx.callback(r.close)
        block = ctx.enter_context(nc.Block())

        @block.sync
        def _(sp):
            def load_idx(c, q, u):
                if reused(c, SLOTS):
                    sp.wait_ge(s_rows[u], 16 * 2 * K * q)
                sp.nop(nofuse=True)
                sp.dma_start(idx[:, u, 0:K], vec(D["src"], c)).then_inc(s_idx[u], 16)
                sp.dma_start(idx[:, u, K:2 * K], vec(D["dst"][1:NP + 1], c)).then_inc(s_idx[u], 16)

            def load_gate(c, q, u):
                if reused(c, SLOTS):
                    sp.wait_ge(s_moved, c - SLOTS + 1)
                sp.nop(nofuse=True)
                sp.dma_start(gate[:, u, :], spread(D["gate"], c, P)).then_inc(s_gate[u], 16)

            def store(c, q, u):
                sp.wait_ge(s_out, c + 1)
                sp.nop(nofuse=True)
                sp.dma_start(rows(D["att"], c), out[:, u, :]).then_inc(s_store[u], 16)

            run_chunks(sp, (load_idx, 0), (load_gate, 1), (store, 5))
            for u in range(SLOTS):
                sp.wait_ge(s_store[u], 16 * len(range(u, NCH, SLOTS)))

        @block.gpsimd
        def _(pool):
            def fetch(c, q, u):
                pool.wait_ge(s_idx[u], 32 * (q + 1))
                if reused(c, SLOTS):
                    pool.wait_ge(s_lin, c - SLOTS + 1)
                    pool.wait_ge(s_turned, c - SLOTS + 1)
                gather(pool, s_rows[u], src[:, u, :], W3, D["table"], idx[:, u, 0:K])
                gather(pool, s_rows[u], dst[:, u, :], H, D["a_dst"], idx[:, u, K:2 * K])

            run_chunks(pool, (fetch, 0))

        @block.vector
        def _(dve):
            dve.memset(top[:, 0, 0:1], -BIG).then_inc(s_first, 1)

            def logits(c, q, u):
                dve.wait_ge(s_rows[u], 16 * 2 * K * (q + 1))
                a_src = src[:, u, :].rearrange("p (k f) -> p k f", k=K)[:, :, F:F + H]
                a_dst = dst[:, u, :].rearrange("p (k h) -> p k h", k=K)
                dve.tensor_tensor(lin[:, u % 2, :, :], a_src, a_dst, ALU.add).then_inc(s_lin, 1)
                dve.wait_ge(s_lin, c + 1)
                dve.scalar_tensor_tensor(logit[:, u % 2, :, :], lin[:, u % 2, :, :], 0.2, lin[:, u % 2, :, :], ALU.mult, ALU.max).then_inc(s_logit, 1)

            def maximum(c, q, u):
                dve.wait_ge(s_turned, c + 1)
                dve.wait_ge(s_gate[u], 16 * (q + 1))
                if reused(c, 1):
                    if reused(c, SLOTS):
                        dve.wait_ge(s_back, c - SLOTS + 1)
                    dve.wait_ge(s_top, c)
                    dve.tensor_copy(top[:, u, 0:1], top[:, (u - 1) % SLOTS, CH:CH + 1]).then_inc(s_first, 1)
                dve.wait_ge(s_first, c + 1)
                dve.tensor_tensor_scan(top[:, u, 1:CH + 1], gate[:, u, :], ps_a[u % 2][:, :], top[:, u, 0:1], ALU.add, ALU.max).then_inc(s_top, 1)
                dve.wait_ge(s_top, c + 1)
                if reused(c, 2):
                    dve.wait_ge(s_exp, c - 1)
                dve.tensor_tensor(moved[:, u % 2, :], top[:, u, 0:CH], gate[:, u, :], ALU.add).then_inc(s_moved, 1)
                dve.tensor_tensor(grow[:, u % 2, 0, :], ps_a[u % 2][:, :], top[:, u, 1:CH + 1], ALU.subtract)
                dve.wait_ge(s_moved, c + 1)
                dve.tensor_tensor(decay[:, u % 2, 0, :], moved[:, u % 2, :], top[:, u, 1:CH + 1], ALU.subtract).then_inc(s_diff, 1)

            def sums(c, q, u):
                dve.wait_ge(s_exp, c + 1)
                dve.tensor_tensor(wrow[:, u % 2, :], grow[:, u % 2, 1, :], ps_h[u % 2][:, :], ALU.mult).then_inc(s_wrow, 1)
                if reused(c, SLOTS):
                    dve.wait_ge(s_back, c - SLOTS + 1)
                first, second = 0.0, 0.0
                if reused(c, 1):
                    dve.wait_ge(s_scan, 2 * c)
                    first = den[:, (u - 1) % SLOTS, CH - 1:CH]
                    second = num[:, (u - 1) % SLOTS, CH - 1:CH]
                dve.tensor_tensor_scan(den[:, u, :], decay[:, u % 2, 1, :], grow[:, u % 2, 1, :], first, ALU.mult, ALU.add).then_inc(s_scan, 1)
                dve.wait_ge(s_wrow, c + 1)
                dve.tensor_tensor_scan(num[:, u, :], decay[:, u % 2, 1, :], wrow[:, u % 2, :], second, ALU.mult, ALU.add).then_inc(s_scan, 1)

            run_chunks(dve, (logits, 0), (maximum, 1), (sums, 2))

        @block.tensor
        def _(pe):
            def turn(c, q, u):
                pe.wait_ge(s_wide, c + 1)
                if reused(c, 2):
                    pe.wait_ge(s_wrow, c - 1)
                    pe.wait_ge(s_diff, c - 1)
                bank = ps_h[u % 2][:, :].rearrange("f (p k) -> f k p", k=K)
                for k in range(K):
                    pe.transpose(bank[:, k, :], src[:, u, k * W3:k * W3 + F], S["ident"][:, :])
                bank = ps_a[u % 2][:, :].rearrange("f (p k) -> f k p", k=K)
                for k in range(K):
                    ins = pe.transpose(bank[:, k, :], wide[:, u % 2, k, :], S["ident"][:, :])
                ins.then_inc(s_turned, 1)

            def back(c, q, u):
                pe.wait_ge(s_scan, 2 * (c + 1))
                if reused(c, 2):
                    pe.wait_ge(s_out, c - 1)
                cols = num[:, u, :].rearrange("f (p k) -> f k p", k=K)
                for k in range(K):
                    pe.transpose(ps_o[u % 2][:, k * F:(k + 1) * F], cols[:, k, :], S["ident"][:, :])
                cols = [t.rearrange("f (p k) -> f k p", k=K) for t in (den[:, u, :], top[:, u, 1:CH + 1])]
                for k in range(K):
                    for j in range(2):
                        at = (2 * k + j) * H
                        ins = pe.matmul(ps_d[u % 2][:, at:at + H], cols[j][:, k, :], S["head_first"][:, :], start=True, stop=True)
                ins.then_inc(s_back, 1)

            run_chunks(pe, (turn, 0), (back, 3))

        @block.scalar
        def _(act):
            def widen(c, q, u):
                act.wait_ge(s_logit, c + 1)
                if reused(c, 2):
                    act.wait_ge(s_turned, c - 1)
                flat = logit[:, u % 2, :, :].rearrange("p k h -> p (k h)")
                act.activation(wide[:, u % 2, :, :].rearrange("p k (h c) -> p (k h) c", h=H),
                               flat.unsqueeze(2).to_broadcast([P, K * H, HC]), ACT.Copy).then_inc(s_wide, 1)

            def exponentials(c, q, u):
                act.wait_ge(s_diff, c + 1)
                if reused(c, 2):
                    act.wait_ge(s_scan, 2 * (c - 1))
                act.activation(grow[:, u % 2, 1, :], grow[:, u % 2, 0, :], ACT.Exp)
                act.activation(decay[:, u % 2, 1, :], decay[:, u % 2, 0, :], ACT.Exp).then_inc(s_exp, 1)

            def leave(c, q, u):
                act.wait_ge(s_back, c + 1)
                if reused(c, SLOTS):
                    act.wait_ge(s_store[u], 16 * q)
                row = out[:, u, :].rearrange("p (k f) -> p k f", k=K)
                act.activation(row[:, :, 0:F], ps_o[u % 2][:, :].rearrange("p (k f) -> p k f", k=K), ACT.Copy)
                act.activation(row[:, :, F:W3], ps_d[u % 2][:, 0:K * 2 * H].rearrange("p (k f) -> p k f", k=K),
                               ACT.Copy).then_inc(s_out, 1)

            run_chunks(act, (widen, 0), (exponentials, 1), (leave, 3))


def node_attention(nc, D, S):
    with ExitStack() as ctx:
        r = Room(nc, ctx, "n3")
        bias = r.sb("bias", [P, 1])
        idx = r.sb("idx", [P, SLOTS, K], i32)
        agg = r.sb("agg", [P, SLOTS, K * W3])
        own = r.sb("own", [P, SLOTS, K * W3])
        t = {n: r.sb(n, [P, 2, K, H]) for n in ("lin", "logit", "top", "den", "rden")}
        ex = r.sb("ex", [P, 2, 2, K * H])
        wgt = r.sb("wgt", [P, 2, 2, K * H])
        part = r.sb("part", [P, 2, 2, CH])
        out = r.sb("out", [P, SLOTS, CH])
        ps_t = [r.ps(f"t{i}") for i in range(2)]
        s_bias = r.sem("bias")
        s_idx = r.sems("idx")
        s_agg = r.sems("agg")
        s_own = r.sems("own")
        s_store = r.sems("store")
        s_step = r.sem("step")
        s_fold = r.sem("fold")
        s_arg = r.sem("arg")
        s_exp = r.sem("exp")
        s_wgt = r.sem("wgt")
        s_part = r.sem("part")
        s_mm = r.sem("mm")
        s_out = r.sem("out")
        s_stats = r.sem("stats")
        ctx.callback(r.close)
        block = ctx.enter_context(nc.Block())

        @block.sync
        def _(sp):
            def load_idx(c, q, u):
                if reused(c, SLOTS):
                    sp.wait_ge(s_agg[u], 16 * K * q)
                sp.nop(nofuse=True)
                sp.dma_start(idx[:, u, :], vec(D["last"], c)).then_inc(s_idx[u], 16)

            def load_own(c, q, u):
                if reused(c, SLOTS):
                    sp.wait_ge(s_part, c - SLOTS + 1)
                sp.nop(nofuse=True)
                sp.dma_start(own[:, u, :], rows(D["table"], c)).then_inc(s_own[u], 16)

            def store(c, q, u):
                sp.wait_ge(s_out, c + 1)
                sp.nop(nofuse=True)
                sp.dma_start(D["gat"][:, bass.ds(c * CH, CH)], out[:, u, :]).then_inc(s_store[u], 16)

            run_chunks(sp, (load_idx, 0), (load_own, 0), (store, 6))
            for u in range(SLOTS):
                sp.wait_ge(s_store[u], 16 * len(range(u, NCH, SLOTS)))

        @block.gpsimd
        def _(pool):
            def fetch(c, q, u):
                pool.wait_ge(s_idx[u], 16 * (q + 1))
                if reused(c, SLOTS):
                    pool.wait_ge(s_part, c - SLOTS + 1)
                gather(pool, s_agg[u], agg[:, u, :], W3, D["att"], idx[:, u, :])

            run_chunks(pool, (fetch, 0))

        @block.vector
        def _(dve):
            def cut(buf, u, a, b):
                return buf[:, u, :].rearrange("p (k f) -> p k f", k=K)[:, :, a:b]

            def four(name, v):
                return t[name][:, v, :, :]

            def exponents(c, q, u):
                v = u % 2
                dve.wait_ge(s_own[u], 16 * (q + 1))
                dve.wait_ge(s_agg[u], 16 * K * (q + 1))
                dve.tensor_tensor(four("lin", v), cut(own, u, F, F + H), cut(own, u, F + H, W3), ALU.add).then_inc(s_step, 1)
                dve.wait_ge(s_step, 3 * c + 1)
                dve.scalar_tensor_tensor(four("logit", v), four("lin", v), 0.2, four("lin", v), ALU.mult, ALU.max).then_inc(s_step, 1)
                dve.wait_ge(s_step, 3 * c + 2)
                dve.tensor_tensor(four("top", v), cut(agg, u, F + H, W3), four("logit", v), ALU.max).then_inc(s_step, 1)
                dve.wait_ge(s_step, 3 * c + 3)
                pair = ex[:, v, :, :].rearrange("p j (k h) -> p j k h", k=K)
                dve.tensor_tensor(pair[:, 0, :, :], cut(agg, u, F + H, W3), four("top", v), ALU.subtract)
                dve.tensor_tensor(pair[:, 1, :, :], four("logit", v), four("top", v), ALU.subtract).then_inc(s_arg, 1)

            def weigh(c, q, u):
                v = u % 2
                dve.wait_ge(s_exp, c + 1)
                pair = ex[:, v, :, :].rearrange("p j (k h) -> p j k h", k=K)
                dve.tensor_tensor(four("den", v), cut(agg, u, F, F + H), pair[:, 0, :, :], ALU.mult).then_inc(s_fold, 1)
                dve.wait_ge(s_fold, 3 * c + 1)
                dve.tensor_tensor(four("den", v), four("den", v), pair[:, 1, :, :], ALU.add).then_inc(s_fold, 1)
                dve.wait_ge(s_fold, 3 * c + 2)
                dve.reciprocal(four("rden", v), four("den", v)).then_inc(s_fold, 1)
                dve.wait_ge(s_fold, 3 * c + 3)
                flat = four("rden", v).rearrange("p k h -> p (k h)")
                for j in range(2):
                    ins = dve.tensor_tensor(wgt[:, v, j, :], ex[:, v, j, :], flat, ALU.mult)
                ins.then_inc(s_wgt, 1)
                dve.wait_ge(s_wgt, c + 1)
                if reused(c, 2):
                    dve.wait_ge(s_mm, c - 1)
                for j, rows_ in ((0, agg), (1, own)):
                    w4 = wgt[:, v, j, :].rearrange("p (k h) -> p k h", k=K).unsqueeze(3).to_broadcast([P, K, H, HC])
                    ins = dve.tensor_tensor(part[:, v, j, :].rearrange("p (k h c) -> p k h c", k=K, h=H),
                                            cut(rows_, u, 0, F).rearrange("p k (h c) -> p k h c", h=H), w4, ALU.mult)
                ins.then_inc(s_part, 1)

            def statistics(c, q, u):
                dve.wait_ge(s_out, c + 1)
                short = isinstance(c, int) and c == NCH - 1
                seen = out[:, u, :].rearrange("f (k p) -> f k p", k=K)[:, :, 0:LAST // K] if short else out[:, u, :]
                dve.nop(nofuse=True)
                dve.bn_stats(S["gat_stats"][:, bass.ds(c * 6, 6)], seen).then_inc(s_stats, 1)

            run_chunks(dve, (exponents, 0), (weigh, 1), (statistics, 3))

        @block.scalar
        def _(act):
            act.dma_start(bias[:, :], D["L3_gnn_bias"].unsqueeze(1)).then_inc(s_bias, 16)

            def exponentials(c, q, u):
                act.wait_ge(s_arg, c + 1)
                both = ex[:, u % 2, :, :].rearrange("p j k -> p (j k)")
                act.activation(both, both, ACT.Exp).then_inc(s_exp, 1)

            def leave(c, q, u):
                act.wait_ge(s_mm, c + 1)
                if reused(c, SLOTS):
                    act.wait_ge(s_store[u], 16 * q)
                    act.wait_ge(s_stats, c - SLOTS + 1)
                act.activation(out[:, u, :], ps_t[u % 2][:, :], ACT.Identity, bias=bias[:, 0:1]).then_inc(s_out, 1)

            act.wait_ge(s_bias, 16)
            run_chunks(act, (exponentials, 0), (leave, 2))

        @block.tensor
        def _(pe):
            def add(c, q, u):
                pe.wait_ge(s_part, c + 1)
                if reused(c, 2):
                    pe.wait_ge(s_out, c - 1)
                for k in range(K):
                    o = ps_t[u % 2][:, k * P:(k + 1) * P]
                    pe.matmul(o, part[:, u % 2, 0, k * F:(k + 1) * F], S["ident"][:, :], start=True, stop=False)
                    ins = pe.matmul(o, part[:, u % 2, 1, k * F:(k + 1) * F], S["ident"][:, :], start=False, stop=True)
                ins.then_inc(s_mm, 1)

            run_chunks(pe, (add, 1))


def finish(nc, D, S):
    with ExitStack() as ctx:
        r = Room(nc, ctx, "fin")
        NC = 7
        MINE = 3
        cols = r.sb("cols", [P, NC])
        GAM, BET, LG, LB, RB, RG, RBET = range(NC)
        mvs = r.sb("mvs", [P, 2, 2])
        dev = r.sb("dev", [P, 2])
        inv = r.sb("inv", [P, 2])
        mu = r.sb("mu", [P, 1])
        tmp = r.sb("tmp", [P, 3])
        vecs = r.sb("vecs", [P, 5])
        diag = r.sb("diag", [P, 3, P])
        gamma_row = r.sb("gamma_row", [P, CH])
        wres = r.sb("wres", [P, F])
        tres = r.sb("tres", [1, F])
        g = r.sb("g", [P, SLOTS, CH])
        x = r.sb("x", [P, SLOTS, CH])
        zT = r.sb("zT", [P, 2, CH])
        shift = r.sb("shift", [P, SLOTS, K])
        zn = r.sb("zn", [P, 2, CH])
        zg = r.sb("zg", [P, 2, CH])
        xT = r.sb("xT", [P, 2, CH])
        sumv = r.sb("sumv", [P, 2, CH])
        y = r.sb("y", [P, SLOTS, CH])
        act_row = r.sb("act_row", [P, 2, CH])
        out = r.sb("out", [P, SLOTS, CH])
        st = [r.sb(f"st{i}", [P, SLOTS, K * 6]) for i in range(2)]
        mv = [r.sb(f"mv{i}", [P, SLOTS, K, 2]) for i in range(2)]
        sd = [r.sb(f"sd{i}", [P, SLOTS, K]) for i in range(2)]
        rs = [r.sb(f"rs{i}", [P, SLOTS, K]) for i in range(2)]
        ps_x = [r.ps(f"x{i}") for i in range(2)]
        ps_i = [r.ps(f"i{i}") for i in range(2)]
        ps_z = [r.ps(f"z{i}") for i in range(4)]
        s_cols = r.sem("cols")
        s_aggr = r.sem("aggr")
        s_dev = r.sem("dev")
        s_vec = r.sem("vec")
        s_diag = r.sem("diag")
        s_row = r.sem("row")
        s_ready = r.sem("ready")
        s_g = r.sems("g")
        s_x = r.sems("x")
        s_store = r.sems("store")
        s_zT = r.sem("zT")
        s_z = r.sem("z")
        s_shift = r.sem("shift")
        s_st = [r.sem(f"st{i}") for i in range(2)]
        s_mv = [r.sem(f"mv{i}") for i in range(2)]
        s_sd = [r.sem(f"sd{i}") for i in range(2)]
        s_rs = [r.sem(f"rs{i}") for i in range(2)]
        s_zn = r.sem("zn")
        s_zg = r.sem("zg")
        s_turned = r.sem("turned")
        s_T = r.sem("T")
        s_mm = r.sem("mm")
        s_sum = r.sem("sum")
        s_relu = r.sem("relu")
        s_y = r.sem("y")
        s_out = r.sem("out")
        s_out_pool = r.sem("out_pool")
        ctx.callback(r.close)
        block = ctx.enter_context(nc.Block())

        @block.sync
        def _(sp):
            for j, name in enumerate(("bn_gamma", "bn_beta", "ln_gamma", "ln_beta", "res_b", "bnres_gamma", "bnres_beta")):
                sp.dma_start(cols[:, j:j + 1], D[f"L3_gnn_{name}"].unsqueeze(1)).then_inc(s_cols, 16)

            def load_g(c, q, u):
                if reused(c, SLOTS):
                    sp.wait_ge(s_zT, c - SLOTS + 1)
                sp.nop(nofuse=True)
                sp.dma_start(g[:, u, :], D["gat"][:, bass.ds(c * CH, CH)]).then_inc(s_g[u], 16)

            def load_x(c, q, u):
                if reused(c, SLOTS):
                    sp.wait_ge(s_y, c - SLOTS + 1)
                sp.nop(nofuse=True)
                sp.dma_start(x[:, u, :], rows(D["x3"], c)).then_inc(s_x[u], 16)

            def store(c, q, u):
                sp.wait_ge(s_out, c + 1)
                sp.wait_ge(s_out_pool, c + 1)
                sp.nop(nofuse=True)
                sp.dma_start(rows(D["x4"], c), out[:, u, :]).then_inc(s_store[u], 16)

            run_chunks(sp, (load_g, 0), (load_x, 1), (store, 13))
            for u in range(SLOTS):
                sp.wait_ge(s_store[u], 16 * len(range(u, NCH, SLOTS)))

        @block.gpsimd
        def _(pool):
            pool.wait_ge(s_ready, 1)

            def gamma(c, q, u):
                pool.wait_ge(s_zn, c + 1)
                if reused(c, 2):
                    pool.wait_ge(s_sum, c - 1)
                pool.tensor_tensor(zg[:, u % 2, :], zn[:, u % 2, :], gamma_row[:, :], ALU.mult).then_inc(s_zg, 1)

            def residual(c, q, u):
                pool.wait_ge(s_relu, c + 1)
                if reused(c, SLOTS):
                    pool.wait_ge(s_out, c - SLOTS + 1)
                    pool.wait_ge(s_out_pool, c - SLOTS + 1)
                pool.tensor_tensor(y[:, u, :], act_row[:, u % 2, :], x[:, u, :], ALU.add).then_inc(s_y, 1)

            def apply_second(c, q, u):
                pool.wait_ge(s_rs[1], c + 1)
                if reused(c, SLOTS):
                    pool.wait_ge(s_store[u], 16 * q)
                pool.nop(nofuse=True)
                for k in range(MINE, K):
                    f = slice(k * F, (k + 1) * F)
                    ins = pool.tensor_scalar(out[:, u, f], y[:, u, f], mv[1][:, u, k, 0:1], rs[1][:, u, k:k + 1], ALU.subtract, ALU.mult)
                ins.then_inc(s_out_pool, 1)

            run_chunks(pool, (gamma, 5), (residual, 8), (apply_second, 11))

        @block.vector
        def _(dve):
            chain = [0]

            def link(ins):
                chain[0] += 1
                ins.then_inc(s_vec, 1)
                dve.wait_ge(s_vec, chain[0])

            dve.bn_aggr(mvs[:, 0, :], S["gat_stats"][:, :])
            dve.bn_aggr(mvs[:, 1, :], S["res_stats"][:, :]).then_inc(s_aggr, 1)
            dve.wait_ge(s_dev, 1)
            dve.wait_ge(s_cols, 16 * NC)
            link(dve.reciprocal(inv[:, :], dev[:, :]))
            link(dve.tensor_tensor(vecs[:, 0:1], cols[:, GAM:GAM + 1], inv[:, 0:1], ALU.mult))
            link(dve.tensor_tensor(tmp[:, 0:1], mvs[:, 0, 0:1], vecs[:, 0:1], ALU.mult))
            link(dve.tensor_tensor(vecs[:, 1:2], cols[:, BET:BET + 1], tmp[:, 0:1], ALU.subtract))
            link(dve.tensor_copy(vecs[:, 2:3], cols[:, LG:LG + 1]))
            link(dve.tensor_tensor(vecs[:, 3:4], cols[:, RG:RG + 1], inv[:, 1:2], ALU.mult))
            link(dve.tensor_tensor(mu[:, :], mvs[:, 1, 0:1], cols[:, RB:RB + 1], ALU.add))
            link(dve.tensor_tensor(tmp[:, 1:2], cols[:, RB:RB + 1], mu[:, :], ALU.subtract))
            link(dve.tensor_tensor(tmp[:, 2:3], tmp[:, 1:2], vecs[:, 3:4], ALU.mult))
            link(dve.tensor_tensor(vecs[:, 4:5], tmp[:, 2:3], cols[:, RBET:RBET + 1], ALU.add))
            link(dve.tensor_tensor(vecs[:, 4:5], vecs[:, 4:5], cols[:, LB:LB + 1], ALU.add))
            for j in range(3):
                dve.tensor_scalar(diag[:, j, :], S["ident"][:, :], vecs[:, 2 + j:3 + j], None, ALU.mult).then_inc(s_diag, 1)
            dve.wait_ge(s_row, 1)
            dve.tensor_copy(gamma_row[:, :], ps_i[0][:, :]).then_inc(s_ready, 1)
            dve.wait_ge(s_row, 3)
            dve.tensor_tensor(wres[:, :], S["res_w"][:, :], ps_x[0][:, 0:F], ALU.mult).then_inc(s_ready, 1)
            dve.tensor_copy(tres[:, :], ps_x[1][0:1, 0:F]).then_inc(s_ready, 1)

            def first_stats(c, q, u):
                dve.wait_ge(s_z, c + 1)
                row_stats(dve, ps_z[u % 4][:, :], st[0][:, u, :]).then_inc(s_st[0], 1)

            def first_moments(c, q, u):
                dve.wait_ge(s_st[0], c + 1)
                row_moments(dve, st[0][:, u, :], mv[0][:, u, :, :]).then_inc(s_mv[0], 1)

            def first_inverse(c, q, u):
                dve.wait_ge(s_sd[0], c + 1)
                dve.reciprocal(rs[0][:, u, :], sd[0][:, u, :]).then_inc(s_rs[0], 1)

            def first_shifts(c, q, u):
                dve.wait_ge(s_rs[0], c + 1)
                dve.scalar_tensor_tensor(shift[:, u, :], mv[0][:, u, :, 0], -1.0, rs[0][:, u, :], ALU.mult, ALU.mult).then_inc(s_shift, 1)

            def total(c, q, u):
                dve.wait_ge(s_zg, c + 1)
                dve.wait_ge(s_mm, c + 1)
                if reused(c, 2):
                    dve.wait_ge(s_relu, c - 1)
                dve.tensor_tensor(sumv[:, u % 2, :], zg[:, u % 2, :], ps_i[u % 2][:, :], ALU.add).then_inc(s_sum, 1)

            def second_stats(c, q, u):
                dve.wait_ge(s_y, c + 1)
                row_stats(dve, y[:, u, :], st[1][:, u, :]).then_inc(s_st[1], 1)

            def second_moments(c, q, u):
                dve.wait_ge(s_st[1], c + 1)
                if reused(c, SLOTS):
                    dve.wait_ge(s_out_pool, c - SLOTS + 1)
                row_moments(dve, st[1][:, u, :], mv[1][:, u, :, :]).then_inc(s_mv[1], 1)

            def second_inverse(c, q, u):
                dve.wait_ge(s_sd[1], c + 1)
                if reused(c, SLOTS):
                    dve.wait_ge(s_out_pool, c - SLOTS + 1)
                dve.reciprocal(rs[1][:, u, :], sd[1][:, u, :]).then_inc(s_rs[1], 1)

            def apply_second(c, q, u):
                dve.wait_ge(s_rs[1], c + 1)
                if reused(c, SLOTS):
                    dve.wait_ge(s_store[u], 16 * q)
                for k in range(MINE):
                    f = slice(k * F, (k + 1) * F)
                    ins = dve.tensor_scalar(out[:, u, f], y[:, u, f], mv[1][:, u, k, 0:1], rs[1][:, u, k:k + 1], ALU.subtract, ALU.mult)
                ins.then_inc(s_out, 1)

            run_chunks(dve, (second_inverse, 11), (first_stats, 2), (first_inverse, 3), (second_stats, 9),
                       (first_moments, 2), (first_shifts, 3), (apply_second, 11), (second_moments, 9), (total, 6))

        @block.scalar
        def _(act):
            act.wait_ge(s_aggr, 1)
            act.activation(dev[:, :], mvs[:, :, 1], ACT.Sqrt, bias=S["eps"][:, 0:1]).then_inc(s_dev, 1)

            def deviation(i):
                def work(c, q, u):
                    act.wait_ge(s_mv[i], c + 1)
                    act.activation(sd[i][:, u, :], mv[i][:, u, :, 1], ACT.Sqrt, bias=S["eps"][:, 0:1]).then_inc(s_sd[i], 1)
                return work

            act.wait_ge(s_vec, 11)

            def affine(c, q, u):
                act.wait_ge(s_g[u], 16 * (q + 1))
                if reused(c, 2):
                    act.wait_ge(s_z, c - 1)
                act.activation(zT[:, u % 2, :], g[:, u, :], ACT.Identity, bias=vecs[:, 1:2], scale=vecs[:, 0:1]).then_inc(s_zT, 1)

            def copy(c, q, u):
                act.wait_ge(s_turned, c + 1)
                if reused(c, 2):
                    act.wait_ge(s_mm, c - 1)
                act.activation(xT[:, u % 2, :], ps_x[u % 2][:, :], ACT.Copy).then_inc(s_T, 1)

            def normalise(c, q, u):
                act.wait_ge(s_shift, c + 1)
                if reused(c, 2):
                    act.wait_ge(s_zg, c - 1)
                row_affine(act, zn[:, u % 2, :], ps_z[u % 4][:, :], rs[0][:, u, :], shift[:, u, :]).then_inc(s_zn, 1)

            def relu(c, q, u):
                act.wait_ge(s_sum, c + 1)
                if reused(c, 2):
                    act.wait_ge(s_y, c - 1)
                act.activation(act_row[:, u % 2, :], sumv[:, u % 2, :], ACT.Relu).then_inc(s_relu, 1)

            run_chunks(act, (affine, 0), (deviation(0), 3), (deviation(1), 10), (copy, 4), (normalise, 4), (relu, 7))

        @block.tensor
        def _(pe):
            pe.wait_ge(s_diag, 1)
            for k in range(K):
                ins = pe.matmul(ps_i[0][:, k * F:(k + 1) * F], S["ones"][:, 0:P], diag[:, 0, :], start=True, stop=True)
            ins.then_inc(s_row, 1)
            for j in range(2):
                pe.wait_ge(s_diag, 2 + j)
                pe.matmul(ps_x[j][:, 0:F], S["ones"][:, 0:P], diag[:, 1 + j, :], start=True, stop=True).then_inc(s_row, 1)
            pe.wait_ge(s_ready, 3)

            def turn_z(c, q, u):
                pe.wait_ge(s_zT, c + 1)
                if reused(c, 4):
                    pe.wait_ge(s_zn, c - 3)
                for k in range(K):
                    ins = pe.transpose(ps_z[u % 4][:, k * F:(k + 1) * F], zT[:, u % 2, k * P:(k + 1) * P], S["ident"][:, :])
                ins.then_inc(s_z, 1)

            def turn(c, q, u):
                pe.wait_ge(s_x[u], 16 * (q + 1))
                if reused(c, 2):
                    pe.wait_ge(s_T, c - 1)
                for k in range(K):
                    ins = pe.transpose(ps_x[u % 2][:, k * P:(k + 1) * P], x[:, u, k * F:(k + 1) * F], S["ident"][:, :])
                ins.then_inc(s_turned, 1)

            def multiply(c, q, u):
                pe.wait_ge(s_T, c + 1)
                if reused(c, 2):
                    pe.wait_ge(s_sum, c - 1)
                for k in range(K):
                    o = ps_i[u % 2][:, k * F:(k + 1) * F]
                    pe.matmul(o, xT[:, u % 2, k * P:(k + 1) * P], wres[:, :], start=True, stop=False)
                    ins = pe.matmul(o, S["ones"][0:1, 0:P], tres[:, :], start=False, stop=True)
                ins.then_inc(s_mm, 1)

            run_chunks(pe, (turn_z, 1), (turn, 3), (multiply, 5))


SCRATCH = [("keep", (NP,), bf16), ("gate", (NP,), bf16), ("rel", (NP,), bf16), ("last", (NP,), i32), ("deg", (NP,), fp32),
           ("agg", (NP + 1, F), fp32), ("att", (NP + 1, W3), fp32),
           ("x1", (NP, F), fp32), ("x2", (NP, F), fp32), ("x3", (NP, F), fp32),
           ("table", (NP, W3), fp32), ("a_dst", (NP, H), fp32), ("gat", (F, NP), fp32),
           ("edge_coef", (NP, NBASE), fp32)]


def build(nc, D):
    with ExitStack() as ctx:
        r = Room(nc, ctx, "all")
        S = {"iota": r.sb("iota", [P, LO], fp16), "iota_p": r.sb("iota_p", [P, 1]), "ones": r.sb("ones", [P, LO]),
             "eps": r.sb("eps", [P, 1]), "ident": r.sb("ident", [P, P]), "before": r.sb("before", [P, P]),
             "hi": r.sb("hi", [P, NP // P]), "lo": r.sb("lo", [P, NP // P]),
             "head": r.sb("head", [P, H]), "head_first": r.sb("head_first", [P, H]),
             "res_w": r.sb("res_w", [P, F]),
             "res_stats": r.sb("res_stats", [P, 6 * NCH]), "gat_stats": r.sb("gat_stats", [P, 6 * NCH])}
        prepare(nc, D, S)
        edge_sum_rows(nc, D, S)
        node_mean(nc, D, S)
        edge_max(nc, D, S)
        node_mlp(nc, D, S)
        edge_relations(nc, D, S)
        node_relations(nc, D, S)
        edge_attention(nc, D, S)
        node_attention(nc, D, S)
        finish(nc, D, S)


_FLOATS = ["L0_gnn_W", "L0_gnn_b", "L1_gnn_W_edge", "L1_gnn_b_edge", "L1_gnn_W_mlp", "L1_gnn_b_mlp",
           "L2_gnn_basis_weights", "L2_gnn_coefficients", "L2_gnn_loop_weight",
           "L3_gnn_W", "L3_gnn_att_src", "L3_gnn_att_dst", "L3_gnn_bias", "L3_gnn_bn_gamma", "L3_gnn_bn_beta",
           "L3_gnn_ln_gamma", "L3_gnn_ln_beta", "L3_gnn_res_W", "L3_gnn_res_b", "L3_gnn_bnres_gamma", "L3_gnn_bnres_beta"]


def kernel(**inputs):
    import numpy as _np
    import concourse.bacc as _bacc
    from concourse.bass_utils import run_bass_kernel_spmd as _run

    def padded(a, fill=0, front=0):
        a = _np.asarray(a)
        out = _np.full((front + NP,) + a.shape[1:], fill, a.dtype)
        out[front:front + N] = a
        return out

    dst = padded(inputs["dst"], N, 1)
    dst[0] = -1
    arrays = {"x0": padded(inputs["x"]), "src": padded(inputs["src"]), "dst": dst,
              "edge_attr_64": padded(inputs["edge_attr_64"]), "edge_type_100": padded(inputs["edge_type_100"])}
    for name in _FLOATS:
        arrays[name] = _np.ascontiguousarray(inputs[name])
    nc = _bacc.Bacc("TRN2", target_bir_lowering=False, num_devices=1)
    D = {n: nc.dram_tensor(f"in_{n}", a.shape, mybir.dt.from_np(a.dtype), kind="ExternalInput").ap()
         for n, a in arrays.items()}
    D["x4"] = nc.dram_tensor("out_x4", (NP, F), fp32, kind="ExternalOutput").ap()
    for name, shape, dt in SCRATCH:
        D[name] = nc.dram_tensor(f"tmp_{name}", shape, dt, kind="Internal").ap()
    build(nc, D)
    r = _run(nc, [{f"in_{n}": a for n, a in arrays.items()}], core_ids=[0])
    return r.results[0]["out_x4"][:N]
```
